# Optimizing a Trainium2 kernel written in Bass

```python
import numpy as np
import jax
import jax.numpy as jnp

def _softmax(x, axis=-1):
    return jax.nn.softmax(x, axis=axis)

def _gelu(x):
    return jax.nn.gelu(x, approximate=True)

def _silu(x):
    return jax.nn.silu(x)

def _sigmoid(x):
    return jax.nn.sigmoid(x)

def _layernorm(x, axis=-1, eps=1e-05):
    m = jnp.mean(x, axis=axis, keepdims=True)
    v = jnp.var(x, axis=axis, keepdims=True)
    return (x - m) / jnp.sqrt(v + eps)

def _scatter_add(tgt, idx, src, axis=0):
    return tgt.at[idx].add(src)

def _segment_sum(src, seg, n):
    return jax.ops.segment_sum(src, seg, n)
kernel_name = 'mk_gnn_resnorm_d2_gnn_r8_f34a00'

def setup_inputs(seed: int=0):
    np.random.seed(seed)
    _w = jnp.asarray

    def _rec_inputs():
        import jax
        import jax.numpy as jnp
        _gk = jax.random.key(seed)
        x = -0.0002117 + 1 * jax.random.normal(jax.random.fold_in(_gk, 1), (3125, 1024), jnp.float32)
        src = jax.random.randint(jax.random.fold_in(_gk, 2), (50000,), 0, 3125, jnp.int32)
        dst = jax.random.randint(jax.random.fold_in(_gk, 3), (50000,), 0, 3125, jnp.int32)
        _o = jnp.argsort(dst, stable=True)
        src = src[_o]
        dst = dst[_o]
        return (x, src, dst)
    x, src, dst = _rec_inputs()

    def _L0_gnn_setup():
        import jax, jax.numpy as jnp
        import numpy as np
        N = 3125
        E = 50000
        H = 4
        C = 256
        D_IN = 1024
        NEG_SLOPE = 0.2
        key = jax.random.key(seed)
        k1, k2, k3, k4, k5, k6 = jax.random.split(key, 6)
        x = jax.random.normal(k1, (N, D_IN), dtype=jnp.float32)
        edge_index = jax.random.randint(k2, (2, E), 0, N, dtype=jnp.int64)
        scale = 1.0 / np.sqrt(D_IN)
        W = jax.random.normal(k3, (D_IN, H * C), dtype=jnp.float32) * scale
        att_src = jax.random.normal(k4, (H, C), dtype=jnp.float32) * 0.1
        att_dst = jax.random.normal(k5, (H, C), dtype=jnp.float32) * 0.1
        bias = jax.random.normal(k6, (H * C,), dtype=jnp.float32) * 0.01
        return {'x': x, 'edge_index': edge_index, 'W': W, 'att_src': att_src, 'att_dst': att_dst, 'bias': bias}
    _L0_gnn_all = _L0_gnn_setup()
    _L0_gnn_in = {k: v for k, v in _L0_gnn_all.items() if k in ('W', 'att_src', 'att_dst', 'bias')}
    del _L0_gnn_all

    def _L1_gnn_setup():
        import jax, jax.numpy as jnp
        import numpy as np
        N = 2500
        E = 40000
        IN = 1024
        HID = 256
        H = 4
        D = HID // H
        OUT = 1024
        EPS = 1e-06
        NEG_SLOPE = 0.2
        key = jax.random.key(seed)
        ks = jax.random.split(key, 8)
        x = jax.random.normal(ks[0], (N, IN), dtype=jnp.float32)
        edge_index = jax.random.randint(ks[1], (2, E), 0, N, dtype=jnp.int64)
        s = 0.02
        return {'x': x, 'edge_index': edge_index, 'rms_w': jnp.ones((IN,), dtype=jnp.float32), 'W_down': jax.random.normal(ks[2], (IN, HID), dtype=jnp.float32) * s, 'Wl': jax.random.normal(ks[3], (HID, HID), dtype=jnp.float32) * s, 'Wr': jax.random.normal(ks[4], (HID, HID), dtype=jnp.float32) * s, 'att': jax.random.normal(ks[5], (H, D), dtype=jnp.float32) * s, 'W_up': jax.random.normal(ks[6], (HID, OUT), dtype=jnp.float32) * s}
    _L1_gnn_all = _L1_gnn_setup()
    _L1_gnn_in = {k: v for k, v in _L1_gnn_all.items() if k in ('rms_w', 'W_down', 'Wl', 'Wr', 'att', 'W_up')}
    del _L1_gnn_all
    return {'x': x, 'src': src, 'dst': dst, 'L0_gnn_W': _L0_gnn_in['W'], 'L0_gnn_att_src': _L0_gnn_in['att_src'], 'L0_gnn_att_dst': _L0_gnn_in['att_dst'], 'L0_gnn_bias': _L0_gnn_in['bias'], 'L1_gnn_rms_w': _L1_gnn_in['rms_w'], 'L1_gnn_W_down': _L1_gnn_in['W_down'], 'L1_gnn_Wl': _L1_gnn_in['Wl'], 'L1_gnn_Wr': _L1_gnn_in['Wr'], 'L1_gnn_att': _L1_gnn_in['att'], 'L1_gnn_W_up': _L1_gnn_in['W_up']}

def reference(x, src, dst, L0_gnn_W, L0_gnn_att_src, L0_gnn_att_dst, L0_gnn_bias, L1_gnn_rms_w, L1_gnn_W_down, L1_gnn_Wl, L1_gnn_Wr, L1_gnn_att, L1_gnn_W_up):
    import jax
    import jax.numpy as jnp

    def _L0_gnn_ref(x, edge_index, W, att_src, att_dst, bias):
        import jax, jax.numpy as jnp
        import numpy as np
        N = 3125
        E = 50000
        H = 4
        C = 256
        D_IN = 1024
        NEG_SLOPE = 0.2
        xp = (x @ W).reshape(N, H, C)
        a_src = jnp.einsum('nhc,hc->nh', xp, att_src)
        a_dst = jnp.einsum('nhc,hc->nh', xp, att_dst)
        loops = jnp.arange(N, dtype=edge_index.dtype)
        src = jnp.concatenate([edge_index[0], loops])
        dst = jnp.concatenate([edge_index[1], loops])
        e = jax.nn.leaky_relu(a_src[src] + a_dst[dst], NEG_SLOPE)
        m = jax.ops.segment_max(e, dst, num_segments=N)
        ee = jnp.exp(e - m[dst])
        z = jax.ops.segment_sum(ee, dst, num_segments=N)
        alpha = ee / z[dst]
        msgs = xp[src] * alpha[:, :, None]
        out = jax.ops.segment_sum(msgs, dst, num_segments=N)
        out = out.reshape(N, H * C) + bias
        return jax.nn.relu(out)

    def _L1_gnn_ref(x, edge_index, rms_w, W_down, Wl, Wr, att, W_up):
        import jax, jax.numpy as jnp
        import numpy as np
        N = 2500
        E = 40000
        IN = 1024
        HID = 256
        H = 4
        D = HID // H
        OUT = 1024
        EPS = 1e-06
        NEG_SLOPE = 0.2
        n = x.shape[0]
        ms = jnp.mean(jnp.square(x), axis=-1, keepdims=True)
        x = x * jax.lax.rsqrt(ms + EPS) * rms_w
        x = x @ W_down
        loop = jnp.arange(n, dtype=edge_index.dtype)
        src = jnp.concatenate([edge_index[0], loop])
        dst = jnp.concatenate([edge_index[1], loop])
        xl = (x @ Wl).reshape(n, H, D)
        xr = (x @ Wr).reshape(n, H, D)
        msg = xl[src] + xr[dst]
        act = jnp.where(msg > 0, msg, NEG_SLOPE * msg)
        e = jnp.einsum('ehd,hd->eh', act, att)
        m = jax.ops.segment_max(e, dst, num_segments=n)
        p = jnp.exp(e - m[dst])
        denom = jax.ops.segment_sum(p, dst, num_segments=n)
        alpha = p / (denom[dst] + 1e-16)
        out = jax.ops.segment_sum(alpha[..., None] * xl[src], dst, num_segments=n)
        out = out.reshape(n, HID)
        return out @ W_up
    edge_index = jnp.stack([src, dst])
    x = _layernorm(x + _L0_gnn_ref(x, edge_index, L0_gnn_W, L0_gnn_att_src, L0_gnn_att_dst, L0_gnn_bias), axis=-1)
    x = _layernorm(x + _L1_gnn_ref(x, edge_index, L1_gnn_rms_w, L1_gnn_W_down, L1_gnn_Wl, L1_gnn_Wr, L1_gnn_att, L1_gnn_W_up), axis=-1)
    return x

_drawn_inputs = setup_inputs


def setup_inputs(seed=0):
    import zlib

    import numpy as np

    out = dict(_drawn_inputs(seed))
    spreads = {'L1_gnn_rms_w': (1.0, 0.6)}
    factors = {'L0_gnn_bias': 7.903,
     'L1_gnn_W_down': 3.283,
     'L1_gnn_Wl': 3.274,
     'L1_gnn_Wr': 8.0,
     'L1_gnn_att': 8.0,
     'L1_gnn_W_up': 3.286}
    for name, (base, spread) in spreads.items():
        noise = np.random.default_rng([zlib.crc32(name.encode()), seed]).standard_normal(out[name].shape)
        drawn = base * np.exp(spread * noise) if base else spread * noise
        out[name] = jnp.asarray(drawn.astype(out[name].dtype))
    for name, factor in factors.items():
        out[name] = (out[name] * factor).astype(out[name].dtype)
    return out
```

```python
import concourse.bass as bass
from concourse import mybir
from contextlib import ExitStack

F32 = mybir.dt.float32
I32 = mybir.dt.int32
ALU = mybir.AluOpType
ACT = mybir.ActivationFunctionType
AX = mybir.AxisListType

P = 128
N, E, D, H, C = 3125, 50000, 1024, 4, 256
HID = 256
HD = HID // H
KD = D // P
KH = HID // P
NT = -(-N // P)
NP = NT * P
N_LAST = N - (NT - 1) * P
NC = -(-E // P)
NCF = E // P
E_LAST = E - NCF * P
NB = 4
U = 4
T = -(-(NC + NT - 1) // (2 * U * NB)) * 2 * U * NB
TB = T // NB
NG = T // U
NO_DST = 8191
BIG = 1e30
SLOPE = 0.2
LN_EPS = 1e-5
RMS_EPS = 1e-6
DEN_EPS = 1e-16
DVE_HEADS = 1
DVE_HEADS1 = 2
W9 = 2 * H + 1
XLW = HID + H
XRW = HID + 2 * H
ACC1 = HID + W9


def wait(eng, sem, value):
    if not isinstance(value, int) or value > 0:
        eng.wait_ge(sem, value)


class Chain:

    def __init__(self, eng, sem, per=0):
        self.eng, self.sem, self.per, self.base, self.k = eng, sem, per, 0, 0

    def tile(self, t):
        assert self.k == (self.per if self.k else 0) or not self.per
        self.base, self.k = t * self.per, 0

    def __call__(self, ins):
        ins.then_inc(self.sem, 1)
        self.k += 1
        self.eng.wait_ge(self.sem, self.base + self.k)


def pipelined(eng, n, stages, ahead=4, ring=2):
    last = n + max(lag for lag, _ in stages)
    ahead += -ahead % ring

    def turn(v):
        for lag, f in stages:
            t = v - lag
            if 0 <= t < n:
                f(t, t % ring, t // ring)

    for v in range(min(ahead, last)):
        turn(v)
    end = n - n % ring
    if end > ahead:
        with eng.Fori(ahead // ring, end // ring) as i:
            for par in range(ring):
                for lag, f in stages:
                    s = (par - lag) % ring
                    f(ring * i + (par - lag), s, i + (par - lag - s) // ring)
    for v in range(max(end, ahead), last):
        turn(v)


def bc(ap, shape):
    return ap.to_broadcast(shape)


class StepTiles:

    def __init__(self, eng, dtab, name, steps=U):
        self.eng, self.dtab, self.steps = eng, dtab, steps
        self.regs = [eng.alloc_register(f"{name}_d{j}") for j in range(steps)]

    def load(self, g):
        self.eng.reg_load(self.regs, self.dtab[0:1, bass.ds(g * self.steps, self.steps)])
        return [self.eng.snap(r, min_val=0, max_val=NT - 1) for r in self.regs]


class PoolGather:

    def __init__(self, pool, rows, bound):
        self.pool, self.bound, self.rows = pool, bound, rows
        pool.reg_mov(bound, rows - 1)

    def wait(self, sem, value):
        if isinstance(value, int) and value <= 0:
            return
        self.pool.wait_ge(sem, value)
        self.pool.reg_alu(self.bound, self.bound, self.rows - 1, ALU.min)

    def rows_of(self, out, table, idx):
        return self.pool.indirect_dma_start(out, None, table, bass.IndirectOffsetOnAxis(ap=idx, axis=0),
                                            bounds_check=self.bound, oob_is_err=False)


def gnn_kernel(nc, x, src, dst, w0, att_s, att_d, bias, rms_w, w_down, wl, wr, att1, w_up, out):
    edge_t = nc.dram_tensor("edge_table", (T, 4 * P), F32, kind="Internal").ap()
    local_t = nc.dram_tensor("local_dst", (T, P), F32, kind="Internal").ap()
    as_t = nc.dram_tensor("a_src_table", (NP, H), F32, kind="Internal").ap()
    xp_t = nc.dram_tensor("xp_table", (NP, D), F32, kind="Internal").ap()
    x1_t = nc.dram_tensor("x1_table", (NP, D), F32, kind="Internal").ap()
    xe_t = nc.dram_tensor("edge_rows", (NG, P, U * XLW), F32, kind="Internal").ap()
    xl_t = nc.dram_tensor("xl_table", (NP, XLW), F32, kind="Internal").ap()

    top = ExitStack()
    sems = [0]

    def sem(name):
        sems[0] += 1
        return top.enter_context(nc.semaphore(name))

    with top:
        def keep(name, shape, dt=F32):
            return top.enter_context(nc.sbuf_tensor(name, shape, dt))

        ident = keep("ident", [P, P])
        iotar = keep("iotar", [P, P])
        pidx = keep("pidx", [P, 1])
        ldst = keep("ldst", [P, T])
        isrc = keep("isrc", [P, T])
        isfirst = keep("isfirst", [P, T])
        dtab = keep("dtab", [1, T], I32)
        rs_f = keep("rs_f", [TB, NB, P])
        rs_b = keep("rs_b", [TB, NB, P])
        pen = keep("pen", [TB, NB, P])
        any_f = keep("any_f", [H, T])
        any_b = keep("any_b", [H, T])
        w9 = keep("w9", [P, T, W9])
        nt0 = keep("nt0", [P, NT, 2 * H])
        bound = nc.gpsimd.alloc_register("row_bound")
        psum = [top.enter_context(nc.psum_tensor(f"bank{i}", [P, 512], F32)) for i in range(8)] \
            if False else top.enter_context(nc.psum_tensor("banks", [P, 8, 512], F32))

        with ExitStack() as ph:
            def sb(name, shape, dt=F32):
                return ph.enter_context(nc.sbuf_tensor(name, shape, dt))
            w_sb = sb("w0_sb", [P, KD, D])
            atts = sb("atts_bc", [P, D])
            attd = sb("attd_bc", [P, D])
            junk = sb("junk", [P, C])
            wa = sb("wa", [P, KD, 2 * H])
            xin = sb("xin", [P, 2, D])
            xT = sb("xT", [P, 2, KD, P])
            a_all = sb("a_all", [P, NT, 2 * H])
            a_sum = sb("a_sum", [P, NT, H])
            dx = sb("dx", [TB, NB, P + 2], I32)
            sx = sb("sx", [TB, NB, P], I32)
            dxf = sb("dxf", [TB, NB, P + 2])
            ct = sb("ct", [TB, NB, 4, P])
            st = sb("st", [TB, NB, 4, P])
            lasti = sb("lasti", [1, NC], I32)
            lastf = sb("lastf", [1, NC])
            lastw = sb("lastw", [1, NC])
            ioti = sb("ioti", [P, NC], I32)
            iotc = sb("iotc", [1, NC])
            step128 = sb("step128", [TB, NB])
            stepi = sb("stepi", [TB, NB], I32)
            ones = sb("ones", [1, P])
            less = sb("less", [TB, NC])
            ci = sb("ci", [TB, NB])
            cii = sb("cii", [TB, NB], I32)
            di = sb("di", [TB, NB])
            dneg = sb("dneg", [TB, NB])
            dcl = sb("dcl", [TB, NB])
            lrow = sb("lrow", [TB, NB, P])
            val = sb("val", [TB, NB, P])
            fv = sb("fv", [TB, NB, P])
            lv = sb("lv", [TB, NB, P])
            af = sb("af", [TB, NB, H])
            ab = sb("ab", [TB, NB, H])

            s_pad = sem("s_pad")
            s_edges = sem("s_edges")
            s_lrow = sem("s_lrow")
            s_att = sem("s_att")
            s_w = [sem(f"s_w{k}") for k in range(2)]
            s_iota = sem("s_iota")
            s_ident = sem("s_ident")
            s_dv = sem("s_setup_chain")
            s_ct = sem("s_ct")
            s_et = sem("s_et")
            s_lastw = sem("s_lastw")
            s_bcast = sem("s_bcast")
            s_ci = sem("s_ci")
            s_st = sem("s_st")
            s_lw = sem("s_lw")
            s_lt = sem("s_ltst")
            s_tp = sem("s_tp")
            s_wa = sem("s_wa")
            s_xi = [sem(f"s_xi{i}") for i in range(2)]
            s_tr = sem("s_tr")
            s_xT = sem("s_xT")
            s_am = sem("s_am")
            s_ac = sem("s_ac")
            s_as = sem("s_as")

            with nc.Block() as block:
                @block.gpsimd
                def _(pool):
                    nc.gpsimd.memset(dx[:], NO_DST).then_inc(s_pad, 1)
                    nc.gpsimd.memset(sx[:], 0).then_inc(s_pad, 1)
                    nc.gpsimd.memset(lasti[:], NO_DST).then_inc(s_pad, 1)
                    nc.gpsimd.iota(ioti[:], pattern=[[P, NC]], base=0, channel_multiplier=0).then_inc(s_iota, 1)
                    pool.wait_ge(s_iota, 1)
                    nc.gpsimd.tensor_copy(iotc[:], ioti[0:1, :]).then_inc(s_iota, 1)
                    nc.gpsimd.iota(stepi[:], pattern=[[P * TB, NB]], base=0, channel_multiplier=P).then_inc(s_iota, 1)
                    pool.wait_ge(s_iota, 3)
                    nc.gpsimd.tensor_copy(step128[:], stepi[:]).then_inc(s_iota, 1)
                    nc.gpsimd.iota(ioti[:, 0:P], pattern=[[1, P]], base=0, channel_multiplier=0).then_inc(s_iota, 1)
                    pool.wait_ge(s_iota, 5)
                    nc.gpsimd.tensor_copy(iotar[:], ioti[:, 0:P]).then_inc(s_iota, 1)
                    nc.gpsimd.iota(ioti[:, P:P + 1], pattern=[[0, 1]], base=0, channel_multiplier=1).then_inc(s_iota, 1)
                    pool.wait_ge(s_iota, 7)
                    nc.gpsimd.tensor_copy(pidx[:], ioti[:, P:P + 1]).then_inc(s_iota, 1)
                    nc.gpsimd.memset(ones[:], 1.0).then_inc(s_iota, 1)
                    nc.gpsimd.memset(xin[:], 0.0).then_inc(s_pad, 1)
                    nc.gpsimd.memset(ident[:], 0.0).then_inc(s_ident, 1)
                    pool.wait_ge(s_ident, 1)
                    nc.gpsimd.affine_select(out=ident[:], in_=ident[:], compare_op=ALU.not_equal, fill=1.0,
                                            base=0, pattern=[[-1, P]], channel_multiplier=1).then_inc(s_ident, 1)
                    gather = PoolGather(pool, T, bound)
                    pool.wait_ge(s_ci, 1)
                    pool.wait_ge(s_et, 16)
                    for b in range(NB):
                        gather.rows_of(st[:, b, :, :].rearrange("p f k -> p (f k)"), edge_t, cii[:, b:b + 1])\
                              .then_inc(s_st, 16)

                @block.sync
                def _(sp):
                    sp.wait_ge(s_pad, 3)
                    dh = dst.tensor
                    first = sp.dma_start(dx[0:1, 0, 1:P + 2], dst[0:P + 1].rearrange("(a k) -> a k", a=1))
                    first.then_inc(s_edges, 16)
                    n_edge = 1
                    for b in range(NB):
                        c0, c1 = max(1, b * TB), min((b + 1) * TB, NCF)
                        sp.dma_start(dx[c0 - b * TB:c1 - b * TB, b, :],
                                     bass.AP(dh, c0 * P - 1, [[P, c1 - c0], [1, P + 2]])).then_inc(s_edges, 16)
                        c0 = b * TB
                        sp.dma_start(sx[0:c1 - c0, b, :],
                                     src[c0 * P:c1 * P].rearrange("(p k) -> p k", k=P)).then_inc(s_edges, 16)
                        n_edge += 2
                    pl, bl = NCF % TB, NCF // TB
                    sp.dma_start(dx[pl:pl + 1, bl, 0:E_LAST + 1],
                                 dst[NCF * P - 1:E].rearrange("(a k) -> a k", a=1)).then_inc(s_edges, 16)
                    sp.dma_start(sx[pl:pl + 1, bl, 0:E_LAST],
                                 src[NCF * P:E].rearrange("(a k) -> a k", a=1)).then_inc(s_edges, 16)
                    assert n_edge + 2 == N_EDGE_DMAS
                    with nc.allow_non_contiguous_dma(reason="one word of each chunk"):
                        sp.dma_start(lasti[0:1, 0:NCF], dst[0:NCF * P].rearrange("(c k) -> k c", k=P)[P - 1:P, :])\
                          .then_inc(s_lrow, 16)
                    for k in range(KD):
                        sp.dma_start(w_sb[:, k, :], w0[k * P:(k + 1) * P, :]).then_inc(s_w[k // (KD // 2)], 16)
                    sp.wait_ge(s_ct, 1)
                    sp.dma_start(edge_t.rearrange("(b p) n -> p b n", b=NB),
                                 ct[:].rearrange("p b f k -> p b (f k)")).then_inc(s_et, 16)
                    sp.wait_ge(s_lw, 1)
                    sp.dma_start(local_t.rearrange("(b p) n -> p b n", b=NB), lrow[:]).then_inc(s_lt, 16)
                    sp.wait_ge(s_ac, NT)
                    with nc.allow_non_contiguous_dma(reason="four words a node"):
                        sp.dma_start(as_t.rearrange("(t p) h -> p t h", p=P), a_all[:, :, 0:H]).then_inc(s_as, 16)
                    sp.wait_ge(s_as, 16)
                    sp.wait_ge(s_lt, 16)

                @block.scalar
                def _(act):
                    act.dma_start(atts[:], att_s.rearrange("h c -> (h c)").partition_broadcast(P)).then_inc(s_att, 16)
                    act.dma_start(attd[:], att_d.rearrange("h c -> (h c)").partition_broadcast(P)).then_inc(s_att, 16)
                    act.wait_ge(s_pad, 4)

                    def load_x(t, s, m):
                        wait(act, s_tr, t - 1)
                        rows = N_LAST if isinstance(t, int) and t == NT - 1 else P
                        act.dma_start(xin[0:rows, s, :], x[bass.ds(t * P, rows), :]).then_inc(s_xi[s], 16)

                    def evict(t, s, m):
                        act.wait_ge(s_tr, t + 1)
                        wait(act, s_am, t - 1)
                        nc.scalar.activation(xT[:, s].rearrange("p k n -> p (k n)"),
                                             psum[:, 2 * s:2 * s + 2].rearrange("p a b -> p (a b)"),
                                             ACT.Copy).then_inc(s_xT, 1)

                    def take_a(t, s, m):
                        act.wait_ge(s_am, t + 1)
                        nc.scalar.activation(a_all[:, bass.ds(t, 1), :], psum[:, 4 + 2 * s, 0:8], ACT.Copy)\
                            .then_inc(s_ac, 1)

                    pipelined(act, NT, [(0, load_x), (1, evict), (3, take_a)])

                @block.tensor
                def _(pe):
                    pe.wait_ge(s_lastw, 1)
                    nc.tensor.matmul(psum[0:TB, 5, 0:NC], ones[0:1, 0:TB], lastw[:], start=True, stop=True)\
                        .then_inc(s_bcast, 1)
                    pe.wait_ge(s_ident, 2)

                    def transposes(t, s, m):
                        pe.wait_ge(s_xi[s], 16 * (m + 1))
                        wait(pe, s_xT, t - 1)
                        for k in range(KD):
                            last = nc.tensor.transpose(
                                psum[:, 2 * s + k // 4, (k % 4) * P:(k % 4 + 1) * P],
                                xin[:, s, k * P:(k + 1) * P], ident[:])
                        last.then_inc(s_tr, 1)

                    def products(t, s, m):
                        if isinstance(t, int) and t == 0:
                            pe.wait_ge(s_wa, 1)
                        pe.wait_ge(s_xT, t + 1)
                        wait(pe, s_ac, t - 1)
                        for k in range(KD):
                            last = nc.tensor.matmul(psum[:, 4 + 2 * s, 0:8], xT[:, s, k, :], wa[:, k, :],
                                                    start=(k == 0), stop=(k == KD - 1))
                        last.then_inc(s_am, 1)

                    pipelined(pe, NT, [(1, transposes), (2, products)])
                    pe.wait_ge(s_lw, 1)
                    pe.wait_ge(s_ac, NT)
                    for i, rows in enumerate((lrow, st, fv)):
                        for b in range(NB):
                            a = rows[:, b, 0, :] if rows is st else rows[:, b, :]
                            nc.tensor.transpose(psum[:, i, b * TB:(b + 1) * TB], a, ident[0:TB, 0:TB])
                    for i, v in enumerate((af, ab)):
                        for b in range(NB):
                            nc.tensor.transpose(psum[0:H, 6 + i, b * TB:(b + 1) * TB], v[:, b, :], ident[0:TB, 0:TB])
                    for b in range(NB):
                        last = nc.tensor.transpose(psum[0:1, 3, b * TB:(b + 1) * TB], dcl[:, b:b + 1], ident[0:TB, 0:TB])
                    last.then_inc(s_tp, 1)

                @block.vector
                def _(dve):
                    link = Chain(dve, s_dv)
                    dve.wait_ge(s_iota, 9)
                    dve.wait_ge(s_lrow, 16)
                    link(nc.vector.tensor_copy(lastf[:], lasti[:]))
                    nc.vector.tensor_tensor(lastw[:], lastf[:], iotc[:], ALU.add).then_inc(s_lastw, 1)
                    dve.wait_ge(s_edges, 16 * N_EDGE_DMAS)
                    link(nc.vector.tensor_copy(dxf[:], dx[:]))
                    nc.vector.tensor_copy(ct[:, :, 0, :], sx[:])
                    nc.vector.tensor_copy(ct[:, :, 1, :], dxf[:, :, 1:P + 1])
                    nc.vector.tensor_tensor(ct[:, :, 2, :], dxf[:, :, 1:P + 1], dxf[:, :, 0:P], ALU.not_equal)
                    nc.vector.tensor_tensor(ct[:, :, 3, :], dxf[:, :, 1:P + 1], dxf[:, :, 2:P + 2], ALU.not_equal)\
                        .then_inc(s_ct, 1)
                    dve.wait_ge(s_bcast, 1)
                    for b in range(NB):
                        link(nc.vector.tensor_scalar(less[:], psum[0:TB, 5, 0:NC], step128[:, b:b + 1], None, ALU.is_lt))
                        link(nc.vector.reduce_sum(ci[:, b:b + 1], less[:], AX.X))
                    link(nc.vector.tensor_scalar_min(ci[:], ci[:], float(NC - 1)))
                    nc.vector.tensor_copy(cii[:], ci[:]).then_inc(s_ci, 1)
                    link(nc.vector.scalar_tensor_tensor(out=dneg[:], in0=ci[:], scalar=float(P), in1=step128[:],
                                                        op0=ALU.mult, op1=ALU.subtract))
                    link(nc.vector.tensor_scalar(di[:], dneg[:], -1.0 / P, None, ALU.mult))
                    link(nc.vector.tensor_scalar_min(dcl[:], di[:], float(NT - 1)))
                    dve.wait_ge(s_att, 32)
                    for k in range(KD):
                        dve.wait_ge(s_w[k // (KD // 2)], 16 * KD // 2)
                        for i, att in enumerate((atts, attd)):
                            for h in range(H):
                                link(nc.vector.tensor_tensor_reduce(
                                    out=junk[:], in0=w_sb[:, k, h * C:(h + 1) * C], in1=att[:, h * C:(h + 1) * C],
                                    scale=1.0, scalar=0.0, op0=ALU.mult, op1=ALU.add,
                                    accum_out=wa[:, k, i * H + h:i * H + h + 1]))
                    nc.vector.tensor_copy(junk[:, 0:1], pidx[:]).then_inc(s_wa, 1)
                    dve.wait_ge(s_st, 16 * NB)
                    for b in range(NB):
                        nc.vector.tensor_scalar(lrow[:, b, :], st[:, b, 1, :], dneg[:, b:b + 1], None, ALU.add)
                    link(nc.vector.tensor_scalar(junk[:, 1:2], pidx[:], 0.0, None, ALU.mult))
                    link(nc.vector.tensor_scalar(val[:], lrow[:], 0.0, None, ALU.is_ge))
                    link(nc.vector.scalar_tensor_tensor(out=val[:], in0=lrow[:], scalar=float(P), in1=val[:],
                                                        op0=ALU.is_lt, op1=ALU.mult))
                    nc.vector.tensor_scalar(pen[:], val[:], BIG, -BIG, ALU.mult, ALU.add)
                    nc.vector.tensor_tensor(fv[:], st[:, :, 2, :], val[:], ALU.mult)
                    link(nc.vector.tensor_tensor(lv[:], st[:, :, 3, :], val[:], ALU.mult))
                    nc.vector.tensor_scalar(rs_f[:], fv[:], -BIG, None, ALU.mult)
                    link(nc.vector.tensor_scalar(rs_b[:], lv[:], -BIG, None, ALU.mult))
                    for h in range(H):
                        nc.vector.tensor_reduce(out=af[:, :, h], in_=rs_f[:], op=ALU.min, axis=AX.X)
                        last = nc.vector.tensor_reduce(out=ab[:, :, h], in_=rs_b[:], op=ALU.min, axis=AX.X)
                    last.then_inc(s_lw, 1)
                    dve.wait_ge(s_ac, NT)
                    nc.vector.tensor_copy(nt0[:, :, 0:H], a_all[:, :, H:2 * H])
                    link(nc.vector.tensor_tensor(a_sum[:], a_all[:, :, 0:H], a_all[:, :, H:2 * H], ALU.add))
                    nc.vector.scalar_tensor_tensor(out=nt0[:, :, H:2 * H], in0=a_sum[:], scalar=SLOPE, in1=a_sum[:],
                                                   op0=ALU.mult, op1=ALU.max)
                    dve.wait_ge(s_tp, 1)
                    nc.vector.tensor_copy(ldst[:], psum[:, 0, 0:T])
                    nc.vector.tensor_copy(isrc[:], psum[:, 1, 0:T])
                    nc.vector.tensor_copy(isfirst[:], psum[:, 2, 0:T])
                    nc.vector.tensor_copy(any_f[:], psum[0:H, 6, 0:T])
                    nc.vector.tensor_copy(any_b[:], psum[0:H, 7, 0:T])
                    nc.vector.tensor_copy(dtab[:], psum[0:1, 3, 0:T])

        UNITS = T // (4 * U)
        with ExitStack() as ph:
            def sb(name, shape, dt=F32):
                return ph.enter_context(nc.sbuf_tensor(name, shape, dt))
            w_sb = sb("w0_sb2", [P, KD, D])
            xin = sb("xin2", [P, D])
            xT = sb("xT2", [P, KD, P])
            xp_st = sb("xp_st", [P, D])
            lt = sb("lt_bc", [P, 2, U, P])
            onehot_t = sb("onehot_t", [P, 2, U, P])
            idx = sb("idx", [P, 2, U], I32)
            ga = sb("ga", [P, 2, U, H])
            esum = sb("esum", [P, 2, U, H])

            s_w = sem("p1_w")
            s_clr = sem("p1_clr")
            s_xi = sem("p1_x")
            s_tr = sem("p1_tr")
            s_xT = sem("p1_xT")
            s_xp = sem("p1_xp")
            s_xe = sem("p1_xe")
            s_xs = sem("p1_xs")
            s_lt = [sem(f"p1_lt{i}") for i in range(2)]
            s_ot = sem("p1_ot")
            s_pg = sem("p1_pg")
            s_ix = sem("p1_ix")
            s_ga = [sem(f"p1_ga{i}") for i in range(2)]
            s_es = sem("p1_es")
            s_lg = sem("p1_lg")

            def units(eng, body):
                body(0, True)
                with eng.Fori(1, NT) as u:
                    body(u, True)
                body(NT, False)

            with nc.Block() as block:
                @block.gpsimd
                def _(pool):
                    nc.gpsimd.memset(xin[:], 0.0).then_inc(s_clr, 1)
                    gather = PoolGather(pool, N, bound)

                    def group(g_all, s, m):
                        gather.wait(s_ga[s], 64 * m)
                        nc.gpsimd.tensor_copy(idx[:, s, :], isrc[:, bass.ds(g_all * U, U)]).then_inc(s_ix, 1)
                        gather.wait(s_ix, g_all + 1)
                        gather.wait(s_lg, g_all - 1)
                        for j in range(U):
                            gather.rows_of(ga[:, s, j, :], as_t, idx[:, s, j:j + 1]).then_inc(s_ga[s], 16)

                    units(pool, lambda u, _: [group(4 * u + g, g % 2, 2 * u + g // 2) for g in range(4)] and None)

                @block.sync
                def _(sp):
                    for k in range(KD):
                        sp.dma_start(w_sb[:, k, :], w0[k * P:(k + 1) * P, :]).then_inc(s_w, 16)
                    sp.wait_ge(s_clr, 1)

                    def load_x(u, rows=P):
                        wait(sp, s_tr, u)
                        sp.dma_start(xin[0:rows, :], x[bass.ds(u * P, rows), :]).then_inc(s_xi, 16)

                    def unit(u, has_x, load=None):
                        if load == "last":
                            load_x(NT - 1, N_LAST)
                        elif load != "none":
                            load_x(u)
                        for g in range(4):
                            g_all = 4 * u + g
                            wait(sp, s_ot, g_all - 1)
                            sp.dma_start(lt[:, g % 2].rearrange("p j e -> p (j e)"),
                                         local_t[bass.ds(g_all * U, U), :].rearrange("j e -> (j e)").partition_broadcast(P))\
                              .then_inc(s_lt[g % 2], 16)
                            if g == 1 and not (isinstance(u, int) and u == 0):
                                sp.wait_ge(s_xe, u)
                                sp.dma_start(xp_t[bass.ds((u - 1) * P, P), :], xp_st[:]).then_inc(s_xs, 16)

                    unit(0, True)
                    with sp.Fori(1, NT - 1) as u:
                        unit(u, True)
                    unit(NT - 1, True, "last")
                    unit(NT, False, "none")
                    sp.wait_ge(s_xs, 16 * NT)

                @block.scalar
                def _(act):
                    def unit(u, has_x):
                        if has_x:
                            act.wait_ge(s_tr, u + 1)
                            nc.scalar.activation(xT[:].rearrange("p k n -> p (k n)"),
                                                 psum[:, 0:2].rearrange("p a b -> p (a b)"), ACT.Copy).then_inc(s_xT, 1)
                            act.wait_ge(s_xp, u + 1)
                            wait(act, s_xs, 16 * u)
                            nc.scalar.activation(xp_st[:], psum[:, 2:4].rearrange("p a b -> p (a b)"),
                                                 ACT.Copy).then_inc(s_xe, 1)
                    units(act, unit)

                @block.tensor
                def _(pe):
                    tiles = StepTiles(pe, dtab, "p1")
                    pe.wait_ge(s_w, 16 * KD)

                    def unit(u, has_x):
                        if has_x:
                            pe.wait_ge(s_xi, 16 * u + 16)
                            for k in range(KD):
                                last = nc.tensor.transpose(psum[:, k // 4, (k % 4) * P:(k % 4 + 1) * P],
                                                           xin[:, k * P:(k + 1) * P], ident[:])
                            last.then_inc(s_tr, 1)
                        for g in range(4):
                            g_all, s = 4 * u + g, g % 2
                            ds = tiles.load(g_all)
                            pe.wait_ge(s_ot, g_all + 1)
                            wait(pe, s_lg, g_all - 1)
                            for j in range(U):
                                last = nc.tensor.matmul(psum[:, 4 + s, j * 8:(j + 1) * 8], onehot_t[:, s, j, :],
                                                        nt0[:, bass.ds(ds[j], 1), :], start=True, stop=True)
                            last.then_inc(s_pg, 1)
                            if has_x:
                                if g == 0:
                                    pe.wait_ge(s_xT, u + 1)
                                for k in range(2 * g, 2 * g + 2):
                                    for i in range(2):
                                        if g == 0 and k == 0 and i == 0:
                                            wait(pe, s_xe, u)
                                        last = nc.tensor.matmul(psum[:, 2 + i], xT[:, k, :],
                                                                w_sb[:, k, i * 512:(i + 1) * 512],
                                                                start=(k == 0), stop=(k == KD - 1))
                                if g == 3:
                                    last.then_inc(s_xp, 1)
                    units(pe, unit)

                @block.vector
                def _(dve):
                    def onehots(g, s, m):
                        dve.wait_ge(s_lt[s], 16 * m + 16)
                        wait(dve, s_pg, g - 1)
                        nc.vector.tensor_scalar(onehot_t[:, s].rearrange("p j e -> p (j e)"),
                                                lt[:, s].rearrange("p j e -> p (j e)"), pidx[:], None,
                                                ALU.is_equal).then_inc(s_ot, 1)

                    def logits(g, s, m):
                        dve.wait_ge(s_pg, g + 1)
                        dve.wait_ge(s_ga[s], 64 * m + 64)
                        pv = psum[:, 4 + s, 0:8 * U].rearrange("p (j n) -> p j n", n=8)
                        nc.vector.tensor_tensor(esum[:, s], pv[:, :, 0:H], ga[:, s], ALU.add).then_inc(s_es, 1)
                        nc.vector.tensor_copy(w9[:, bass.ds(g * U, U), H:2 * H], pv[:, :, H:2 * H])
                        dve.wait_ge(s_es, g + 1)
                        nc.vector.scalar_tensor_tensor(out=w9[:, bass.ds(g * U, U), 0:H], in0=esum[:, s], scalar=SLOPE,
                                                       in1=esum[:, s], op0=ALU.mult, op1=ALU.max).then_inc(s_lg, 1)

                    def unit(u, _):
                        for g in range(4):
                            onehots(4 * u + g, g % 2, 2 * u + g // 2)
                            if g or not isinstance(u, int) or u:
                                gp = g - 1
                                logits(4 * u + gp, gp % 2, 2 * u + gp // 2)
                    units(dve, unit)
                    logits(NG - 1, 1, NG // 2 - 1)

        acc = keep("acc", [P, NT, D])
        zacc = keep("zacc", [P, NT, W9])
        weigh_edges(nc, sem, "l0", psum, w9, ident, isfirst, rs_f, rs_b, pen, any_f, any_b)

        with ExitStack() as ph:
            def sb(name, shape, dt=F32):
                return ph.enter_context(nc.sbuf_tensor(name, shape, dt))
            rows = sb("rows0", [P, 2, U, D])
            onehot = sb("onehot0", [P, 2, U, P])
            wone = sb("wone", [P, 2, U, H, P])
            idx = sb("idx2", [P, 2, U], I32)
            s_ix = sem("p2_ix")
            s_r = [sem(f"p2_r{i}") for i in range(2)]
            s_o = sem("p2_o")
            s_pd = sem("p2_pd")
            s_pa = sem("p2_pa")
            s_mm = sem("p2_mm")
            s_acc = sem("p2_acc")
            with nc.Block() as block:
                @block.gpsimd
                def _(pool):
                    gather = PoolGather(pool, N, bound)

                    def group(g, s, m):
                        gather.wait(s_r[s], 64 * m)
                        nc.gpsimd.tensor_copy(idx[:, s, :], isrc[:, bass.ds(g * U, U)]).then_inc(s_ix, 1)
                        gather.wait(s_ix, g + 1)
                        for j in range(U):
                            gather.wait(s_mm, (g - 2) * U + j + 1)
                            gather.rows_of(rows[:, s, j, :], xp_t, idx[:, s, j:j + 1]).then_inc(s_r[s], 16)
                    pipelined(pool, NG, [(0, group)])

                @block.scalar
                def _(act):
                    def weights(g, s, m):
                        act.wait_ge(s_o, g + 1)
                        for j in range(U):
                            wait(act, s_mm, (g - 2) * U + j + 1)
                            for h in range(DVE_HEADS, H):
                                last = nc.scalar.activation(wone[:, s, j, h, :], onehot[:, s, j, :], ACT.Copy,
                                                            scale=w9[:, bass.ds(g * U + j, 1), h:h + 1].rearrange("p a b -> p (a b)"))
                            last.then_inc(s_pa, 1)
                    pipelined(act, NG, [(0, weights)])

                @block.tensor
                def _(pe):
                    def group(g, s, m):
                        for j in range(U):
                            i = g * U + j
                            if j == 0:
                                pe.wait_ge(s_r[s], 64 * m + 64)
                            pe.wait_ge(s_pd, i + 1)
                            pe.wait_ge(s_pa, i + 1)
                            wait(pe, s_acc, i)
                            for h in range(H):
                                nc.tensor.matmul(psum[:, 2 * (j % 2) + h // 2, (h % 2) * C:(h % 2 + 1) * C],
                                                 wone[:, s, j, h, :], rows[:, s, j, h * C:(h + 1) * C],
                                                 start=True, stop=True)
                            nc.tensor.matmul(psum[:, 4 + j % 2, 0:W9], onehot[:, s, j, :],
                                             w9[:, bass.ds(i, 1), :], start=True, stop=True).then_inc(s_mm, 1)
                    pipelined(pe, NG, [(0, group)])

                @block.vector
                def _(dve):
                    tiles = StepTiles(dve, dtab, "p2")
                    nc.vector.memset(acc[:], 0.0).then_inc(s_acc, 1)
                    nc.vector.memset(zacc[:], 0.0)

                    def group(g, s, m, build=True, add=True):
                        if build:
                            wait(dve, s_mm, (g - 1) * U)
                            wait(dve, s_pa, (g - 1) * U)
                            nc.vector.tensor_tensor(
                                onehot[:, s], bc(iotar[:].unsqueeze(1), [P, U, P]),
                                bc(ldst[:, bass.ds(g * U, U)].unsqueeze(2), [P, U, P]), ALU.is_equal).then_inc(s_o, 1)
                        if add:
                            ds = tiles.load(g - 1)
                        for j in range(U):
                            if build:
                                for h in range(DVE_HEADS):
                                    last = nc.vector.tensor_scalar(
                                        wone[:, s, j, h, :], iotar[:], ldst[:, bass.ds(g * U + j, 1)],
                                        w9[:, bass.ds(g * U + j, 1), h:h + 1].rearrange("p a b -> p (a b)"),
                                        ALU.is_equal, ALU.mult)
                                last.then_inc(s_pd, 1)
                            if add:
                                i = (g - 1) * U + j
                                dve.wait_ge(s_mm, i + 1)
                                dve.wait_ge(s_acc, i + 1)
                                av = acc[:, bass.ds(ds[j], 1), :].rearrange("p a n -> p (a n)")
                                zv = zacc[:, bass.ds(ds[j], 1), :].rearrange("p a n -> p (a n)")
                                nc.vector.tensor_tensor(zv, psum[:, 4 + j % 2, 0:W9], zv, ALU.add)
                                nc.vector.tensor_tensor(av, psum[:, 2 * (j % 2):2 * (j % 2) + 2].rearrange("p a b -> p (a b)"),
                                                        av, ALU.add).then_inc(s_acc, 1)
                    pipelined(dve, NG, [(0, lambda g, s, m: group(g, s, m, True, not (isinstance(g, int) and g == 0)))])
                    group(NG, 0, NG // 2, False, True)

        xr = acc[:, :, 0:XRW]
        acc1 = acc[:, :, 2 * C:2 * C + ACC1]
        acc1_odd = acc[:, :, 0:ACC1]
        with ExitStack() as ph:
            def sb(name, shape, dt=F32):
                return ph.enter_context(nc.sbuf_tensor(name, shape, dt))
            wd = sb("wd", [P, KD, HID])
            rmsw = sb("rmsw", [P, KD])
            wlr = sb("wlr", [P, KH, 2 * HID])
            bias_bc = sb("bias_bc", [P, D])
            att_bc = sb("att_bc", [P, HID])
            noself = sb("noself", [P, NT])
            wself = sb("wself", [P, NT, H])
            rz = sb("rz", [P, NT, H])
            sw = sb("sw", [P, NT, H])
            eps = sb("eps", [P, 2])
            xpt = sb("xpt", [P, 2, D])
            xin = sb("xin5", [P, 2, D])
            y = sb("y", [P, 2, D])
            sq = sb("sq", [P, D])
            xT = sb("xT5", [P, 2, KD, P])
            st = sb("st5", [P, 2, 12])
            mv = sb("mv", [P, 2, 2])
            mark = sb("mark5", [P, 1])
            sd = sb("sd", [P, 2])
            rs = sb("rs", [P, 2, 2])
            ss = sb("ss", [P, 2])
            sr = sb("sr", [P, 2])
            rr = sb("rr", [P, 2])
            hd = sb("hd", [P, 2, HID])
            hT = sb("hT", [P, 2, KH, P])
            xls = sb("xls", [P, 2, XLW])
            tmp = sb("tmp5", [P, 2 * HID])
            tmp2 = sb("tmp52", [P, HID])
            linear = sb("linear", [P, 2, 2 * H])
            relu_part = sb("relu_part", [P, H])
            both = sb("both", [P, H])
            att_lin = sb("att_lin", [P, HID])
            att_relu = sb("att_relu", [P, HID])
            names = "ldw clr z wd y0 B mv sd D rs x1 E sr rr tr xT hp hd ht hT lr xlr sf att".split()
            S = {n: sem("n_" + n) for n in names}
            s_ld = [sem(f"n_ld{i}") for i in range(2)]
            s_x1s = [sem(f"n_x1s{i}") for i in range(2)]
            s_xls = [sem(f"n_xls{i}") for i in range(2)]
            N_LDW = 4 + KH * 2
            AHEAD = 8
            with nc.Block() as block:
                @block.gpsimd
                def _(pool):
                    nc.gpsimd.memset(xin[:], 0.0).then_inc(S["clr"], 1)
                    nc.gpsimd.memset(eps[:, 0:1], LN_EPS).then_inc(S["clr"], 1)
                    nc.gpsimd.memset(eps[:, 1:2], RMS_EPS).then_inc(S["clr"], 1)

                @block.sync
                def _(sp):
                    with nc.allow_non_contiguous_dma(reason="rms weights by rows of W_down, once"):
                        sp.dma_start(rmsw[:], rms_w.rearrange("(k p) -> p k", p=P)).then_inc(S["ldw"], 16)
                    sp.dma_start(wd[:], w_down.rearrange("(k p) n -> p k n", p=P)).then_inc(S["ldw"], 16)
                    sp.dma_start(bias_bc[:], bias.partition_broadcast(P)).then_inc(S["ldw"], 16)
                    sp.dma_start(att_bc[:], att1.rearrange("h c -> (h c)").partition_broadcast(P)).then_inc(S["ldw"], 16)
                    for k in range(KH):
                        sp.dma_start(wlr[:, k, 0:HID], wl[k * P:(k + 1) * P, :]).then_inc(S["ldw"], 16)
                        sp.dma_start(wlr[:, k, HID:2 * HID], wr[k * P:(k + 1) * P, :]).then_inc(S["ldw"], 16)
                    sp.wait_ge(S["clr"], 1)

                    def load(t, s, m):
                        wait(sp, S["mv"], t - 1)
                        rows = N_LAST if isinstance(t, int) and t == NT - 1 else P
                        sp.dma_start(xpt[:, s, :], xp_t[bass.ds(t * P, P), :]).then_inc(s_ld[s], 16)
                        sp.dma_start(xin[0:rows, s, :], x[bass.ds(t * P, rows), :]).then_inc(s_ld[s], 16)

                    def store_x1(t, s, m):
                        sp.wait_ge(S["x1"], t + 1)
                        sp.dma_start(x1_t[bass.ds(t * P, P), :], y[:, s, :]).then_inc(s_x1s[s], 16)

                    def store_xl(t, s, m):
                        sp.wait_ge(S["sf"], t + 1)
                        sp.dma_start(xl_t[bass.ds(t * P, P), :], xls[:, s, :]).then_inc(s_xls[s], 16)
                    pipelined(sp, NT, [(0, load), (2, store_x1), (5, store_xl)], AHEAD)
                    for s in range(2):
                        sp.wait_ge(s_x1s[s], 16 * ((NT + 1 - s) // 2))
                        sp.wait_ge(s_xls[s], 16 * ((NT + 1 - s) // 2))

                @block.scalar
                def _(act):
                    act.wait_ge(S["z"], 1)
                    act.wait_ge(S["clr"], 3)

                    def divide(t, s, m):
                        wait(act, S["tr"], t - 1)
                        wait(act, s_x1s[s], 16 * m)
                        for h in range(H):
                            last = nc.scalar.activation(
                                y[:, s, h * C:(h + 1) * C],
                                acc[:, bass.ds(t, 1), h * C:(h + 1) * C].rearrange("p a n -> p (a n)"), ACT.Copy,
                                scale=rz[:, bass.ds(t, 1), h:h + 1].rearrange("p a n -> p (a n)"))
                        last.then_inc(S["y0"], 1)

                    def deviation(t, s, m):
                        act.wait_ge(S["mv"], t + 1)
                        nc.scalar.activation(sd[:, s:s + 1], mv[:, s, 1:2], ACT.Sqrt, bias=eps[:, 0:1]).then_inc(S["sd"], 1)

                    def normalise(t, s, m):
                        act.wait_ge(S["rs"], t + 1)
                        nc.scalar.activation(y[:, s, :], y[:, s, :], ACT.Identity, bias=rs[:, s, 1:2],
                                             scale=rs[:, s, 0:1]).then_inc(S["x1"], 1)
                        act.wait_ge(S["x1"], t + 1)
                        wait(act, S["E"], t)
                        nc.scalar.activation(sq[:], y[:, s, :], ACT.Square, accum_out=ss[:, s:s + 1]).then_inc(S["E"], 1)
                        act.wait_ge(S["E"], t + 1)
                        nc.scalar.activation(sr[:, s:s + 1], ss[:, s:s + 1], ACT.Sqrt, bias=eps[:, 1:2],
                                             scale=1.0 / D).then_inc(S["sr"], 1)

                    def take_xT(t, s, m):
                        act.wait_ge(S["tr"], t + 1)
                        wait(act, S["hp"], t - 1)
                        nc.scalar.activation(xT[:, s].rearrange("p k n -> p (k n)"),
                                             psum[:, 2 * s:2 * s + 2].rearrange("p a b -> p (a b)"),
                                             ACT.Copy).then_inc(S["xT"], 1)

                    def take_hT(t, s, m):
                        act.wait_ge(S["ht"], t + 1)
                        wait(act, S["lr"], t - 1)
                        nc.scalar.activation(hT[:, s].rearrange("p k n -> p (k n)"), psum[:, 5, 0:HID],
                                             ACT.Copy).then_inc(S["hT"], 1)

                    def take_xlr(t, s, m):
                        act.wait_ge(S["lr"], t + 1)
                        wait(act, S["sf"], t - 1)
                        wait(act, s_xls[s], 16 * m)
                        nc.scalar.activation(xls[:, s, 0:HID], psum[:, 6 + s, 0:HID], ACT.Copy).then_inc(S["xlr"], 1)
                        nc.scalar.activation(xr[:, bass.ds(t, 1), 0:HID].rearrange("p a n -> p (a n)"),
                                             psum[:, 6 + s, HID:2 * HID], ACT.Copy).then_inc(S["xlr"], 1)
                    pipelined(act, NT, [(2, deviation), (4, take_hT), (5, take_xlr), (2, normalise), (1, divide),
                                        (2, take_xT)], AHEAD)

                @block.tensor
                def _(pe):
                    pe.wait_ge(S["wd"], 1)

                    def transposes(t, s, m):
                        pe.wait_ge(S["x1"], t + 1)
                        wait(pe, S["xT"], t - 1)
                        for k in range(KD):
                            last = nc.tensor.transpose(psum[:, 2 * s + k // 4, (k % 4) * P:(k % 4 + 1) * P],
                                                       y[:, s, k * P:(k + 1) * P], ident[:])
                        last.then_inc(S["tr"], 1)

                    def down(t, s, m):
                        pe.wait_ge(S["xT"], t + 1)
                        wait(pe, S["hd"], t)
                        for k in range(KD):
                            last = nc.tensor.matmul(psum[:, 4, 0:HID], xT[:, s, k, :], wd[:, k, :],
                                                    start=(k == 0), stop=(k == KD - 1))
                        last.then_inc(S["hp"], 1)

                    def transposes_h(t, s, m):
                        pe.wait_ge(S["hd"], t + 1)
                        wait(pe, S["hT"], t)
                        for k in range(KH):
                            last = nc.tensor.transpose(psum[:, 5, k * P:(k + 1) * P], hd[:, s, k * P:(k + 1) * P], ident[:])
                        last.then_inc(S["ht"], 1)

                    def left_right(t, s, m):
                        pe.wait_ge(S["hT"], t + 1)
                        wait(pe, S["xlr"], 2 * t - 2)
                        for k in range(KH):
                            last = nc.tensor.matmul(psum[:, 6 + s, :], hT[:, s, k, :], wlr[:, k, :],
                                                    start=(k == 0), stop=(k == KH - 1))
                        last.then_inc(S["lr"], 1)
                    pipelined(pe, NT, [(4, transposes_h), (3, down), (4, left_right), (2, transposes)], AHEAD)

                @block.vector
                def _(dve):
                    divisor(nc, dve, sem("n_zc"), zacc, noself, wself, rz, sw, 0.0).then_inc(S["z"], 1)
                    dve.wait_ge(S["ldw"], 16 * N_LDW)
                    for k in range(KD):
                        last = nc.vector.tensor_scalar(wd[:, k, :], wd[:, k, :], rmsw[:, k:k + 1], None, ALU.mult)
                    last.then_inc(S["wd"], 1)
                    nc.vector.tensor_scalar(att_lin[:], att_bc[:], SLOPE, None, ALU.mult)
                    nc.vector.tensor_scalar(att_relu[:], att_bc[:], 1.0 - SLOPE, None, ALU.mult).then_inc(S["att"], 1)
                    dve.wait_ge(S["att"], 1)
                    linkB = Chain(dve, S["B"], 4)
                    linkD = Chain(dve, S["D"], 1)

                    def combine(t, s, m):
                        linkB.tile(t)
                        dve.wait_ge(S["y0"], t + 1)
                        dve.wait_ge(s_ld[s], 32 * m + 32)
                        for h in range(H):
                            cols = slice(h * C, (h + 1) * C)
                            last = nc.vector.scalar_tensor_tensor(
                                out=y[:, s, cols], in0=xpt[:, s, cols],
                                scalar=sw[:, bass.ds(t, 1), h:h + 1].rearrange("p a n -> p (a n)"),
                                in1=y[:, s, cols], op0=ALU.mult, op1=ALU.add)
                        linkB(last)
                        linkB(nc.vector.tensor_tensor(y[:, s], y[:, s], bias_bc[:], ALU.add))
                        linkB(nc.vector.scalar_tensor_tensor(out=y[:, s], in0=y[:, s], scalar=0.0, in1=xin[:, s],
                                                             op0=ALU.max, op1=ALU.add))
                        for i in range(2):
                            last = nc.vector.bn_stats(st[:, s, 6 * i:6 * i + 6], y[:, s, i * 512:(i + 1) * 512])
                        linkB(last)
                        nc.vector.tensor_copy(mark[:], st[:, s, 0:1])
                        nc.vector.bn_aggr(mv[:, s, :], st[:, s, :]).then_inc(S["mv"], 1)

                    def factors(t, s, m):
                        linkD.tile(t)
                        dve.wait_ge(S["sd"], t + 1)
                        linkD(nc.vector.reciprocal(rs[:, s, 0:1], sd[:, s:s + 1]))
                        nc.vector.tensor_scalar(rs[:, s, 1:2], mv[:, s, 0:1], rs[:, s, 0:1], -1.0, ALU.mult, ALU.mult)\
                            .then_inc(S["rs"], 1)

                    def rms(t, s, m):
                        dve.wait_ge(S["sr"], t + 1)
                        nc.vector.reciprocal(rr[:, s:s + 1], sr[:, s:s + 1]).then_inc(S["rr"], 1)

                    def scale_h(t, s, m):
                        dve.wait_ge(S["hp"], t + 1)
                        dve.wait_ge(S["rr"], t + 1)
                        wait(dve, S["ht"], t - 1)
                        nc.vector.tensor_scalar(hd[:, s, :], psum[:, 4, 0:HID], rr[:, s:s + 1], None, ALU.mult)\
                            .then_inc(S["hd"], 1)

                    linkS = Chain(dve, sem("n_sfc"), 4)

                    def self_logit(t, s, m):
                        linkS.tile(t)
                        xrt = xr[:, bass.ds(t, 1), :].rearrange("p a n -> p (a n)")
                        dve.wait_ge(S["xlr"], 2 * t + 2)
                        wait(dve, S["sf"], t)
                        nc.vector.tensor_tensor(tmp[:, 0:HID], xls[:, s, 0:HID], att_lin[:], ALU.mult)
                        nc.vector.tensor_tensor(tmp[:, HID:2 * HID], xrt[:, 0:HID], att_lin[:], ALU.mult)
                        linkS(nc.vector.tensor_tensor(tmp2[:], xls[:, s, 0:HID], xrt[:, 0:HID], ALU.add))
                        linkS(nc.vector.scalar_tensor_tensor(out=tmp2[:], in0=tmp2[:], scalar=0.0, in1=att_relu[:],
                                                             op0=ALU.max, op1=ALU.mult))
                        nc.vector.tensor_reduce(out=linear[:, s, :], in_=tmp[:].rearrange("p (h c) -> p h c", c=HD),
                                                op=ALU.add, axis=AX.X)
                        linkS(nc.vector.tensor_reduce(out=relu_part[:], in_=tmp2[:].rearrange("p (h c) -> p h c", h=H),
                                                      op=ALU.add, axis=AX.X))
                        nc.vector.tensor_copy(xls[:, s, HID:XLW], linear[:, s, 0:H])
                        nc.vector.tensor_copy(xrt[:, HID:XLW], linear[:, s, H:2 * H])
                        linkS(nc.vector.tensor_tensor(both[:], linear[:, s, 0:H], linear[:, s, H:2 * H], ALU.add))
                        nc.vector.tensor_tensor(xrt[:, XLW:XRW], relu_part[:], both[:], ALU.add).then_inc(S["sf"], 1)
                    pipelined(dve, NT, [(2, factors), (1, combine), (2, rms), (3, scale_h), (5, self_logit)], AHEAD)

        with ExitStack() as ph:
            def sb(name, shape, dt=F32):
                return ph.enter_context(nc.sbuf_tensor(name, shape, dt))
            att_bc = sb("att_bc6", [P, HID])
            RING = 4
            lt = sb("lt6", [P, 2, U, P])
            onehot_t = sb("onehot_t6", [P, 2, U, P])
            rows = sb("rows6", [P, RING, U, XLW])
            msg = sb("msg6", [P, 2, U, XLW])
            prod = sb("prod6", [P, 2, U, HID])
            part = sb("part6", [P, 2, U, H])
            att_relu = sb("att_relu6", [P, HID])
            idx = sb("idx6", [P, RING, U], I32)
            s_att = sem("q_att")
            s_lt = [sem(f"q_lt{i}") for i in range(2)]
            s_r = [sem(f"q_r{i}") for i in range(RING)]
            s_xe = [sem(f"q_xe{i}") for i in range(RING)]
            s_ix, s_ot, s_pg, s_ad, s_pr, s_sc, s_pd, s_pt, s_rd = (sem("q_" + n) for n in
                                                              "ix ot pg ad pr sc pd pt rd".split())
            with nc.Block() as block:
                @block.gpsimd
                def _(pool):
                    gather = PoolGather(pool, N, bound)

                    def group(g, s, m):
                        gather.wait(s_r[s], 64 * m)
                        nc.gpsimd.tensor_copy(idx[:, s, :], isrc[:, bass.ds(g * U, U)]).then_inc(s_ix, 1)
                        gather.wait(s_ix, g + 1)
                        gather.wait(s_ad, g - RING + 1)
                        gather.wait(s_xe[s], 16 * m)
                        for j in range(U):
                            gather.rows_of(rows[:, s, j, :], xl_t, idx[:, s, j:j + 1]).then_inc(s_r[s], 16)
                    pipelined(pool, NG, [(0, group)], RING, RING)

                @block.sync
                def _(sp):
                    sp.dma_start(att_bc[:], att1.rearrange("h c -> (h c)").partition_broadcast(P)).then_inc(s_att, 16)

                    def load(g, s, m):
                        wait(sp, s_ot, g - 1)
                        s = s % 2
                        sp.dma_start(lt[:, s].rearrange("p j e -> p (j e)"),
                                     local_t[bass.ds(g * U, U), :].rearrange("j e -> (j e)").partition_broadcast(P))\
                          .then_inc(s_lt[s], 16)

                    def store_rows(g, s, m):
                        sp.wait_ge(s_r[s], 64 * m + 64)
                        sp.dma_start(xe_t[bass.ds(g, 1)].rearrange("a p n -> p (a n)"),
                                     rows[:, s].rearrange("p j n -> p (j n)")).then_inc(s_xe[s], 16)
                    pipelined(sp, NG, [(1, store_rows), (0, load)], RING, RING)
                    for s in range(RING):
                        sp.wait_ge(s_xe[s], 16 * NG // RING)

                @block.scalar
                def _(act):
                    def self_logits(g, s, m):
                        act.wait_ge(s_ad, g + 1)
                        nc.scalar.activation(w9[:, bass.ds(g * U, U), H:2 * H], psum[:, 4 * s:4 * s + 4, XLW:XRW],
                                             ACT.Copy).then_inc(s_sc, 1)
                    pipelined(act, NG, [(1, self_logits)])

                @block.tensor
                def _(pe):
                    tiles = StepTiles(pe, dtab, "q1")

                    def group(g, s, m):
                        ds = tiles.load(g)
                        pe.wait_ge(s_ot, g + 1)
                        wait(pe, s_sc, g - 1)
                        for j in range(U):
                            last = nc.tensor.matmul(psum[:, 4 * s + j, 0:XRW], onehot_t[:, s, j, :],
                                                    xr[:, bass.ds(ds[j], 1), :], start=True, stop=True)
                        last.then_inc(s_pg, 1)
                    pipelined(pe, NG, [(0, group)])

                @block.vector
                def _(dve):
                    dve.wait_ge(s_att, 16)
                    nc.vector.tensor_scalar(att_relu[:], att_bc[:], 1.0 - SLOPE, None, ALU.mult).then_inc(s_pr, 1)
                    dve.wait_ge(s_pr, 1)

                    def onehots(g, s, m):
                        s2, m2 = s % 2, (RING // 2) * m + s // 2
                        dve.wait_ge(s_lt[s2], 16 * m2 + 16)
                        wait(dve, s_pg, g - 1)
                        nc.vector.tensor_scalar(onehot_t[:, s2].rearrange("p j e -> p (j e)"),
                                                lt[:, s2].rearrange("p j e -> p (j e)"), pidx[:], None,
                                                ALU.is_equal).then_inc(s_ot, 1)

                    def add(g, s, m):
                        dve.wait_ge(s_pg, g + 1)
                        dve.wait_ge(s_r[s], 64 * m + 64)
                        wait(dve, s_rd, g - 1)
                        s2 = s % 2
                        nc.vector.tensor_tensor(msg[:, s2], psum[:, 4 * s2:4 * s2 + 4, 0:XLW], rows[:, s], ALU.add)\
                            .then_inc(s_ad, 1)

                    def reduce(g, s, m):
                        s = s % 2
                        dve.wait_ge(s_ad, g + 1)
                        wait(dve, s_rd, g - 1)
                        nc.vector.scalar_tensor_tensor(out=prod[:, s], in0=msg[:, s, :, 0:HID], scalar=0.0,
                                                       in1=bc(att_relu[:].unsqueeze(1), [P, U, HID]),
                                                       op0=ALU.max, op1=ALU.mult).then_inc(s_pd, 1)
                        dve.wait_ge(s_pd, g + 1)
                        nc.vector.tensor_reduce(out=part[:, s], in_=prod[:, s].rearrange("p j (h c) -> p j h c", h=H),
                                                op=ALU.add, axis=AX.X).then_inc(s_pt, 1)
                        dve.wait_ge(s_pt, g + 1)
                        nc.vector.tensor_tensor(w9[:, bass.ds(g * U, U), 0:H], part[:, s], msg[:, s, :, HID:XLW],
                                                ALU.add).then_inc(s_rd, 1)
                    pipelined(dve, NG, [(0, onehots), (1, add), (2, reduce)], RING, RING)

        weigh_edges(nc, sem, "l1", psum, w9, ident, isfirst, rs_f, rs_b, pen, any_f, any_b)

        with ExitStack() as ph:
            def sb(name, shape, dt=F32):
                return ph.enter_context(nc.sbuf_tensor(name, shape, dt))
            U2 = 2 * U
            NG2 = T // U2
            rows = sb("rows8", [P, 2, U2, XLW])
            onehot = sb("onehot8", [P, 2, U2, P])
            msg = sb("msg8", [P, 2, U2, ACC1])
            s_r = [sem(f"r_r{i}") for i in range(2)]
            s_o, s_ms, s_ma, s_mm, s_acc = (sem("r_" + n) for n in "o ms ma mm acc".split())
            with nc.Block() as block:
                @block.sync
                def _(sp):
                    def load(g, s, m):
                        wait(sp, s_ma, (g - 1) * U2)
                        wait(sp, s_ms, g - 1)
                        sp.dma_start(rows[:, s].rearrange("p (a j) n -> p a (j n)", a=2),
                                     xe_t.rearrange("(g a) p n -> g a p n", a=2)[bass.ds(g, 1)]
                                     .rearrange("g a p n -> p (g a) n")).then_inc(s_r[s], 16)
                    pipelined(sp, NG2, [(0, load)])

                @block.scalar
                def _(act):
                    def weights(g, s, m):
                        wait(act, s_mm, (g - 1) * U2)
                        nc.scalar.activation(msg[:, s, :, HID:ACC1], w9[:, bass.ds(g * U2, U2), :], ACT.Copy)
                        act.wait_ge(s_r[s], 16 * m + 16)
                        for j in range(U2):
                            for h in range(DVE_HEADS1, H):
                                cols = slice(h * HD, (h + 1) * HD)
                                last = nc.scalar.activation(
                                    msg[:, s, j, cols], rows[:, s, j, cols], ACT.Copy,
                                    scale=w9[:, bass.ds(g * U2 + j, 1), h:h + 1].rearrange("p a b -> p (a b)"))
                            last.then_inc(s_ma, 1)
                    pipelined(act, NG2, [(0, weights)])

                @block.tensor
                def _(pe):
                    def group(g, s, m):
                        pe.wait_ge(s_o, g + 1)
                        pe.wait_ge(s_ms, g + 1)
                        for j in range(U2):
                            pe.wait_ge(s_ma, g * U2 + j + 1)
                            wait(pe, s_acc, g * U2 + j - 5)
                            nc.tensor.matmul(psum[:, j, 0:ACC1], onehot[:, s, j, :], msg[:, s, j, :],
                                             start=True, stop=True).then_inc(s_mm, 1)
                    pipelined(pe, NG2, [(0, group)])

                @block.vector
                def _(dve):
                    tiles = StepTiles(dve, dtab, "r1", U2)
                    nc.vector.memset(acc1, 0.0).then_inc(s_acc, 1)
                    nc.vector.memset(acc1_odd, 0.0).then_inc(s_acc, 1)
                    wide = DVE_HEADS1 * HD

                    def build(g, s, m):
                        wait(dve, s_mm, (g - 1) * U2)
                        nc.vector.tensor_tensor(
                            onehot[:, s], bc(iotar[:].unsqueeze(1), [P, U2, P]),
                            bc(ldst[:, bass.ds(g * U2, U2)].unsqueeze(2), [P, U2, P]), ALU.is_equal).then_inc(s_o, 1)
                        dve.wait_ge(s_r[s], 16 * m + 16)
                        nc.vector.tensor_tensor(
                            msg[:, s, :, 0:wide].rearrange("p j (h c) -> p j h c", c=HD),
                            rows[:, s, :, 0:wide].rearrange("p j (h c) -> p j h c", c=HD),
                            bc(w9[:, bass.ds(g * U2, U2), 0:DVE_HEADS1].unsqueeze(3), [P, U2, DVE_HEADS1, HD]),
                            ALU.mult).then_inc(s_ms, 1)

                    def add(g, s, m):
                        ds = tiles.load(g)
                        for j in range(U2):
                            i = g * U2 + j
                            dve.wait_ge(s_mm, i + 1)
                            dve.wait_ge(s_acc, i + 1)
                            sums = acc1_odd if j % 2 else acc1
                            av = sums[:, bass.ds(ds[j], 1), :].rearrange("p a n -> p (a n)")
                            nc.vector.tensor_tensor(av, psum[:, j, 0:ACC1], av, ALU.add).then_inc(s_acc, 1)
                    pipelined(dve, NG2, [(0, build), (1, add)])
                    dve.wait_ge(s_acc, T + 2)
                    nc.vector.tensor_tensor(acc1, acc1, acc1_odd, ALU.add)

        with ExitStack() as ph:
            def sb(name, shape, dt=F32):
                return ph.enter_context(nc.sbuf_tensor(name, shape, dt))
            wu = sb("wu", [P, KH, D])
            noself = sb("noself9", [P, NT])
            wself = sb("wself9", [P, NT, H])
            rz = sb("rz9", [P, NT, H])
            sw = sb("sw9", [P, NT, H])
            eps = sb("eps9", [P, 1])
            xl_in = sb("xl_in", [P, 2, HID])
            x1_in = sb("x1_in", [P, 2, D])
            gsum = sb("gsum", [P, 2, HID])
            gT = sb("gT", [P, 2, KH, P])
            y = sb("y9", [P, 2, D])
            o = sb("o9", [P, 2, D])
            st = sb("st9", [P, 2, 12])
            mv = sb("mv9", [P, 2, 2])
            mark = sb("mark9", [P, 1])
            sd = sb("sd9", [P, 2])
            rs = sb("rs9", [P, 2, 2])
            F = {n: sem("f_" + n) for n in "w z eps g0 g tr gT up s mv sd D rs o".split()}
            s_xl = [sem(f"f_xl{i}") for i in range(2)]
            s_x1 = [sem(f"f_x1{i}") for i in range(2)]
            s_out = [sem(f"f_out{i}") for i in range(2)]
            AHEAD = 6
            with nc.Block() as block:
                @block.sync
                def _(sp):
                    sp.dma_start(wu[:], w_up.rearrange("(k p) n -> p k n", p=P)).then_inc(F["w"], 16)

                    def load_xl(t, s, m):
                        wait(sp, F["g"], t - 1)
                        sp.dma_start(xl_in[:, s, :], xl_t[bass.ds(t * P, P), 0:HID]).then_inc(s_xl[s], 16)

                    def load_x1(t, s, m):
                        wait(sp, F["s"], 2 * t - 2)
                        sp.dma_start(x1_in[:, s, :], x1_t[bass.ds(t * P, P), :]).then_inc(s_x1[s], 16)

                    def store(t, s, m):
                        sp.wait_ge(F["o"], t + 1)
                        rows = N_LAST if isinstance(t, int) and t == NT - 1 else P
                        sp.dma_start(out[bass.ds(t * P, rows), :], o[0:rows, s, :]).then_inc(s_out[s], 16)
                    pipelined(sp, NT, [(0, load_xl), (2, load_x1), (4, store)], AHEAD)
                    for s in range(2):
                        sp.wait_ge(s_out[s], 16 * ((NT + 1 - s) // 2))

                @block.gpsimd
                def _(pool):
                    nc.gpsimd.memset(eps[:], LN_EPS).then_inc(F["eps"], 1)

                @block.scalar
                def _(act):
                    act.wait_ge(F["z"], 1)
                    act.wait_ge(F["eps"], 1)

                    def divide(t, s, m):
                        wait(act, F["tr"], t - 1)
                        for h in range(H):
                            last = nc.scalar.activation(
                                gsum[:, s, h * HD:(h + 1) * HD],
                                acc1[:, bass.ds(t, 1), h * HD:(h + 1) * HD].rearrange("p a n -> p (a n)"), ACT.Copy,
                                scale=rz[:, bass.ds(t, 1), h:h + 1].rearrange("p a n -> p (a n)"))
                        last.then_inc(F["g0"], 1)

                    def take_gT(t, s, m):
                        act.wait_ge(F["tr"], t + 1)
                        wait(act, F["up"], t - 1)
                        nc.scalar.activation(gT[:, s].rearrange("p k n -> p (k n)"), psum[:, s, 0:HID],
                                             ACT.Copy).then_inc(F["gT"], 1)

                    def deviation(t, s, m):
                        act.wait_ge(F["mv"], t + 1)
                        nc.scalar.activation(sd[:, s:s + 1], mv[:, s, 1:2], ACT.Sqrt, bias=eps[:, 0:1]).then_inc(F["sd"], 1)

                    def normalise(t, s, m):
                        act.wait_ge(F["rs"], t + 1)
                        wait(act, s_out[s], 16 * m)
                        nc.scalar.activation(o[:, s, :], y[:, s, :], ACT.Identity, bias=rs[:, s, 1:2],
                                             scale=rs[:, s, 0:1]).then_inc(F["o"], 1)
                    pipelined(act, NT, [(4, deviation), (1, divide), (2, take_gT), (4, normalise)], AHEAD)

                @block.tensor
                def _(pe):
                    pe.wait_ge(F["w"], 16)

                    def transposes(t, s, m):
                        pe.wait_ge(F["g"], t + 1)
                        wait(pe, F["gT"], t - 1)
                        for k in range(KH):
                            last = nc.tensor.transpose(psum[:, s, k * P:(k + 1) * P], gsum[:, s, k * P:(k + 1) * P], ident[:])
                        last.then_inc(F["tr"], 1)

                    def up(t, s, m):
                        pe.wait_ge(F["gT"], t + 1)
                        wait(pe, F["s"], 2 * t - 2)
                        for k in range(KH):
                            for i in range(2):
                                last = nc.tensor.matmul(psum[:, 2 + 2 * s + i, :], gT[:, s, k, :],
                                                        wu[:, k, i * 512:(i + 1) * 512], start=(k == 0), stop=(k == KH - 1))
                        last.then_inc(F["up"], 1)
                    pipelined(pe, NT, [(2, up), (1, transposes)], AHEAD)

                @block.vector
                def _(dve):
                    divisor(nc, dve, sem("f_zc"), acc1[:, :, HID:ACC1], noself, wself, rz, sw, DEN_EPS)\
                        .then_inc(F["z"], 1)
                    linkD = Chain(dve, F["D"], 1)

                    def add_self(t, s, m):
                        dve.wait_ge(F["g0"], t + 1)
                        dve.wait_ge(s_xl[s], 16 * m + 16)
                        for h in range(H):
                            cols = slice(h * HD, (h + 1) * HD)
                            last = nc.vector.scalar_tensor_tensor(
                                out=gsum[:, s, cols], in0=xl_in[:, s, cols],
                                scalar=sw[:, bass.ds(t, 1), h:h + 1].rearrange("p a n -> p (a n)"),
                                in1=gsum[:, s, cols], op0=ALU.mult, op1=ALU.add)
                        last.then_inc(F["g"], 1)

                    def residual(t, s, m):
                        dve.wait_ge(F["up"], t + 1)
                        dve.wait_ge(s_x1[s], 16 * m + 16)
                        wait(dve, F["o"], t - 1)
                        nc.vector.tensor_tensor(y[:, s], psum[:, 2 + 2 * s:4 + 2 * s].rearrange("p a b -> p (a b)"),
                                                x1_in[:, s], ALU.add).then_inc(F["s"], 1)
                        dve.wait_ge(F["s"], 2 * t + 1)
                        for i in range(2):
                            last = nc.vector.bn_stats(st[:, s, 6 * i:6 * i + 6], y[:, s, i * 512:(i + 1) * 512])
                        last.then_inc(F["s"], 1)
                        dve.wait_ge(F["s"], 2 * t + 2)
                        nc.vector.tensor_copy(mark[:], st[:, s, 0:1])
                        nc.vector.bn_aggr(mv[:, s, :], st[:, s, :]).then_inc(F["mv"], 1)

                    def factors(t, s, m):
                        linkD.tile(t)
                        dve.wait_ge(F["sd"], t + 1)
                        linkD(nc.vector.reciprocal(rs[:, s, 0:1], sd[:, s:s + 1]))
                        nc.vector.tensor_scalar(rs[:, s, 1:2], mv[:, s, 0:1], rs[:, s, 0:1], -1.0, ALU.mult, ALU.mult)\
                            .then_inc(F["rs"], 1)
                    pipelined(dve, NT, [(4, factors), (1, add_self), (3, residual)], AHEAD)


def divisor(nc, dve, chain, z9, noself, wself, rz, sw, eps):
    link = Chain(dve, chain)
    link(nc.vector.tensor_scalar(noself[:], z9[:, :, 2 * H], -1.0, 1.0, ALU.mult, ALU.add))
    link(nc.vector.tensor_tensor(wself[:], z9[:, :, H:2 * H], bc(noself[:].unsqueeze(2), [P, NT, H]), ALU.add))
    link(nc.vector.tensor_tensor(rz[:], z9[:, :, 0:H], wself[:], ALU.add))
    if eps:
        link(nc.vector.tensor_scalar_add(rz[:], rz[:], eps))
    link(nc.vector.reciprocal(rz[:], rz[:]))
    return nc.vector.tensor_tensor(sw[:], wself[:], rz[:], ALU.mult)


N_EDGE_DMAS = 3 + 2 * NB


def weigh_edges(nc, sem, tag, psum, w9, ident, isfirst, rs_f, rs_b, pen, any_f, any_b):
    with ExitStack() as ph:
        def sb(name, shape, dt=F32):
            return ph.enter_context(nc.sbuf_tensor(f"{tag}_{name}", shape, dt))
        v = sb("v", [TB, NB, H, P])
        sv = sb("sv", [TB, NB, H, P])
        fw = sb("fw", [TB, NB, H, P])
        bw = sb("bw", [TB, NB, H, P])
        cf = sb("cf", [H, T + 1])
        cb = sb("cb", [H, T + 1])
        cin = sb("cin", [TB, 2, NB, H])
        s_t1 = sem(f"{tag}_t1")
        s_sv = sem(f"{tag}_sv")
        s_dv = sem(f"{tag}_chain")
        s_f1 = sem(f"{tag}_f1")
        s_t2 = sem(f"{tag}_t2")
        s_c = sem(f"{tag}_c")
        s_t3 = sem(f"{tag}_t3")
        s_m = sem(f"{tag}_m")
        s_e = sem(f"{tag}_e")
        s_t4 = sem(f"{tag}_t4")
        with nc.Block() as block:
            @block.tensor
            def _(pe):
                for b in range(NB):
                    for h in range(H):
                        for i in range(2):
                            last = nc.tensor.transpose(psum[0:TB, 4 * i + b, h * P:(h + 1) * P],
                                                       w9[:, b * TB:(b + 1) * TB, i * H + h], ident[:])
                    last.then_inc(s_t1, 1)
                pe.wait_ge(s_f1, 1)
                pe.wait_ge(s_sv, NB)
                for b in range(NB):
                    nc.tensor.transpose(psum[0:H, 0, b * TB:(b + 1) * TB], fw[:, b, :, P - 1], ident[0:TB, 0:TB])
                    last = nc.tensor.transpose(psum[0:H, 1, b * TB:(b + 1) * TB], bw[:, b, :, 0], ident[0:TB, 0:TB])
                last.then_inc(s_t2, 1)
                pe.wait_ge(s_c, 1)
                for b in range(NB):
                    nc.tensor.transpose(psum[0:TB, 2, b * H:(b + 1) * H], cf[:, b * TB:(b + 1) * TB], ident[0:H, 0:H])
                    last = nc.tensor.transpose(psum[0:TB, 2, (NB + b) * H:(NB + b + 1) * H],
                                               cb[:, b * TB + 1:(b + 1) * TB + 1], ident[0:H, 0:H])
                last.then_inc(s_t3, 1)
                for b in range(NB):
                    pe.wait_ge(s_e, b + 1)
                    for h in range(H):
                        nc.tensor.transpose(psum[:, b, h * TB:(h + 1) * TB], v[:, b, h, :], ident[0:TB, 0:TB])
                        last = nc.tensor.transpose(psum[:, 4 + b, h * TB:(h + 1) * TB], sv[:, b, h, :], ident[0:TB, 0:TB])
                    last.then_inc(s_t4, 1)

            @block.scalar
            def _(act):
                for b in range(NB):
                    act.wait_ge(s_t1, b + 1)
                    nc.scalar.activation(sv[:, b].rearrange("p h e -> p (h e)"), psum[0:TB, 4 + b, :], ACT.Copy)\
                        .then_inc(s_sv, 1)
                for b in range(NB):
                    act.wait_ge(s_m, b + 1)
                    nc.scalar.activation(v[:, b], v[:, b], ACT.Exp)
                    nc.scalar.activation(sv[:, b], sv[:, b], ACT.Exp).then_inc(s_e, 1)
                for b in range(NB):
                    act.wait_ge(s_t4, b + 1)
                    nc.scalar.activation(w9[:, b * TB:(b + 1) * TB, 0:H].rearrange("p t h -> p h t"),
                                         psum[:, b, 0:H * TB].rearrange("p (h t) -> p h t", h=H), ACT.Copy)

            @block.vector
            def _(dve):
                link = Chain(dve, s_dv)
                nc.vector.memset(cf[:], -BIG)
                nc.vector.memset(cb[:], -BIG)
                for b in range(NB):
                    dve.wait_ge(s_t1, b + 1)
                    link(nc.vector.tensor_tensor(v[:, b], psum[0:TB, b, :].rearrange("p (h e) -> p h e", h=H),
                                                 bc(pen[:, b, :].unsqueeze(1), [TB, H, P]), ALU.add))

                def scans(start):
                    for b in range(NB):
                        for h in range(H):
                            nc.vector.tensor_tensor_scan(fw[:, b, h, :], rs_f[:, b, :], v[:, b, h, :],
                                                         start(0, b, h), ALU.add, ALU.max)
                            last = nc.vector.tensor_tensor_scan(bw[:, b, h, ::-1], rs_b[:, b, ::-1], v[:, b, h, ::-1],
                                                                start(1, b, h), ALU.add, ALU.max)
                    return last
                scans(lambda i, b, h: -BIG).then_inc(s_f1, 1)
                dve.wait_ge(s_t2, 1)
                nc.vector.tensor_tensor_scan(cf[:, 1:T + 1], any_f[:], psum[0:H, 0, 0:T], -BIG, ALU.add, ALU.max)
                nc.vector.tensor_tensor_scan(cb[:, T - 1::-1], any_b[:, ::-1], psum[0:H, 1, T - 1::-1], -BIG,
                                             ALU.add, ALU.max).then_inc(s_c, 1)
                dve.wait_ge(s_t3, 1)
                link(nc.vector.tensor_copy(cin[:].rearrange("p i b h -> p (i b h)"), psum[0:TB, 2, 0:2 * NB * H]))
                link(scans(lambda i, b, h: cin[:, i, b, h:h + 1]))
                dve.wait_ge(s_sv, NB)
                for b in range(NB):
                    link(nc.vector.tensor_tensor(fw[:, b], fw[:, b], bw[:, b], ALU.max))
                    link(nc.vector.tensor_tensor(fw[:, b], fw[:, b], sv[:, b], ALU.max))
                    nc.vector.tensor_tensor(v[:, b], v[:, b], fw[:, b], ALU.subtract)
                    nc.vector.tensor_tensor(sv[:, b], sv[:, b], fw[:, b], ALU.subtract).then_inc(s_m, 1)
                for b in range(NB):
                    dve.wait_ge(s_t4, b + 1)
                    nc.vector.tensor_tensor(w9[:, b * TB:(b + 1) * TB, H:2 * H].rearrange("p t h -> p h t"),
                                            psum[:, 4 + b, 0:H * TB].rearrange("p (h t) -> p h t", h=H),
                                            bc(isfirst[:, b * TB:(b + 1) * TB].unsqueeze(1), [P, H, TB]), ALU.mult)
                nc.vector.tensor_copy(w9[:, :, 2 * H], isfirst[:])


_INS = ['x', 'src', 'dst', 'L0_gnn_W', 'L0_gnn_att_src', 'L0_gnn_att_dst', 'L0_gnn_bias', 'L1_gnn_rms_w',
        'L1_gnn_W_down', 'L1_gnn_Wl', 'L1_gnn_Wr', 'L1_gnn_att', 'L1_gnn_W_up']


def kernel(**inputs):
    import numpy as np
    import concourse.bacc as bacc
    from concourse import mybir
    from concourse.bass_utils import run_bass_kernel_spmd
    nc = bacc.Bacc("TRN2", target_bir_lowering=False, num_devices=1)
    arrays, args = {}, []
    for name in _INS:
        a = np.ascontiguousarray(inputs[name])
        arrays["in_" + name] = a
        args.append(nc.dram_tensor("in_" + name, a.shape, mybir.dt.from_np(a.dtype), kind="ExternalInput").ap())
    out = nc.dram_tensor("out_0", (N, D), F32, kind="ExternalOutput").ap()
    gnn_kernel(nc, *args, out)
    r = run_bass_kernel_spmd(nc, [arrays], core_ids=[0])
    return r.results[0]["out_0"]
```

```python
import concourse.bass as bass
from concourse import mybir
from contextlib import ExitStack

F32 = mybir.dt.float32
I32 = mybir.dt.int32
BF16 = mybir.dt.bfloat16
ALU = mybir.AluOpType
ACT = mybir.ActivationFunctionType
AX = mybir.AxisListType

P = 128
N, E, D, H, C = 3125, 50000, 1024, 4, 256
HID = 256
HD = HID // H
KD = D // P
KH = HID // P
NT = -(-N // P)
NP = NT * P
N_LAST = N - (NT - 1) * P
NC = -(-E // P)
NCF = E // P
E_LAST = E - NCF * P
NB = 4
U = 4
T = -(-(NC + NT - 1) // (2 * U * NB)) * 2 * U * NB
TB = T // NB
NG = T // U
NO_DST = 8191
BIG = 1e30
SLOPE = 0.2
LN_EPS = 1e-5
RMS_EPS = 1e-6
DEN_EPS = 1e-16
PARTS = 3
DVE_HEADS = 1
W9 = 2 * H + 1
XLW = HID + H
XRW = HID + 2 * H
ACC1 = HID + W9


def wait(eng, sem, value):
    if not isinstance(value, int) or value > 0:
        eng.wait_ge(sem, value)


class Chain:

    def __init__(self, eng, sem, per=0):
        self.eng, self.sem, self.per, self.base, self.k = eng, sem, per, 0, 0

    def tile(self, t):
        assert self.k == (self.per if self.k else 0) or not self.per
        self.base, self.k = t * self.per, 0

    def __call__(self, ins):
        ins.then_inc(self.sem, 1)
        self.k += 1
        self.eng.wait_ge(self.sem, self.base + self.k)


def pipelined(eng, n, stages, ahead=4, ring=2):
    last = n + max(lag for lag, _ in stages)
    ahead += -ahead % ring

    def turn(v):
        for lag, f in stages:
            t = v - lag
            if 0 <= t < n:
                f(t, t % ring, t // ring)

    for v in range(min(ahead, last)):
        turn(v)
    end = n - n % ring
    if end > ahead:
        with eng.Fori(ahead // ring, end // ring) as i:
            for par in range(ring):
                for lag, f in stages:
                    s = (par - lag) % ring
                    f(ring * i + (par - lag), s, i + (par - lag - s) // ring)
    for v in range(max(end, ahead), last):
        turn(v)


def bc(ap, shape):
    return ap.to_broadcast(shape)


class StepTiles:

    def __init__(self, eng, dtab, name, steps=U):
        self.eng, self.dtab, self.steps = eng, dtab, steps
        self.regs = [eng.alloc_register(f"{name}_d{j}") for j in range(steps)]

    def load(self, g):
        self.eng.reg_load(self.regs, self.dtab[0:1, bass.ds(g * self.steps, self.steps)])
        return [self.eng.snap(r, min_val=0, max_val=NT - 1) for r in self.regs]


class PoolGather:

    def __init__(self, pool, rows, bound):
        self.pool, self.bound, self.rows = pool, bound, rows
        pool.reg_mov(bound, rows - 1)

    def wait(self, sem, value):
        if isinstance(value, int) and value <= 0:
            return
        self.pool.wait_ge(sem, value)
        self.pool.reg_alu(self.bound, self.bound, self.rows - 1, ALU.min)

    def rows_of(self, out, table, idx):
        return self.pool.indirect_dma_start(out, None, table, bass.IndirectOffsetOnAxis(ap=idx, axis=0),
                                            bounds_check=self.bound, oob_is_err=False)


def gnn_kernel(nc, x, src, dst, w0, att_s, att_d, bias, rms_w, w_down, wl, wr, att1, w_up, out):
    edge_t = nc.dram_tensor("edge_table", (T, 4 * P), F32, kind="Internal").ap()
    local_t = nc.dram_tensor("local_dst", (T, P), F32, kind="Internal").ap()
    as_t = nc.dram_tensor("a_src_table", (NP, H), F32, kind="Internal").ap()
    xp_t = nc.dram_tensor("xp_table", (NP, D), F32, kind="Internal").ap()
    x1_t = nc.dram_tensor("x1_table", (NP, D), F32, kind="Internal").ap()
    xe_t = nc.dram_tensor("edge_rows", (NG, P, U * XLW), F32, kind="Internal").ap()
    xl_t = nc.dram_tensor("xl_table", (NP, XLW), F32, kind="Internal").ap()

    top = ExitStack()
    sems = [0]

    def sem(name):
        sems[0] += 1
        return top.enter_context(nc.semaphore(name))

    with top:
        def keep(name, shape, dt=F32):
            return top.enter_context(nc.sbuf_tensor(name, shape, dt))

        ident = keep("ident", [P, P])
        iotar = keep("iotar", [P, P])
        pidx = keep("pidx", [P, 1])
        ldst = keep("ldst", [P, T])
        isrc = keep("isrc", [P, T + U])
        isfirst = keep("isfirst", [P, T])
        dtab = keep("dtab", [1, T], I32)
        rs_f = keep("rs_f", [TB, NB, P])
        rs_b = keep("rs_b", [TB, NB, P])
        pen = keep("pen", [TB, NB, P])
        any_f = keep("any_f", [H, T])
        any_b = keep("any_b", [H, T])
        w9 = keep("w9", [P, T, W9])
        nt0 = keep("nt0", [P, NT, PARTS, 2 * H], BF16)
        bound = nc.gpsimd.alloc_register("row_bound")
        psum = [top.enter_context(nc.psum_tensor(f"bank{i}", [P, 512], F32)) for i in range(8)] \
            if False else top.enter_context(nc.psum_tensor("banks", [P, 8, 512], F32))

        with ExitStack() as ph:
            def sb(name, shape, dt=F32):
                return ph.enter_context(nc.sbuf_tensor(name, shape, dt))
            w_sb = sb("w0_sb", [P, KD, D])
            atts = sb("atts_bc", [P, D])
            attd = sb("attd_bc", [P, D])
            NJ = 8
            junk = sb("junk", [P, NJ, C])
            wa = sb("wa", [P, KD, 2 * H])
            mark0 = sb("mark0", [P, 1])
            mark1 = sb("mark1", [P, 1])
            NPAIR = -(-NT // 2)
            xin = sb("xin", [P, 2, 2, D])
            xT = sb("xT", [P, 2, KD, 2 * P])
            aT = sb("aT", [2 * H, NPAIR, 2 * P])
            a_all = sb("a_all", [P, NT, 2 * H])
            a_sum = sb("a_sum", [P, NT, H])
            nodes = sb("nodes", [P, NT, 2 * H])
            dx = sb("dx", [TB, NB, P + 2], I32)
            sx = sb("sx", [TB, NB, P], I32)
            dxf = sb("dxf", [TB, NB, P + 2])
            ct = sb("ct", [TB, NB, 4, P])
            st = sb("st", [TB, NB, 4, P])
            lasti = sb("lasti", [1, NC], I32)
            lastf = sb("lastf", [1, NC])
            lastw = sb("lastw", [1, NC])
            ioti = sb("ioti", [P, NC], I32)
            iotc = sb("iotc", [1, NC])
            step128 = sb("step128", [TB, NB])
            stepi = sb("stepi", [TB, NB], I32)
            ones = sb("ones", [1, P])
            less = sb("less", [TB, NC])
            ci = sb("ci", [TB, NB])
            cii = sb("cii", [TB, NB], I32)
            di = sb("di", [TB, NB])
            dneg = sb("dneg", [TB, NB])
            dcl = sb("dcl", [TB, NB])
            lrow = sb("lrow", [TB, NB, P])
            val = sb("val", [TB, NB, P])
            fv = sb("fv", [TB, NB, P])
            lv = sb("lv", [TB, NB, P])
            af = sb("af", [TB, NB, H])
            ab = sb("ab", [TB, NB, H])

            s_pad = sem("s_pad")
            s_edges = sem("s_edges")
            s_lrow = sem("s_lrow")
            s_att = sem("s_att")
            s_w = [sem(f"s_w{k}") for k in range(2)]
            s_iota = sem("s_iota")
            s_ident = sem("s_ident")
            s_dv = sem("s_setup_chain")
            s_ct = sem("s_ct")
            s_et = sem("s_et")
            s_lastw = sem("s_lastw")
            s_bcast = sem("s_bcast")
            s_ci = sem("s_ci")
            s_st = sem("s_st")
            s_lw = sem("s_lw")
            s_lt = sem("s_ltst")
            s_tp = sem("s_tp")
            s_wa = sem("s_wa")
            s_xi = [sem(f"s_xi{i}") for i in range(2)]
            s_tr = sem("s_tr")
            s_xT = sem("s_xT")
            s_am = sem("s_am")
            s_ac = sem("s_ac")
            s_at = sem("s_at")
            s_all = sem("s_all")
            s_as = sem("s_as")

            with nc.Block() as block:
                @block.gpsimd
                def _(pool):
                    nc.gpsimd.memset(dx[:], NO_DST).then_inc(s_pad, 1)
                    nc.gpsimd.memset(sx[:], 0).then_inc(s_pad, 1)
                    nc.gpsimd.memset(lasti[:], NO_DST).then_inc(s_pad, 1)
                    nc.gpsimd.iota(ioti[:], pattern=[[P, NC]], base=0, channel_multiplier=0).then_inc(s_iota, 1)
                    pool.wait_ge(s_iota, 1)
                    nc.gpsimd.tensor_copy(iotc[:], ioti[0:1, :]).then_inc(s_iota, 1)
                    nc.gpsimd.iota(stepi[:], pattern=[[P * TB, NB]], base=0, channel_multiplier=P).then_inc(s_iota, 1)
                    pool.wait_ge(s_iota, 3)
                    nc.gpsimd.tensor_copy(step128[:], stepi[:]).then_inc(s_iota, 1)
                    nc.gpsimd.iota(ioti[:, 0:P], pattern=[[1, P]], base=0, channel_multiplier=0).then_inc(s_iota, 1)
                    pool.wait_ge(s_iota, 5)
                    nc.gpsimd.tensor_copy(iotar[:], ioti[:, 0:P]).then_inc(s_iota, 1)
                    nc.gpsimd.iota(ioti[:, P:P + 1], pattern=[[0, 1]], base=0, channel_multiplier=1).then_inc(s_iota, 1)
                    pool.wait_ge(s_iota, 7)
                    nc.gpsimd.tensor_copy(pidx[:], ioti[:, P:P + 1]).then_inc(s_iota, 1)
                    nc.gpsimd.memset(ones[:], 1.0).then_inc(s_iota, 1)
                    nc.gpsimd.memset(xin[:], 0.0).then_inc(s_pad, 1)
                    nc.gpsimd.memset(isrc[:, T:T + U], 0.0)
                    nc.gpsimd.memset(ident[:], 0.0).then_inc(s_ident, 1)
                    pool.wait_ge(s_ident, 1)
                    nc.gpsimd.affine_select(out=ident[:], in_=ident[:], compare_op=ALU.not_equal, fill=1.0,
                                            base=0, pattern=[[-1, P]], channel_multiplier=1).then_inc(s_ident, 1)
                    gather = PoolGather(pool, T, bound)
                    pool.wait_ge(s_ci, 1)
                    pool.wait_ge(s_et, 16)
                    for b in range(NB):
                        gather.rows_of(st[:, b, :, :].rearrange("p f k -> p (f k)"), edge_t, cii[:, b:b + 1])\
                              .then_inc(s_st, 16)

                @block.sync
                def _(sp):
                    sp.wait_ge(s_pad, 3)
                    dh = dst.tensor
                    first = sp.dma_start(dx[0:1, 0, 1:P + 2], dst[0:P + 1].rearrange("(a k) -> a k", a=1))
                    first.then_inc(s_edges, 16)
                    n_edge = 1
                    for b in range(NB):
                        c0, c1 = max(1, b * TB), min((b + 1) * TB, NCF)
                        sp.dma_start(dx[c0 - b * TB:c1 - b * TB, b, :],
                                     bass.AP(dh, c0 * P - 1, [[P, c1 - c0], [1, P + 2]])).then_inc(s_edges, 16)
                        c0 = b * TB
                        sp.dma_start(sx[0:c1 - c0, b, :],
                                     src[c0 * P:c1 * P].rearrange("(p k) -> p k", k=P)).then_inc(s_edges, 16)
                        n_edge += 2
                    pl, bl = NCF % TB, NCF // TB
                    sp.dma_start(dx[pl:pl + 1, bl, 0:E_LAST + 1],
                                 dst[NCF * P - 1:E].rearrange("(a k) -> a k", a=1)).then_inc(s_edges, 16)
                    sp.dma_start(sx[pl:pl + 1, bl, 0:E_LAST],
                                 src[NCF * P:E].rearrange("(a k) -> a k", a=1)).then_inc(s_edges, 16)
                    assert n_edge + 2 == N_EDGE_DMAS
                    with nc.allow_non_contiguous_dma(reason="one word of each chunk"):
                        sp.dma_start(lasti[0:1, 0:NCF], dst[0:NCF * P].rearrange("(c k) -> k c", k=P)[P - 1:P, :])\
                          .then_inc(s_lrow, 16)
                    for k in range(KD):
                        sp.dma_start(w_sb[:, k, :], w0[k * P:(k + 1) * P, :]).then_inc(s_w[k // (KD // 2)], 16)
                    sp.wait_ge(s_ct, 1)
                    sp.dma_start(edge_t.rearrange("(b p) n -> p b n", b=NB),
                                 ct[:].rearrange("p b f k -> p b (f k)")).then_inc(s_et, 16)
                    sp.wait_ge(s_lw, 1)
                    sp.dma_start(local_t.rearrange("(b p) n -> p b n", b=NB), lrow[:]).then_inc(s_lt, 16)
                    sp.wait_ge(s_all, 1)
                    with nc.allow_non_contiguous_dma(reason="four words a node"):
                        sp.dma_start(as_t.rearrange("(t p) h -> p t h", p=P), a_all[:, :, 0:H]).then_inc(s_as, 16)
                    sp.wait_ge(s_as, 16)
                    sp.wait_ge(s_lt, 16)

                @block.scalar
                def _(act):
                    act.dma_start(atts[:], att_s.rearrange("h c -> (h c)").partition_broadcast(P)).then_inc(s_att, 16)
                    act.dma_start(attd[:], att_d.rearrange("h c -> (h c)").partition_broadcast(P)).then_inc(s_att, 16)
                    act.wait_ge(s_pad, 4)

                    def load_x(t, s, m):
                        wait(act, s_tr, 2 * t - 2)
                        if isinstance(t, int) and t == NPAIR - 1:
                            act.dma_start(xin[0:N_LAST, s, 0, :], x[t * 2 * P:N, :]).then_inc(s_xi[s], 16)
                        else:
                            act.dma_start(xin[:, s], x[bass.ds(t * 2 * P, 2 * P), :].rearrange("(a p) d -> p a d", a=2))\
                               .then_inc(s_xi[s], 16)

                    def evict(t, s, m):
                        for a in range(2):
                            act.wait_ge(s_tr, 2 * t + a + 1)
                            if a == 0:
                                wait(act, s_am, t - 1)
                            nc.scalar.activation(xT[:, s, :, a * P:(a + 1) * P],
                                                 psum[:, 2 * a:2 * a + 2].rearrange("p b (k n) -> p (b k) n", n=P),
                                                 ACT.Copy).then_inc(s_xT, 1)

                    def take_a(t, s, m):
                        act.wait_ge(s_am, t + 1)
                        nc.scalar.activation(aT[:, bass.ds(t, 1), :].rearrange("p a n -> p (a n)"),
                                             psum[0:2 * H, 4 + 2 * s, 0:2 * P], ACT.Copy).then_inc(s_ac, 1)

                    pipelined(act, NPAIR, [(0, load_x), (1, evict), (3, take_a)])
                    act.wait_ge(s_at, 1)
                    nc.scalar.activation(a_all[:], psum[:, 4, 0:NT * 2 * H].rearrange("p (t n) -> p t n", n=2 * H),
                                         ACT.Copy).then_inc(s_all, 1)

                @block.tensor
                def _(pe):
                    pe.wait_ge(s_lastw, 1)
                    nc.tensor.matmul(psum[0:TB, 5, 0:NC], ones[0:1, 0:TB], lastw[:], start=True, stop=True)\
                        .then_inc(s_bcast, 1)
                    pe.wait_ge(s_ident, 2)

                    def transposes(t, s, m):
                        pe.wait_ge(s_xi[s], 16 * (m + 1))
                        for a in range(2):
                            wait(pe, s_xT, 2 * t + a - 1)
                            for k in range(KD):
                                last = nc.tensor.transpose(
                                    psum[:, 2 * a + k // 4, (k % 4) * P:(k % 4 + 1) * P],
                                    xin[:, s, a, k * P:(k + 1) * P], ident[:])
                            last.then_inc(s_tr, 1)

                    def products(t, s, m):
                        if isinstance(t, int) and t == 0:
                            pe.wait_ge(s_wa, 1)
                        pe.wait_ge(s_xT, 2 * t + 2)
                        wait(pe, s_ac, t - 1)
                        for k in range(KD):
                            last = nc.tensor.matmul(psum[0:2 * H, 4 + 2 * s, 0:2 * P], wa[:, k, :], xT[:, s, k, :],
                                                    start=(k == 0), stop=(k == KD - 1))
                        last.then_inc(s_am, 1)

                    pipelined(pe, NPAIR, [(1, transposes), (2, products)])
                    pe.wait_ge(s_ac, NPAIR)
                    for t in range(NT):
                        last = nc.tensor.transpose(psum[:, 4, t * 2 * H:(t + 1) * 2 * H],
                                                   aT[:, t // 2, (t % 2) * P:(t % 2 + 1) * P], ident[0:2 * H, 0:2 * H])
                    last.then_inc(s_at, 1)
                    pe.wait_ge(s_lw, 1)
                    for i, rows in enumerate((lrow, st, fv)):
                        for b in range(NB):
                            a = rows[:, b, 0, :] if rows is st else rows[:, b, :]
                            nc.tensor.transpose(psum[:, i, b * TB:(b + 1) * TB], a, ident[0:TB, 0:TB])
                    for i, v in enumerate((af, ab)):
                        for b in range(NB):
                            nc.tensor.transpose(psum[0:H, 6 + i, b * TB:(b + 1) * TB], v[:, b, :], ident[0:TB, 0:TB])
                    for b in range(NB):
                        last = nc.tensor.transpose(psum[0:1, 3, b * TB:(b + 1) * TB], dcl[:, b:b + 1], ident[0:TB, 0:TB])
                    last.then_inc(s_tp, 1)

                @block.vector
                def _(dve):
                    link = Chain(dve, s_dv)
                    dve.wait_ge(s_iota, 9)
                    dve.wait_ge(s_lrow, 16)
                    link(nc.vector.tensor_copy(lastf[:], lasti[:]))
                    nc.vector.tensor_tensor(lastw[:], lastf[:], iotc[:], ALU.add).then_inc(s_lastw, 1)
                    dve.wait_ge(s_edges, 16 * N_EDGE_DMAS)
                    link(nc.vector.tensor_copy(dxf[:], dx[:]))
                    nc.vector.tensor_copy(ct[:, :, 0, :], sx[:])
                    nc.vector.tensor_copy(ct[:, :, 1, :], dxf[:, :, 1:P + 1])
                    nc.vector.tensor_tensor(ct[:, :, 2, :], dxf[:, :, 1:P + 1], dxf[:, :, 0:P], ALU.not_equal)
                    nc.vector.tensor_tensor(ct[:, :, 3, :], dxf[:, :, 1:P + 1], dxf[:, :, 2:P + 2], ALU.not_equal)\
                        .then_inc(s_ct, 1)
                    dve.wait_ge(s_bcast, 1)
                    for b in range(NB):
                        link(nc.vector.tensor_scalar(less[:], psum[0:TB, 5, 0:NC], step128[:, b:b + 1], None, ALU.is_lt))
                        link(nc.vector.reduce_sum(ci[:, b:b + 1], less[:], AX.X))
                    link(nc.vector.tensor_scalar_min(ci[:], ci[:], float(NC - 1)))
                    nc.vector.tensor_copy(cii[:], ci[:]).then_inc(s_ci, 1)
                    link(nc.vector.scalar_tensor_tensor(out=dneg[:], in0=ci[:], scalar=float(P), in1=step128[:],
                                                        op0=ALU.mult, op1=ALU.subtract))
                    link(nc.vector.tensor_scalar(di[:], dneg[:], -1.0 / P, None, ALU.mult))
                    link(nc.vector.tensor_scalar_min(dcl[:], di[:], float(NT - 1)))
                    dve.wait_ge(s_att, 32)
                    for k in range(KD):
                        dve.wait_ge(s_w[k // (KD // 2)], 16 * KD // 2)
                        for i, att in enumerate((atts, attd)):
                            for h in range(H):
                                n = (k * 2 + i) * H + h
                                last = nc.vector.tensor_tensor_reduce(
                                    out=junk[:, n % NJ, :], in0=w_sb[:, k, h * C:(h + 1) * C],
                                    in1=att[:, h * C:(h + 1) * C], scale=1.0, scalar=0.0, op0=ALU.mult, op1=ALU.add,
                                    accum_out=wa[:, k, i * H + h:i * H + h + 1])
                                if n % NJ == NJ - 1:
                                    link(last)
                    nc.vector.tensor_copy(mark0[:], pidx[:]).then_inc(s_wa, 1)
                    dve.wait_ge(s_st, 16 * NB)
                    for b in range(NB):
                        nc.vector.tensor_scalar(lrow[:, b, :], st[:, b, 1, :], dneg[:, b:b + 1], None, ALU.add)
                    link(nc.vector.tensor_copy(mark1[:], pidx[:]))
                    link(nc.vector.tensor_scalar(val[:], lrow[:], 0.0, None, ALU.is_ge))
                    link(nc.vector.scalar_tensor_tensor(out=val[:], in0=lrow[:], scalar=float(P), in1=val[:],
                                                        op0=ALU.is_lt, op1=ALU.mult))
                    nc.vector.tensor_scalar(pen[:], val[:], BIG, -BIG, ALU.mult, ALU.add)
                    nc.vector.tensor_tensor(fv[:], st[:, :, 2, :], val[:], ALU.mult)
                    link(nc.vector.tensor_tensor(lv[:], st[:, :, 3, :], val[:], ALU.mult))
                    nc.vector.tensor_scalar(rs_f[:], fv[:], -BIG, None, ALU.mult)
                    link(nc.vector.tensor_scalar(rs_b[:], lv[:], -BIG, None, ALU.mult))
                    for h in range(H):
                        nc.vector.tensor_reduce(out=af[:, :, h], in_=rs_f[:], op=ALU.min, axis=AX.X)
                        last = nc.vector.tensor_reduce(out=ab[:, :, h], in_=rs_b[:], op=ALU.min, axis=AX.X)
                    last.then_inc(s_lw, 1)
                    dve.wait_ge(s_all, 1)
                    nc.vector.tensor_copy(nodes[:, :, 0:H], a_all[:, :, H:2 * H])
                    link(nc.vector.tensor_tensor(a_sum[:], a_all[:, :, 0:H], a_all[:, :, H:2 * H], ALU.add))
                    link(nc.vector.scalar_tensor_tensor(out=nodes[:, :, H:2 * H], in0=a_sum[:], scalar=SLOPE,
                                                        in1=a_sum[:], op0=ALU.mult, op1=ALU.max))
                    for i in range(PARTS):
                        link(nc.vector.tensor_copy(nt0[:, :, i, :], nodes[:]))
                        if i < PARTS - 1:
                            link(nc.vector.tensor_tensor(nodes[:], nodes[:], nt0[:, :, i, :], ALU.subtract))
                    dve.wait_ge(s_tp, 1)
                    nc.vector.tensor_copy(ldst[:], psum[:, 0, 0:T])
                    nc.vector.tensor_copy(isrc[:, 0:T], psum[:, 1, 0:T])
                    nc.vector.tensor_copy(isfirst[:], psum[:, 2, 0:T])
                    nc.vector.tensor_copy(any_f[:], psum[0:H, 6, 0:T])
                    nc.vector.tensor_copy(any_b[:], psum[0:H, 7, 0:T])
                    nc.vector.tensor_copy(dtab[:], psum[0:1, 3, 0:T])

        UNITS = T // (4 * U)
        with ExitStack() as ph:
            def sb(name, shape, dt=F32):
                return ph.enter_context(nc.sbuf_tensor(name, shape, dt))
            w_sb = sb("w0_sb2", [P, KD, D])
            xin = sb("xin2", [P, D])
            xT = sb("xT2", [P, KD, P])
            xp_st = sb("xp_st", [P, D])
            lt = sb("lt_bc", [P, 2, U, P])
            onehot_t = sb("onehot_t", [P, 2, U, P], BF16)
            at_dst = sb("at_dst", [P, 2, U, 2 * H])
            idx = sb("idx", [P, 4, U], I32)
            ga = sb("ga", [P, 4, U, H])
            esum = sb("esum", [P, 2, U, H])

            s_w = sem("p1_w")
            s_clr = sem("p1_clr")
            s_xi = sem("p1_x")
            s_tr = sem("p1_tr")
            s_xT = sem("p1_xT")
            s_xp = sem("p1_xp")
            s_xe = sem("p1_xe")
            s_xs = sem("p1_xs")
            s_lt = [sem(f"p1_lt{i}") for i in range(2)]
            s_ot = sem("p1_ot")
            s_pg = sem("p1_pg")
            s_ix = sem("p1_ix")
            s_ga = [sem(f"p1_ga{i}") for i in range(4)]
            s_es = sem("p1_es")
            s_lg = sem("p1_lg")

            def units(eng, body):
                body(0, True)
                with eng.Fori(1, NT) as u:
                    body(u, True)
                body(NT, False)

            with nc.Block() as block:
                @block.gpsimd
                def _(pool):
                    nc.gpsimd.memset(xin[:], 0.0).then_inc(s_clr, 1)
                    gather = PoolGather(pool, N, bound)

                    def indices(g_all, s):
                        nc.gpsimd.tensor_copy(idx[:, s, :], isrc[:, bass.ds(g_all * U, U)]).then_inc(s_ix, 1)

                    def unit(u, _):
                        for g in range(4):
                            g_all = 4 * u + g
                            gather.wait(s_ix, g_all + 1)
                            gather.wait(s_lg, g_all - 3)
                            for j in range(U):
                                gather.rows_of(ga[:, g, j, :], as_t, idx[:, g, j:j + 1]).then_inc(s_ga[g], 16)
                                if j == 1:
                                    g2 = (g + 1) % 4
                                    gather.wait(s_ga[g2], 64 * (u if g2 else u + 1))
                                    indices(g_all + 1, g2)
                    indices(0, 0)
                    units(pool, unit)

                @block.sync
                def _(sp):
                    for k in range(KD):
                        sp.dma_start(w_sb[:, k, :], w0[k * P:(k + 1) * P, :]).then_inc(s_w, 16)
                    sp.wait_ge(s_clr, 1)

                    def load_x(u, rows=P):
                        wait(sp, s_tr, u)
                        sp.dma_start(xin[0:rows, :], x[bass.ds(u * P, rows), :]).then_inc(s_xi, 16)

                    def unit(u, has_x, load=None):
                        if load == "last":
                            load_x(NT - 1, N_LAST)
                        elif load != "none":
                            load_x(u)
                        for g in range(4):
                            g_all = 4 * u + g
                            wait(sp, s_ot, g_all - 1)
                            sp.dma_start(lt[:, g % 2].rearrange("p j e -> p (j e)"),
                                         local_t[bass.ds(g_all * U, U), :].rearrange("j e -> (j e)").partition_broadcast(P))\
                              .then_inc(s_lt[g % 2], 16)
                            if g == 1 and not (isinstance(u, int) and u == 0):
                                sp.wait_ge(s_xe, u)
                                sp.dma_start(xp_t[bass.ds((u - 1) * P, P), :], xp_st[:]).then_inc(s_xs, 16)

                    unit(0, True)
                    with sp.Fori(1, NT - 1) as u:
                        unit(u, True)
                    unit(NT - 1, True, "last")
                    unit(NT, False, "none")
                    sp.wait_ge(s_xs, 16 * NT)

                @block.scalar
                def _(act):
                    def unit(u, has_x):
                        if has_x:
                            act.wait_ge(s_tr, u + 1)
                            nc.scalar.activation(xT[:].rearrange("p k n -> p (k n)"),
                                                 psum[:, 0:2].rearrange("p a b -> p (a b)"), ACT.Copy).then_inc(s_xT, 1)
                            act.wait_ge(s_xp, u + 1)
                            wait(act, s_xs, 16 * u)
                            nc.scalar.activation(xp_st[:], psum[:, 2:4].rearrange("p a b -> p (a b)"),
                                                 ACT.Copy).then_inc(s_xe, 1)
                    units(act, unit)

                @block.tensor
                def _(pe):
                    tiles = StepTiles(pe, dtab, "p1")
                    pe.wait_ge(s_w, 16 * KD)

                    def unit(u, has_x):
                        if has_x:
                            pe.wait_ge(s_xi, 16 * u + 16)
                            for k in range(KD):
                                last = nc.tensor.transpose(psum[:, k // 4, (k % 4) * P:(k % 4 + 1) * P],
                                                           xin[:, k * P:(k + 1) * P], ident[:])
                            last.then_inc(s_tr, 1)
                        for g in range(4):
                            g_all, s = 4 * u + g, g % 2
                            ds = tiles.load(g_all)
                            pe.wait_ge(s_ot, g_all + 1)
                            wait(pe, s_lg, g_all - 1)
                            for j in range(U):
                                last = nc.tensor.matmul(
                                    psum[:, 4 + s, j * PARTS * 2 * H:(j + 1) * PARTS * 2 * H], onehot_t[:, s, j, :],
                                    nt0[:, bass.ds(ds[j], 1)].rearrange("p a k n -> p (a k n)"), start=True, stop=True)
                            last.then_inc(s_pg, 1)
                            if has_x:
                                if g == 0:
                                    pe.wait_ge(s_xT, u + 1)
                                for k in range(2 * g, 2 * g + 2):
                                    for i in range(2):
                                        if g == 0 and k == 0 and i == 0:
                                            wait(pe, s_xe, u)
                                        last = nc.tensor.matmul(psum[:, 2 + i], xT[:, k, :],
                                                                w_sb[:, k, i * 512:(i + 1) * 512],
                                                                start=(k == 0), stop=(k == KD - 1))
                                if g == 3:
                                    last.then_inc(s_xp, 1)
                    units(pe, unit)

                @block.vector
                def _(dve):
                    def onehots(g, s, m):
                        dve.wait_ge(s_lt[s], 16 * m + 16)
                        wait(dve, s_pg, g - 1)
                        nc.vector.tensor_scalar(onehot_t[:, s].rearrange("p j e -> p (j e)"),
                                                lt[:, s].rearrange("p j e -> p (j e)"), pidx[:], None,
                                                ALU.is_equal).then_inc(s_ot, 1)

                    def logits(g, s, m):
                        u, slot = m
                        dve.wait_ge(s_pg, g + 1)
                        dve.wait_ge(s_ga[slot], 64 * u + 64)
                        pv = psum[:, 4 + s, 0:U * PARTS * 2 * H].rearrange("p (j k n) -> p j n k", k=PARTS, n=2 * H)
                        nc.vector.tensor_reduce(out=at_dst[:, s], in_=pv, op=ALU.add, axis=AX.X).then_inc(s_es, 1)
                        dve.wait_ge(s_es, 2 * g + 1)
                        nc.vector.tensor_tensor(esum[:, s], at_dst[:, s, :, 0:H], ga[:, slot], ALU.add).then_inc(s_es, 1)
                        nc.vector.tensor_copy(w9[:, bass.ds(g * U, U), H:2 * H], at_dst[:, s, :, H:2 * H])
                        dve.wait_ge(s_es, 2 * g + 2)
                        nc.vector.scalar_tensor_tensor(out=w9[:, bass.ds(g * U, U), 0:H], in0=esum[:, s], scalar=SLOPE,
                                                       in1=esum[:, s], op0=ALU.mult, op1=ALU.max).then_inc(s_lg, 1)

                    def unit(u, _):
                        for g in range(4):
                            onehots(4 * u + g, g % 2, 2 * u + g // 2)
                            if g or not isinstance(u, int) or u:
                                gp = g - 1
                                logits(4 * u + gp, gp % 2, (u, gp) if g else (u - 1, 3))
                    units(dve, unit)
                    logits(NG - 1, 1, (NG // 4 - 1, 3))

        acc = keep("acc", [P, NT, D])
        zacc = keep("zacc", [P, NT, W9])
        weigh_edges(nc, sem, "l0", psum, w9, ident, isfirst, rs_f, rs_b, pen, any_f, any_b, [acc[:], zacc[:]])

        with ExitStack() as ph:
            def sb(name, shape, dt=F32):
                return ph.enter_context(nc.sbuf_tensor(name, shape, dt))
            rows = sb("rows0", [P, 2, U, D])
            onehot = sb("onehot0", [P, 2, U, P])
            wone = sb("wone", [P, 2, U, H, P])
            idx = sb("idx2", [P, 2, U], I32)
            s_ix = sem("p2_ix")
            s_r = [sem(f"p2_r{i}") for i in range(2)]
            s_o = sem("p2_o")
            s_pd = sem("p2_pd")
            s_pa = sem("p2_pa")
            s_mm = sem("p2_mm")
            s_acc = sem("p2_acc")
            with nc.Block() as block:
                @block.gpsimd
                def _(pool):
                    gather = PoolGather(pool, N, bound)

                    def group(g, s, m):
                        gather.wait(s_r[s], 64 * m)
                        nc.gpsimd.tensor_copy(idx[:, s, :], isrc[:, bass.ds(g * U, U)]).then_inc(s_ix, 1)
                        gather.wait(s_ix, g + 1)
                        for j in range(U):
                            gather.wait(s_mm, (g - 2) * U + j + 1)
                            gather.rows_of(rows[:, s, j, :], xp_t, idx[:, s, j:j + 1]).then_inc(s_r[s], 16)
                    pipelined(pool, NG, [(0, group)])

                @block.scalar
                def _(act):
                    def weights(g, s, m):
                        act.wait_ge(s_o, g + 1)
                        for j in range(U):
                            wait(act, s_mm, (g - 2) * U + j + 1)
                            for h in range(DVE_HEADS, H):
                                last = nc.scalar.activation(wone[:, s, j, h, :], onehot[:, s, j, :], ACT.Copy,
                                                            scale=w9[:, bass.ds(g * U + j, 1), h:h + 1].rearrange("p a b -> p (a b)"))
                            last.then_inc(s_pa, 1)
                    pipelined(act, NG, [(0, weights)])

                @block.tensor
                def _(pe):
                    def group(g, s, m):
                        for j in range(U):
                            i = g * U + j
                            if j == 0:
                                pe.wait_ge(s_r[s], 64 * m + 64)
                            pe.wait_ge(s_pd, i + 1)
                            pe.wait_ge(s_pa, i + 1)
                            wait(pe, s_acc, i - 1)
                            for h in range(H):
                                nc.tensor.matmul(psum[:, 2 * (j % 2) + h // 2, (h % 2) * C:(h % 2 + 1) * C],
                                                 wone[:, s, j, h, :], rows[:, s, j, h * C:(h + 1) * C],
                                                 start=True, stop=True)
                            nc.tensor.matmul(psum[:, 4 + j % 2, 0:W9], onehot[:, s, j, :],
                                             w9[:, bass.ds(i, 1), :], start=True, stop=True).then_inc(s_mm, 1)
                    pipelined(pe, NG, [(0, group)])

                @block.vector
                def _(dve):
                    tiles = StepTiles(dve, dtab, "p2")

                    def group(g, s, m, build=True, add=True):
                        if build:
                            wait(dve, s_mm, (g - 1) * U)
                            wait(dve, s_pa, (g - 1) * U)
                            nc.vector.tensor_tensor(
                                onehot[:, s], bc(iotar[:].unsqueeze(1), [P, U, P]),
                                bc(ldst[:, bass.ds(g * U, U)].unsqueeze(2), [P, U, P]), ALU.is_equal).then_inc(s_o, 1)
                        if add:
                            ds = tiles.load(g - 1)
                        for j in range(U):
                            if build:
                                for h in range(DVE_HEADS):
                                    last = nc.vector.tensor_scalar(
                                        wone[:, s, j, h, :], iotar[:], ldst[:, bass.ds(g * U + j, 1)],
                                        w9[:, bass.ds(g * U + j, 1), h:h + 1].rearrange("p a b -> p (a b)"),
                                        ALU.is_equal, ALU.mult)
                                last.then_inc(s_pd, 1)
                            if add:
                                i = (g - 1) * U + j
                                dve.wait_ge(s_mm, i + 1)
                                wait(dve, s_acc, i)
                                av = acc[:, bass.ds(ds[j], 1), :].rearrange("p a n -> p (a n)")
                                zv = zacc[:, bass.ds(ds[j], 1), :].rearrange("p a n -> p (a n)")
                                nc.vector.tensor_tensor(zv, psum[:, 4 + j % 2, 0:W9], zv, ALU.add)
                                nc.vector.tensor_tensor(av, psum[:, 2 * (j % 2):2 * (j % 2) + 2].rearrange("p a b -> p (a b)"),
                                                        av, ALU.add).then_inc(s_acc, 1)
                    pipelined(dve, NG, [(0, lambda g, s, m: group(g, s, m, True, not (isinstance(g, int) and g == 0)))])
                    group(NG, 0, NG // 2, False, True)

        xr = acc[:, :, 0:XRW]
        acc1 = acc[:, :, 2 * C:2 * C + ACC1]
        acc1_odd = acc[:, :, 0:ACC1]
        with ExitStack() as ph:
            def sb(name, shape, dt=F32):
                return ph.enter_context(nc.sbuf_tensor(name, shape, dt))
            wd = sb("wd", [P, KD, HID])
            rmsw = sb("rmsw", [P, KD])
            wlr = sb("wlr", [P, KH, 2 * HID + 2 * H])
            bias_bc = sb("bias_bc", [P, D])
            att_bc = sb("att_bc", [P, HID])
            noself = sb("noself", [P, NT])
            wself = sb("wself", [P, NT, H])
            rz = sb("rz", [P, NT, H])
            sw = sb("sw", [P, NT, H])
            eps = sb("eps", [P, 2])
            xpt = sb("xpt", [P, 2, D])
            xin = sb("xin5", [P, 2, D])
            g0 = sb("g0", [P, 2, D])
            y = sb("y", [P, 2, D])
            sq = sb("sq", [P, D])
            xT = sb("xT5", [P, 2, KD, P])
            st = sb("st5", [P, 2, 12])
            mv = sb("mv", [P, 2, 2])
            mark = sb("mark5", [P, 1])
            sd = sb("sd", [P, 2])
            rs = sb("rs", [P, 2, 2])
            ss = sb("ss", [P, 2])
            sr = sb("sr", [P, 2])
            rr = sb("rr", [P, 2])
            hd = sb("hd", [P, 2, HID])
            hT = sb("hT", [P, 2, KH, P])
            xls = sb("xls", [P, 2, XRW])
            tmp2 = sb("tmp52", [P, HID])
            relu_part = sb("relu_part", [P, H])
            both = sb("both", [P, H])
            att_lin = sb("att_lin", [P, HID])
            att_relu = sb("att_relu", [P, HID])
            names = "ldw clr z wd y0 pb B mv sd D rs x1 E sr rr tr xT hp hd ht hT lr xlr sf att".split()
            S = {n: sem("n_" + n) for n in names}
            s_ld = [sem(f"n_ld{i}") for i in range(2)]
            s_x1s = [sem(f"n_x1s{i}") for i in range(2)]
            s_xls = [sem(f"n_xls{i}") for i in range(2)]
            N_LDW = 4 + KH * 2
            AHEAD = 8
            with nc.Block() as block:
                @block.gpsimd
                def _(pool):
                    nc.gpsimd.memset(xin[:], 0.0).then_inc(S["clr"], 1)
                    nc.gpsimd.memset(eps[:, 0:1], LN_EPS).then_inc(S["clr"], 1)
                    nc.gpsimd.memset(eps[:, 1:2], RMS_EPS).then_inc(S["clr"], 1)
                    pool.wait_ge(S["ldw"], 16 * N_LDW)

                    def add_bias(t, s, m):
                        pool.wait_ge(S["y0"], t + 1)
                        nc.gpsimd.tensor_tensor(g0[:, s], g0[:, s], bias_bc[:], ALU.add).then_inc(S["pb"], 1)
                    pipelined(pool, NT, [(1, add_bias)], AHEAD)

                @block.sync
                def _(sp):
                    with nc.allow_non_contiguous_dma(reason="rms weights by rows of W_down, once"):
                        sp.dma_start(rmsw[:], rms_w.rearrange("(k p) -> p k", p=P)).then_inc(S["ldw"], 16)
                    sp.dma_start(wd[:], w_down.rearrange("(k p) n -> p k n", p=P)).then_inc(S["ldw"], 16)
                    sp.dma_start(bias_bc[:], bias.partition_broadcast(P)).then_inc(S["ldw"], 16)
                    sp.dma_start(att_bc[:], att1.rearrange("h c -> (h c)").partition_broadcast(P)).then_inc(S["ldw"], 16)
                    for k in range(KH):
                        sp.dma_start(wlr[:, k, 0:HID], wl[k * P:(k + 1) * P, :]).then_inc(S["ldw"], 16)
                        sp.dma_start(wlr[:, k, XRW:XRW + HID], wr[k * P:(k + 1) * P, :]).then_inc(S["ldw"], 16)
                    sp.wait_ge(S["clr"], 1)

                    def load(t, s, m):
                        wait(sp, S["mv"], t - 1)
                        rows = N_LAST if isinstance(t, int) and t == NT - 1 else P
                        sp.dma_start(xpt[:, s, :], xp_t[bass.ds(t * P, P), :]).then_inc(s_ld[s], 16)
                        sp.dma_start(xin[0:rows, s, :], x[bass.ds(t * P, rows), :]).then_inc(s_ld[s], 16)

                    def store_x1(t, s, m):
                        sp.wait_ge(S["x1"], t + 1)
                        sp.dma_start(x1_t[bass.ds(t * P, P), :], y[:, s, :]).then_inc(s_x1s[s], 16)

                    def store_xl(t, s, m):
                        sp.wait_ge(S["sf"], t + 1)
                        sp.dma_start(xl_t[bass.ds(t * P, P), :], xls[:, s, 0:XLW]).then_inc(s_xls[s], 16)
                    pipelined(sp, NT, [(1, load), (3, store_x1), (6, store_xl)], AHEAD)
                    for s in range(2):
                        sp.wait_ge(s_x1s[s], 16 * ((NT + 1 - s) // 2))
                        sp.wait_ge(s_xls[s], 16 * ((NT + 1 - s) // 2))

                @block.scalar
                def _(act):
                    act.wait_ge(S["z"], 1)
                    act.wait_ge(S["clr"], 3)

                    def divide(t, s, m):
                        wait(act, S["mv"], t - 1)
                        for h in range(H):
                            last = nc.scalar.activation(
                                g0[:, s, h * C:(h + 1) * C],
                                acc[:, bass.ds(t, 1), h * C:(h + 1) * C].rearrange("p a n -> p (a n)"), ACT.Copy,
                                scale=rz[:, bass.ds(t, 1), h:h + 1].rearrange("p a n -> p (a n)"))
                        last.then_inc(S["y0"], 1)

                    def deviation(t, s, m):
                        act.wait_ge(S["mv"], t + 1)
                        nc.scalar.activation(sd[:, s:s + 1], mv[:, s, 1:2], ACT.Sqrt, bias=eps[:, 0:1]).then_inc(S["sd"], 1)

                    def normalise(t, s, m):
                        act.wait_ge(S["rs"], t + 1)
                        nc.scalar.activation(y[:, s, :], y[:, s, :], ACT.Identity, bias=rs[:, s, 1:2],
                                             scale=rs[:, s, 0:1]).then_inc(S["x1"], 1)
                        act.wait_ge(S["x1"], t + 1)
                        wait(act, S["E"], t)
                        nc.scalar.activation(sq[:], y[:, s, :], ACT.Square, accum_out=ss[:, s:s + 1]).then_inc(S["E"], 1)
                        act.wait_ge(S["E"], t + 1)
                        nc.scalar.activation(sr[:, s:s + 1], ss[:, s:s + 1], ACT.Sqrt, bias=eps[:, 1:2],
                                             scale=1.0 / D).then_inc(S["sr"], 1)

                    def take_xT(t, s, m):
                        act.wait_ge(S["tr"], t + 1)
                        wait(act, S["hp"], t - 1)
                        nc.scalar.activation(xT[:, s].rearrange("p k n -> p (k n)"),
                                             psum[:, 2 * s:2 * s + 2].rearrange("p a b -> p (a b)"),
                                             ACT.Copy).then_inc(S["xT"], 1)

                    def take_hT(t, s, m):
                        act.wait_ge(S["ht"], t + 1)
                        wait(act, S["lr"], t - 1)
                        nc.scalar.activation(hT[:, s].rearrange("p k n -> p (k n)"), psum[:, 5, 0:HID],
                                             ACT.Copy).then_inc(S["hT"], 1)

                    def take_xlr(t, s, m):
                        act.wait_ge(S["lr"], t + 1)
                        wait(act, S["sf"], t - 1)
                        wait(act, s_xls[s], 16 * m)
                        nc.scalar.activation(xls[:, s, :], psum[:, 6, 0:XRW], ACT.Copy).then_inc(S["xlr"], 1)
                        nc.scalar.activation(xr[:, bass.ds(t, 1), 0:HID].rearrange("p a n -> p (a n)"),
                                             psum[:, 7, 0:HID], ACT.Copy).then_inc(S["xlr"], 1)
                    pipelined(act, NT, [(3, deviation), (5, take_hT), (6, take_xlr), (3, normalise), (0, divide),
                                        (3, take_xT)], AHEAD)

                @block.tensor
                def _(pe):
                    pe.wait_ge(S["wd"], 1)

                    def transposes(t, s, m):
                        pe.wait_ge(S["x1"], t + 1)
                        wait(pe, S["xT"], t - 1)
                        for k in range(KD):
                            last = nc.tensor.transpose(psum[:, 2 * s + k // 4, (k % 4) * P:(k % 4 + 1) * P],
                                                       y[:, s, k * P:(k + 1) * P], ident[:])
                        last.then_inc(S["tr"], 1)

                    def down(t, s, m):
                        pe.wait_ge(S["xT"], t + 1)
                        wait(pe, S["hd"], t)
                        for k in range(KD):
                            last = nc.tensor.matmul(psum[:, 4, 0:HID], xT[:, s, k, :], wd[:, k, :],
                                                    start=(k == 0), stop=(k == KD - 1))
                        last.then_inc(S["hp"], 1)

                    def transposes_h(t, s, m):
                        pe.wait_ge(S["hd"], t + 1)
                        wait(pe, S["hT"], t)
                        for k in range(KH):
                            last = nc.tensor.transpose(psum[:, 5, k * P:(k + 1) * P], hd[:, s, k * P:(k + 1) * P], ident[:])
                        last.then_inc(S["ht"], 1)

                    def left_right(t, s, m):
                        pe.wait_ge(S["hT"], t + 1)
                        if isinstance(t, int) and t == 0:
                            pe.wait_ge(S["wd"], 2)
                        wait(pe, S["xlr"], 2 * t)
                        for k in range(KH):
                            nc.tensor.matmul(psum[:, 6, 0:XRW], hT[:, s, k, :], wlr[:, k, 0:XRW],
                                             start=(k == 0), stop=(k == KH - 1))
                            last = nc.tensor.matmul(psum[:, 7, 0:HID], hT[:, s, k, :], wlr[:, k, XRW:XRW + HID],
                                                    start=(k == 0), stop=(k == KH - 1))
                        last.then_inc(S["lr"], 1)
                    pipelined(pe, NT, [(5, transposes_h), (4, down), (5, left_right), (3, transposes)], AHEAD)

                @block.vector
                def _(dve):
                    divisor(nc, dve, sem("n_zc"), zacc, noself, wself, rz, sw, 0.0).then_inc(S["z"], 1)
                    dve.wait_ge(S["ldw"], 16 * N_LDW)
                    for k in range(KD):
                        last = nc.vector.tensor_scalar(wd[:, k, :], wd[:, k, :], rmsw[:, k:k + 1], None, ALU.mult)
                    last.then_inc(S["wd"], 1)
                    nc.vector.tensor_scalar(att_lin[:], att_bc[:], SLOPE, None, ALU.mult)
                    nc.vector.tensor_scalar(att_relu[:], att_bc[:], 1.0 - SLOPE, None, ALU.mult).then_inc(S["att"], 1)
                    dve.wait_ge(S["att"], 1)
                    for k in range(KH):
                        for i in range(2):
                            for h in range(H):
                                n = (k * 2 + i) * H + h
                                w_cols = i * XRW + h * HD
                                last = nc.vector.tensor_tensor_reduce(
                                    out=sq[:, n * HD:(n + 1) * HD], in0=wlr[:, k, w_cols:w_cols + HD],
                                    in1=att_lin[:, h * HD:(h + 1) * HD], scale=1.0, scalar=0.0, op0=ALU.mult,
                                    op1=ALU.add, accum_out=wlr[:, k, HID + i * H + h:HID + i * H + h + 1])
                    last.then_inc(S["wd"], 1)
                    linkB = Chain(dve, S["B"], 3)
                    linkD = Chain(dve, S["D"], 1)

                    def combine(t, s, m):
                        linkB.tile(t)
                        wait(dve, S["tr"], t - 1)
                        wait(dve, s_x1s[s], 16 * m)
                        dve.wait_ge(S["pb"], t + 1)
                        dve.wait_ge(s_ld[s], 32 * m + 32)
                        for h in range(H):
                            cols = slice(h * C, (h + 1) * C)
                            last = nc.vector.scalar_tensor_tensor(
                                out=y[:, s, cols], in0=xpt[:, s, cols],
                                scalar=sw[:, bass.ds(t, 1), h:h + 1].rearrange("p a n -> p (a n)"),
                                in1=g0[:, s, cols], op0=ALU.mult, op1=ALU.add)
                        linkB(last)
                        linkB(nc.vector.scalar_tensor_tensor(out=y[:, s], in0=y[:, s], scalar=0.0, in1=xin[:, s],
                                                             op0=ALU.max, op1=ALU.add))
                        for i in range(2):
                            last = nc.vector.bn_stats(st[:, s, 6 * i:6 * i + 6], y[:, s, i * 512:(i + 1) * 512])
                        linkB(last)
                        nc.vector.tensor_copy(mark[:], st[:, s, 0:1])
                        nc.vector.bn_aggr(mv[:, s, :], st[:, s, :]).then_inc(S["mv"], 1)

                    def factors(t, s, m):
                        linkD.tile(t)
                        dve.wait_ge(S["sd"], t + 1)
                        linkD(nc.vector.reciprocal(rs[:, s, 0:1], sd[:, s:s + 1]))
                        nc.vector.tensor_scalar(rs[:, s, 1:2], mv[:, s, 0:1], rs[:, s, 0:1], -1.0, ALU.mult, ALU.mult)\
                            .then_inc(S["rs"], 1)

                    def rms(t, s, m):
                        dve.wait_ge(S["sr"], t + 1)
                        nc.vector.reciprocal(rr[:, s:s + 1], sr[:, s:s + 1]).then_inc(S["rr"], 1)

                    def scale_h(t, s, m):
                        dve.wait_ge(S["hp"], t + 1)
                        dve.wait_ge(S["rr"], t + 1)
                        wait(dve, S["ht"], t - 1)
                        nc.vector.tensor_scalar(hd[:, s, :], psum[:, 4, 0:HID], rr[:, s:s + 1], None, ALU.mult)\
                            .then_inc(S["hd"], 1)

                    linkS = Chain(dve, sem("n_sfc"), 3)

                    def self_logit(t, s, m):
                        linkS.tile(t)
                        xrt = xr[:, bass.ds(t, 1), :].rearrange("p a n -> p (a n)")
                        dve.wait_ge(S["xlr"], 2 * t + 2)
                        wait(dve, S["sf"], t)
                        nc.vector.tensor_copy(xrt[:, HID:XLW], xls[:, s, XLW:XRW])
                        linkS(nc.vector.tensor_tensor(tmp2[:], xls[:, s, 0:HID], xrt[:, 0:HID], ALU.add))
                        nc.vector.tensor_tensor(both[:], xls[:, s, HID:XLW], xls[:, s, XLW:XRW], ALU.add)
                        linkS(nc.vector.scalar_tensor_tensor(out=tmp2[:], in0=tmp2[:], scalar=0.0, in1=att_relu[:],
                                                             op0=ALU.max, op1=ALU.mult))
                        linkS(nc.vector.tensor_reduce(out=relu_part[:], in_=tmp2[:].rearrange("p (h c) -> p h c", h=H),
                                                      op=ALU.add, axis=AX.X))
                        nc.vector.tensor_tensor(xrt[:, XLW:XRW], relu_part[:], both[:], ALU.add).then_inc(S["sf"], 1)
                    pipelined(dve, NT, [(3, factors), (2, combine), (6, self_logit), (3, rms), (4, scale_h)], AHEAD)

        with ExitStack() as ph:
            def sb(name, shape, dt=F32):
                return ph.enter_context(nc.sbuf_tensor(name, shape, dt))
            att_bc = sb("att_bc6", [P, HID])
            RING = 4
            lt = sb("lt6", [P, 2, U, P])
            onehot_t = sb("onehot_t6", [P, 2, U, P])
            rows = sb("rows6", [P, RING, U, XLW])
            msg = sb("msg6", [P, 2, U, XLW])
            prod = sb("prod6", [P, 2, U, HID])
            part = sb("part6", [P, 2, U, H])
            att_relu = sb("att_relu6", [P, HID])
            idx = sb("idx6", [P, RING, U], I32)
            s_att = sem("q_att")
            s_lt = [sem(f"q_lt{i}") for i in range(2)]
            s_r = [sem(f"q_r{i}") for i in range(RING)]
            s_xe = [sem(f"q_xe{i}") for i in range(RING)]
            s_ix, s_ot, s_pg, s_ad, s_pr, s_sc, s_pd, s_pt, s_rd = (sem("q_" + n) for n in
                                                              "ix ot pg ad pr sc pd pt rd".split())
            with nc.Block() as block:
                @block.gpsimd
                def _(pool):
                    gather = PoolGather(pool, N, bound)

                    def indices(g, s):
                        nc.gpsimd.tensor_copy(idx[:, s, :], isrc[:, bass.ds(g * U, U)]).then_inc(s_ix, 1)

                    def group(g, s, m):
                        gather.wait(s_ix, g + 1)
                        gather.wait(s_ad, g - RING + 1)
                        gather.wait(s_xe[s], 16 * m)
                        for j in range(U):
                            gather.rows_of(rows[:, s, j, :], xl_t, idx[:, s, j:j + 1]).then_inc(s_r[s], 16)
                            if j == 1:
                                s2 = (s + 1) % RING
                                gather.wait(s_r[s2], 64 * (m if s2 else m + 1))
                                indices(g + 1, s2)
                    indices(0, 0)
                    pipelined(pool, NG, [(0, group)], RING, RING)

                @block.sync
                def _(sp):
                    sp.dma_start(att_bc[:], att1.rearrange("h c -> (h c)").partition_broadcast(P)).then_inc(s_att, 16)

                    def load(g, s, m):
                        wait(sp, s_ot, g - 1)
                        s = s % 2
                        sp.dma_start(lt[:, s].rearrange("p j e -> p (j e)"),
                                     local_t[bass.ds(g * U, U), :].rearrange("j e -> (j e)").partition_broadcast(P))\
                          .then_inc(s_lt[s], 16)

                    def store_rows(g, s, m):
                        sp.wait_ge(s_r[s], 64 * m + 64)
                        sp.dma_start(xe_t[bass.ds(g, 1)].rearrange("a p n -> p (a n)"),
                                     rows[:, s].rearrange("p j n -> p (j n)")).then_inc(s_xe[s], 16)
                    pipelined(sp, NG, [(1, store_rows), (0, load)], RING, RING)
                    for s in range(RING):
                        sp.wait_ge(s_xe[s], 16 * NG // RING)

                @block.scalar
                def _(act):
                    def self_logits(g, s, m):
                        act.wait_ge(s_ad, g + 1)
                        nc.scalar.activation(w9[:, bass.ds(g * U, U), H:2 * H], psum[:, 4 * s:4 * s + 4, XLW:XRW],
                                             ACT.Copy).then_inc(s_sc, 1)
                    pipelined(act, NG, [(1, self_logits)])

                @block.tensor
                def _(pe):
                    tiles = StepTiles(pe, dtab, "q1")

                    def group(g, s, m):
                        ds = tiles.load(g)
                        pe.wait_ge(s_ot, g + 1)
                        wait(pe, s_sc, g - 1)
                        for j in range(U):
                            last = nc.tensor.matmul(psum[:, 4 * s + j, 0:XRW], onehot_t[:, s, j, :],
                                                    xr[:, bass.ds(ds[j], 1), :], start=True, stop=True)
                        last.then_inc(s_pg, 1)
                    pipelined(pe, NG, [(0, group)])

                @block.vector
                def _(dve):
                    dve.wait_ge(s_att, 16)
                    nc.vector.tensor_scalar(att_relu[:], att_bc[:], 1.0 - SLOPE, None, ALU.mult).then_inc(s_pr, 1)
                    dve.wait_ge(s_pr, 1)

                    def onehots(g, s, m):
                        s2, m2 = s % 2, (RING // 2) * m + s // 2
                        dve.wait_ge(s_lt[s2], 16 * m2 + 16)
                        wait(dve, s_pg, g - 1)
                        nc.vector.tensor_scalar(onehot_t[:, s2].rearrange("p j e -> p (j e)"),
                                                lt[:, s2].rearrange("p j e -> p (j e)"), pidx[:], None,
                                                ALU.is_equal).then_inc(s_ot, 1)

                    def add(g, s, m):
                        dve.wait_ge(s_pg, g + 1)
                        dve.wait_ge(s_r[s], 64 * m + 64)
                        wait(dve, s_rd, g - 1)
                        s2 = s % 2
                        nc.vector.tensor_tensor(msg[:, s2], psum[:, 4 * s2:4 * s2 + 4, 0:XLW], rows[:, s], ALU.add)\
                            .then_inc(s_ad, 1)

                    def reduce(g, s, m):
                        s = s % 2
                        dve.wait_ge(s_ad, g + 1)
                        wait(dve, s_rd, g - 1)
                        nc.vector.scalar_tensor_tensor(out=prod[:, s], in0=msg[:, s, :, 0:HID], scalar=0.0,
                                                       in1=bc(att_relu[:].unsqueeze(1), [P, U, HID]),
                                                       op0=ALU.max, op1=ALU.mult).then_inc(s_pd, 1)
                        dve.wait_ge(s_pd, g + 1)
                        nc.vector.tensor_reduce(out=part[:, s], in_=prod[:, s].rearrange("p j (h c) -> p j h c", h=H),
                                                op=ALU.add, axis=AX.X).then_inc(s_pt, 1)
                        dve.wait_ge(s_pt, g + 1)
                        nc.vector.tensor_tensor(w9[:, bass.ds(g * U, U), 0:H], part[:, s], msg[:, s, :, HID:XLW],
                                                ALU.add).then_inc(s_rd, 1)
                    pipelined(dve, NG, [(0, onehots), (1, add), (2, reduce)], RING, RING)

        weigh_edges(nc, sem, "l1", psum, w9, ident, isfirst, rs_f, rs_b, pen, any_f, any_b, [acc1, acc1_odd])

        with ExitStack() as ph:
            def sb(name, shape, dt=F32):
                return ph.enter_context(nc.sbuf_tensor(name, shape, dt))
            U2 = 2 * U
            NG2 = T // U2
            rows = sb("rows8", [P, 2, U2, XLW])
            onehot = sb("onehot8", [P, 2, U2, P])
            msg = sb("msg8", [P, 2, U2, ACC1])
            s_r = [sem(f"r_r{i}") for i in range(2)]
            s_o, s_ms, s_mp, s_ma, s_mm, s_acc = (sem("r_" + n) for n in "o ms mp ma mm acc".split())
            with nc.Block() as block:
                @block.sync
                def _(sp):
                    def load(g, s, m):
                        wait(sp, s_ma, (g - 1) * U2)
                        wait(sp, s_ms, g - 1)
                        wait(sp, s_mp, g - 1)
                        sp.dma_start(rows[:, s].rearrange("p (a j) n -> p a (j n)", a=2),
                                     xe_t.rearrange("(g a) p n -> g a p n", a=2)[bass.ds(g, 1)]
                                     .rearrange("g a p n -> p (g a) n")).then_inc(s_r[s], 16)
                    pipelined(sp, NG2, [(0, load)])

                @block.gpsimd
                def _(pool):
                    waits = PoolGather(pool, N, bound)

                    def weigh(g, s, m):
                        waits.wait(s_mm, (g - 1) * U2)
                        waits.wait(s_r[s], 16 * m + 16)
                        nc.gpsimd.tensor_tensor(
                            msg[:, s, :, HD:2 * HD], rows[:, s, :, HD:2 * HD],
                            bc(w9[:, bass.ds(g * U2, U2), 1:2], [P, U2, HD]), ALU.mult).then_inc(s_mp, 1)
                    pipelined(pool, NG2, [(0, weigh)])

                @block.scalar
                def _(act):
                    def weights(g, s, m):
                        wait(act, s_mm, (g - 1) * U2)
                        nc.scalar.activation(msg[:, s, :, HID:ACC1], w9[:, bass.ds(g * U2, U2), :], ACT.Copy)
                        act.wait_ge(s_r[s], 16 * m + 16)
                        for j in range(U2):
                            for h in range(2, H):
                                cols = slice(h * HD, (h + 1) * HD)
                                last = nc.scalar.activation(
                                    msg[:, s, j, cols], rows[:, s, j, cols], ACT.Copy,
                                    scale=w9[:, bass.ds(g * U2 + j, 1), h:h + 1].rearrange("p a b -> p (a b)"))
                            last.then_inc(s_ma, 1)
                    pipelined(act, NG2, [(0, weights)])

                @block.tensor
                def _(pe):
                    def group(g, s, m):
                        pe.wait_ge(s_o, g + 1)
                        pe.wait_ge(s_ms, g + 1)
                        pe.wait_ge(s_mp, g + 1)
                        for j in range(U2):
                            pe.wait_ge(s_ma, g * U2 + j + 1)
                            wait(pe, s_acc, g * U2 + j - 7)
                            nc.tensor.matmul(psum[:, j, 0:ACC1], onehot[:, s, j, :], msg[:, s, j, :],
                                             start=True, stop=True).then_inc(s_mm, 1)
                    pipelined(pe, NG2, [(0, group)])

                @block.vector
                def _(dve):
                    tiles = StepTiles(dve, dtab, "r1", U2)

                    def build(g, s, m):
                        wait(dve, s_mm, (g - 1) * U2)
                        nc.vector.tensor_tensor(
                            onehot[:, s], bc(iotar[:].unsqueeze(1), [P, U2, P]),
                            bc(ldst[:, bass.ds(g * U2, U2)].unsqueeze(2), [P, U2, P]), ALU.is_equal).then_inc(s_o, 1)
                        dve.wait_ge(s_r[s], 16 * m + 16)
                        nc.vector.tensor_tensor(msg[:, s, :, 0:HD], rows[:, s, :, 0:HD],
                                                bc(w9[:, bass.ds(g * U2, U2), 0:1], [P, U2, HD]), ALU.mult).then_inc(s_ms, 1)

                    def add(g, s, m):
                        ds = tiles.load(g)
                        for j in range(U2):
                            i = g * U2 + j
                            dve.wait_ge(s_mm, i + 1)
                            wait(dve, s_acc, i - 1)
                            sums = acc1_odd if j % 2 else acc1
                            av = sums[:, bass.ds(ds[j], 1), :].rearrange("p a n -> p (a n)")
                            nc.vector.tensor_tensor(av, psum[:, j, 0:ACC1], av, ALU.add).then_inc(s_acc, 1)
                    pipelined(dve, NG2, [(0, build), (1, add)])
                    dve.wait_ge(s_acc, T)
                    nc.vector.tensor_tensor(acc1, acc1, acc1_odd, ALU.add)

        with ExitStack() as ph:
            def sb(name, shape, dt=F32):
                return ph.enter_context(nc.sbuf_tensor(name, shape, dt))
            wu = sb("wu", [P, KH, D])
            noself = sb("noself9", [P, NT])
            wself = sb("wself9", [P, NT, H])
            rz = sb("rz9", [P, NT, H])
            sw = sb("sw9", [P, NT, H])
            eps = sb("eps9", [P, 1])
            XL1 = 5
            xl_in = sb("xl_in", [P, NT, HID])
            x1_in = sb("x1_in", [P, 2, D])
            gsum = sb("gsum", [P, 2, HID])
            gT = sb("gT", [P, 2, KH, P])
            y = sb("y9", [P, 2, D])
            o = sb("o9", [P, 2, D])
            st = sb("st9", [P, 2, 12])
            mv = sb("mv9", [P, 2, 2])
            mark = sb("mark9", [P, 1])
            sd = sb("sd9", [P, 2])
            rs = sb("rs9", [P, 2, 2])
            F = {n: sem("f_" + n) for n in "w z eps g0 g tr gT up s mv sd D rs o".split()}
            s_xl = [sem(f"f_xl{i}") for i in range(2)]
            s_x1 = [sem(f"f_x1{i}") for i in range(2)]
            s_out = [sem(f"f_out{i}") for i in range(2)]
            AHEAD = 8
            with nc.Block() as block:
                @block.sync
                def _(sp):
                    sp.dma_start(wu[:], w_up.rearrange("(k p) n -> p k n", p=P)).then_inc(F["w"], 16)

                    for i, (t0, t1) in enumerate(((0, XL1), (XL1, NT))):
                        sp.dma_start(xl_in[:, t0:t1, :], xl_t[t0 * P:t1 * P, 0:HID].rearrange("(t p) n -> p t n", p=P))\
                          .then_inc(s_xl[i], 16)

                    def load_x1(t, s, m):
                        wait(sp, F["s"], 2 * t - 2)
                        sp.dma_start(x1_in[:, s, :], x1_t[bass.ds(t * P, P), :]).then_inc(s_x1[s], 16)

                    def store(t, s, m):
                        sp.wait_ge(F["o"], t + 1)
                        rows = N_LAST if isinstance(t, int) and t == NT - 1 else P
                        sp.dma_start(out[bass.ds(t * P, rows), :], o[0:rows, s, :]).then_inc(s_out[s], 16)
                    pipelined(sp, NT, [(4, load_x1), (7, store)], AHEAD)
                    for s in range(2):
                        sp.wait_ge(s_out[s], 16 * ((NT + 1 - s) // 2))

                @block.gpsimd
                def _(pool):
                    nc.gpsimd.memset(eps[:], LN_EPS).then_inc(F["eps"], 1)

                @block.scalar
                def _(act):
                    act.wait_ge(F["z"], 1)
                    act.wait_ge(F["eps"], 1)

                    def divide(t, s, m):
                        wait(act, F["tr"], t - 1)
                        for h in range(H):
                            last = nc.scalar.activation(
                                gsum[:, s, h * HD:(h + 1) * HD],
                                acc1[:, bass.ds(t, 1), h * HD:(h + 1) * HD].rearrange("p a n -> p (a n)"), ACT.Copy,
                                scale=rz[:, bass.ds(t, 1), h:h + 1].rearrange("p a n -> p (a n)"))
                        last.then_inc(F["g0"], 1)

                    def take_gT(t, s, m):
                        act.wait_ge(F["tr"], t + 1)
                        wait(act, F["up"], t - 1)
                        nc.scalar.activation(gT[:, s].rearrange("p k n -> p (k n)"), psum[:, s, 0:HID],
                                             ACT.Copy).then_inc(F["gT"], 1)

                    def deviation(t, s, m):
                        act.wait_ge(F["mv"], t + 1)
                        nc.scalar.activation(sd[:, s:s + 1], mv[:, s, 1:2], ACT.Sqrt, bias=eps[:, 0:1]).then_inc(F["sd"], 1)

                    def normalise(t, s, m):
                        act.wait_ge(F["rs"], t + 1)
                        wait(act, s_out[s], 16 * m)
                        nc.scalar.activation(o[:, s, :], y[:, s, :], ACT.Identity, bias=rs[:, s, 1:2],
                                             scale=rs[:, s, 0:1]).then_inc(F["o"], 1)
                    pipelined(act, NT, [(6, deviation), (3, take_gT), (6, normalise), (0, divide)], AHEAD)

                @block.tensor
                def _(pe):
                    pe.wait_ge(F["w"], 16)

                    def transposes(t, s, m):
                        pe.wait_ge(F["g"], t + 1)
                        wait(pe, F["gT"], t - 1)
                        for k in range(KH):
                            last = nc.tensor.transpose(psum[:, s, k * P:(k + 1) * P], gsum[:, s, k * P:(k + 1) * P], ident[:])
                        last.then_inc(F["tr"], 1)

                    def up(t, s, m):
                        pe.wait_ge(F["gT"], t + 1)
                        wait(pe, F["s"], 2 * t - 2)
                        for k in range(KH):
                            for i in range(2):
                                last = nc.tensor.matmul(psum[:, 2 + 2 * s + i, :], gT[:, s, k, :],
                                                        wu[:, k, i * 512:(i + 1) * 512], start=(k == 0), stop=(k == KH - 1))
                        last.then_inc(F["up"], 1)
                    pipelined(pe, NT, [(2, transposes), (4, up)], AHEAD)

                @block.vector
                def _(dve):
                    divisor(nc, dve, sem("f_zc"), acc1[:, :, HID:ACC1], noself, wself, rz, sw, DEN_EPS)\
                        .then_inc(F["z"], 1)
                    linkD = Chain(dve, F["D"], 1)

                    def add_self(t, s, m):
                        dve.wait_ge(F["g0"], t + 1)
                        if isinstance(t, int) and t in (0, XL1):
                            dve.wait_ge(s_xl[t // XL1], 16)
                        for h in range(H):
                            cols = slice(h * HD, (h + 1) * HD)
                            last = nc.vector.scalar_tensor_tensor(
                                out=gsum[:, s, cols], in0=xl_in[:, bass.ds(t, 1), cols].rearrange("p a n -> p (a n)"),
                                scalar=sw[:, bass.ds(t, 1), h:h + 1].rearrange("p a n -> p (a n)"),
                                in1=gsum[:, s, cols], op0=ALU.mult, op1=ALU.add)
                        last.then_inc(F["g"], 1)

                    def residual(t, s, m):
                        dve.wait_ge(F["up"], t + 1)
                        dve.wait_ge(s_x1[s], 16 * m + 16)
                        wait(dve, F["o"], t - 1)
                        nc.vector.tensor_tensor(y[:, s], psum[:, 2 + 2 * s:4 + 2 * s].rearrange("p a b -> p (a b)"),
                                                x1_in[:, s], ALU.add).then_inc(F["s"], 1)
                        dve.wait_ge(F["s"], 2 * t + 1)
                        for i in range(2):
                            last = nc.vector.bn_stats(st[:, s, 6 * i:6 * i + 6], y[:, s, i * 512:(i + 1) * 512])
                        last.then_inc(F["s"], 1)
                        dve.wait_ge(F["s"], 2 * t + 2)
                        nc.vector.tensor_copy(mark[:], st[:, s, 0:1])
                        nc.vector.bn_aggr(mv[:, s, :], st[:, s, :]).then_inc(F["mv"], 1)

                    def factors(t, s, m):
                        linkD.tile(t)
                        dve.wait_ge(F["sd"], t + 1)
                        linkD(nc.vector.reciprocal(rs[:, s, 0:1], sd[:, s:s + 1]))
                        nc.vector.tensor_scalar(rs[:, s, 1:2], mv[:, s, 0:1], rs[:, s, 0:1], -1.0, ALU.mult, ALU.mult)\
                            .then_inc(F["rs"], 1)
                    pipelined(dve, NT, [(1, add_self), (6, factors), (5, residual)], AHEAD)


def divisor(nc, dve, chain, z9, noself, wself, rz, sw, eps):
    link = Chain(dve, chain)
    link(nc.vector.tensor_scalar(noself[:], z9[:, :, 2 * H], -1.0, 1.0, ALU.mult, ALU.add))
    link(nc.vector.tensor_tensor(wself[:], z9[:, :, H:2 * H], bc(noself[:].unsqueeze(2), [P, NT, H]), ALU.add))
    link(nc.vector.tensor_tensor(rz[:], z9[:, :, 0:H], wself[:], ALU.add))
    if eps:
        link(nc.vector.tensor_scalar_add(rz[:], rz[:], eps))
    link(nc.vector.reciprocal(rz[:], rz[:]))
    return nc.vector.tensor_tensor(sw[:], wself[:], rz[:], ALU.mult)


N_EDGE_DMAS = 3 + 2 * NB


def weigh_edges(nc, sem, tag, psum, w9, ident, isfirst, rs_f, rs_b, pen, any_f, any_b, sums):
    with ExitStack() as ph:
        def sb(name, shape, dt=F32):
            return ph.enter_context(nc.sbuf_tensor(f"{tag}_{name}", shape, dt))
        v = sb("v", [TB, NB, H, P])
        sv = sb("sv", [TB, NB, H, P])
        fw = sb("fw", [TB, NB, H, P])
        bw = sb("bw", [TB, NB, H, P])
        cf = sb("cf", [H, T + 1])
        cb = sb("cb", [H, T + 1])
        cin = sb("cin", [TB, 2, NB, H])
        s_t1 = sem(f"{tag}_t1")
        s_sv = sem(f"{tag}_sv")
        s_dv = sem(f"{tag}_chain")
        s_f1 = sem(f"{tag}_f1")
        s_t2 = sem(f"{tag}_t2")
        s_c = sem(f"{tag}_c")
        s_t3 = sem(f"{tag}_t3")
        s_m = sem(f"{tag}_m")
        s_e = sem(f"{tag}_e")
        s_t4 = sem(f"{tag}_t4")
        with nc.Block() as block:
            @block.gpsimd
            def _(pool):
                for a in sums:
                    nc.gpsimd.memset(a, 0.0)

            @block.tensor
            def _(pe):
                for b in range(NB):
                    for h in range(H):
                        for i in range(2):
                            last = nc.tensor.transpose(psum[0:TB, 4 * i + b, h * P:(h + 1) * P],
                                                       w9[:, b * TB:(b + 1) * TB, i * H + h], ident[:])
                    last.then_inc(s_t1, 1)
                pe.wait_ge(s_f1, 1)
                pe.wait_ge(s_sv, NB)
                for b in range(NB):
                    nc.tensor.transpose(psum[0:H, 0, b * TB:(b + 1) * TB], fw[:, b, :, P - 1], ident[0:TB, 0:TB])
                    last = nc.tensor.transpose(psum[0:H, 1, b * TB:(b + 1) * TB], bw[:, b, :, 0], ident[0:TB, 0:TB])
                last.then_inc(s_t2, 1)
                pe.wait_ge(s_c, 1)
                for b in range(NB):
                    nc.tensor.transpose(psum[0:TB, 2, b * H:(b + 1) * H], cf[:, b * TB:(b + 1) * TB], ident[0:H, 0:H])
                    last = nc.tensor.transpose(psum[0:TB, 2, (NB + b) * H:(NB + b + 1) * H],
                                               cb[:, b * TB + 1:(b + 1) * TB + 1], ident[0:H, 0:H])
                last.then_inc(s_t3, 1)
                for b in range(NB):
                    pe.wait_ge(s_e, b + 1)
                    for h in range(H):
                        nc.tensor.transpose(psum[:, b, h * TB:(h + 1) * TB], v[:, b, h, :], ident[0:TB, 0:TB])
                        last = nc.tensor.transpose(psum[:, 4 + b, h * TB:(h + 1) * TB], sv[:, b, h, :], ident[0:TB, 0:TB])
                    last.then_inc(s_t4, 1)

            @block.scalar
            def _(act):
                for b in range(NB):
                    act.wait_ge(s_t1, b + 1)
                    nc.scalar.activation(sv[:, b].rearrange("p h e -> p (h e)"), psum[0:TB, 4 + b, :], ACT.Copy)\
                        .then_inc(s_sv, 1)
                for b in range(NB):
                    act.wait_ge(s_m, b + 1)
                    nc.scalar.activation(v[:, b], v[:, b], ACT.Exp)
                    nc.scalar.activation(sv[:, b], sv[:, b], ACT.Exp).then_inc(s_e, 1)
                for b in range(NB):
                    act.wait_ge(s_t4, b + 1)
                    nc.scalar.activation(w9[:, b * TB:(b + 1) * TB, 0:H].rearrange("p t h -> p h t"),
                                         psum[:, b, 0:H * TB].rearrange("p (h t) -> p h t", h=H), ACT.Copy)

            @block.vector
            def _(dve):
                link = Chain(dve, s_dv)
                nc.vector.memset(cf[:], -BIG)
                nc.vector.memset(cb[:], -BIG)
                for b in range(NB):
                    dve.wait_ge(s_t1, b + 1)
                    link(nc.vector.tensor_tensor(v[:, b], psum[0:TB, b, :].rearrange("p (h e) -> p h e", h=H),
                                                 bc(pen[:, b, :].unsqueeze(1), [TB, H, P]), ALU.add))

                def scans(start):
                    for b in range(NB):
                        for h in range(H):
                            nc.vector.tensor_tensor_scan(fw[:, b, h, :], rs_f[:, b, :], v[:, b, h, :],
                                                         start(0, b, h), ALU.add, ALU.max)
                            last = nc.vector.tensor_tensor_scan(bw[:, b, h, ::-1], rs_b[:, b, ::-1], v[:, b, h, ::-1],
                                                                start(1, b, h), ALU.add, ALU.max)
                    return last
                scans(lambda i, b, h: -BIG).then_inc(s_f1, 1)
                dve.wait_ge(s_t2, 1)
                nc.vector.tensor_tensor_scan(cf[:, 1:T + 1], any_f[:], psum[0:H, 0, 0:T], -BIG, ALU.add, ALU.max)
                nc.vector.tensor_tensor_scan(cb[:, T - 1::-1], any_b[:, ::-1], psum[0:H, 1, T - 1::-1], -BIG,
                                             ALU.add, ALU.max).then_inc(s_c, 1)
                dve.wait_ge(s_t3, 1)
                link(nc.vector.tensor_copy(cin[:].rearrange("p i b h -> p (i b h)"), psum[0:TB, 2, 0:2 * NB * H]))
                link(scans(lambda i, b, h: cin[:, i, b, h:h + 1]))
                dve.wait_ge(s_sv, NB)
                for b in range(NB):
                    link(nc.vector.tensor_tensor(fw[:, b], fw[:, b], bw[:, b], ALU.max))
                    link(nc.vector.tensor_tensor(fw[:, b], fw[:, b], sv[:, b], ALU.max))
                    nc.vector.tensor_tensor(v[:, b], v[:, b], fw[:, b], ALU.subtract)
                    nc.vector.tensor_tensor(sv[:, b], sv[:, b], fw[:, b], ALU.subtract).then_inc(s_m, 1)
                for b in range(NB):
                    dve.wait_ge(s_t4, b + 1)
                    nc.vector.tensor_tensor(w9[:, b * TB:(b + 1) * TB, H:2 * H].rearrange("p t h -> p h t"),
                                            psum[:, 4 + b, 0:H * TB].rearrange("p (h t) -> p h t", h=H),
                                            bc(isfirst[:, b * TB:(b + 1) * TB].unsqueeze(1), [P, H, TB]), ALU.mult)
                nc.vector.tensor_copy(w9[:, :, 2 * H], isfirst[:])


_INS = ['x', 'src', 'dst', 'L0_gnn_W', 'L0_gnn_att_src', 'L0_gnn_att_dst', 'L0_gnn_bias', 'L1_gnn_rms_w',
        'L1_gnn_W_down', 'L1_gnn_Wl', 'L1_gnn_Wr', 'L1_gnn_att', 'L1_gnn_W_up']


def kernel(**inputs):
    import numpy as np
    import concourse.bacc as bacc
    from concourse import mybir
    from concourse.bass_utils import run_bass_kernel_spmd
    nc = bacc.Bacc("TRN2", target_bir_lowering=False, num_devices=1)
    arrays, args = {}, []
    for name in _INS:
        a = np.ascontiguousarray(inputs[name])
        arrays["in_" + name] = a
        args.append(nc.dram_tensor("in_" + name, a.shape, mybir.dt.from_np(a.dtype), kind="ExternalInput").ap())
    out = nc.dram_tensor("out_0", (N, D), F32, kind="ExternalOutput").ap()
    gnn_kernel(nc, *args, out)
    r = run_bass_kernel_spmd(nc, [arrays], core_ids=[0])
    return r.results[0]["out_0"]
```

```python
import concourse.bass as bass
from concourse import mybir
from contextlib import ExitStack

F32 = mybir.dt.float32
I32 = mybir.dt.int32
BF16 = mybir.dt.bfloat16
ALU = mybir.AluOpType
ACT = mybir.ActivationFunctionType
AX = mybir.AxisListType

P = 128
N, E, D, H, C = 3125, 50000, 1024, 4, 256
HID = 256
HD = HID // H
KD = D // P
KH = HID // P
NT = -(-N // P)
NP = NT * P
N_LAST = N - (NT - 1) * P
NC = -(-E // P)
NCF = E // P
E_LAST = E - NCF * P
NB = 4
U = 4
T = -(-(NC + NT - 1) // (2 * U * NB)) * 2 * U * NB
TB = T // NB
NG = T // U
NO_DST = 8191
BIG = 1e30
SLOPE = 0.2
LN_EPS = 1e-5
RMS_EPS = 1e-6
DEN_EPS = 1e-16
POOL_HEADS = 3
PARTS = 3
W9 = 2 * H + 1
XLW = HID + H
XRW = HID + 2 * H
ACC1 = HID + W9


def wait(eng, sem, value):
    if not isinstance(value, int) or value > 0:
        eng.wait_ge(sem, value)


class Chain:

    def __init__(self, eng, sem, per=0, base=0):
        self.eng, self.sem, self.per, self.base, self.k = eng, sem, per, base, 0

    def tile(self, t):
        assert self.k == (self.per if self.k else 0) or not self.per
        self.base, self.k = t * self.per, 0

    def __call__(self, ins):
        ins.then_inc(self.sem, 1)
        self.k += 1
        self.eng.wait_ge(self.sem, self.base + self.k)


def pipelined(eng, n, stages, ahead=4, ring=2, unroll=1):
    last = n + max(lag for lag, _ in stages)
    first = ahead + -ahead % ring
    body = ring * unroll
    count = max(0, (n - first) // body)

    def turns(v0, v1):
        for v in range(v0, min(v1, last)):
            for lag, f in stages:
                t = v - lag
                if 0 <= t < n:
                    f(t, t % ring, t // ring)

    turns(0, first)
    if count:
        with eng.Fori(0, count) as i:
            for par in range(body):
                for lag, f in stages:
                    c = first + par - lag
                    f(body * i + c, c % ring, unroll * i + c // ring)
    turns(first + count * body, last)


def bc(ap, shape):
    return ap.to_broadcast(shape)


class StepTiles:

    def __init__(self, eng, dtab, name, steps=U):
        self.eng, self.dtab, self.steps = eng, dtab, steps
        self.regs = [eng.alloc_register(f"{name}_d{j}") for j in range(steps)]

    def load(self, g):
        self.eng.reg_load(self.regs, self.dtab[0:1, bass.ds(g * self.steps, self.steps)])
        return [self.eng.snap(r, min_val=0, max_val=NT - 1) for r in self.regs]


class PoolGather:

    def __init__(self, pool, rows, bound):
        self.pool, self.bound, self.rows = pool, bound, rows
        pool.reg_mov(bound, rows - 1)

    def wait(self, sem, value):
        if isinstance(value, int) and value <= 0:
            return
        self.pool.wait_ge(sem, value)
        self.pool.reg_alu(self.bound, self.bound, self.rows - 1, ALU.min)

    def rows_of(self, out, table, idx):
        return self.pool.indirect_dma_start(out, None, table, bass.IndirectOffsetOnAxis(ap=idx, axis=0),
                                            bounds_check=self.bound, oob_is_err=False)


ROW = E // 125
EC = -(-E // P)
E_TAIL = E - (P - 1) * EC
KEYS = N
KEY_BLOCKS = E // KEYS


def order_edges(nc, sem, psum, dst, src, dst_t, src_t, bound, load_weights):
    assert KEY_BLOCKS * KEYS == E and ROW * 125 == E
    with ExitStack() as ph:
        def sb(name, shape, dt=F32):
            return ph.enter_context(nc.sbuf_tensor("order_" + name, shape, dt))
        near = sb("near", [125, ROW + 1], I32)
        near_f = sb("near_f", [125, ROW + 1])
        falls = sb("falls", [125, ROW])
        row_falls = sb("row_falls", [125, 1])
        one = sb("one", [125, 1])
        flag = sb("flag", [1, 1], I32)
        pair = sb("pair", [P, 2, EC], I32)
        dst_key = sb("dst_key", [P, EC])
        block_i = sb("block_i", [P, KEYS], I32)
        key = sb("key", [P, KEYS])
        below = sb("below", [P, KEYS])
        within_i = sb("within_i", [P, KEYS], I32)
        within = sb("within", [P, KEYS])
        edge_i = sb("edge_i", [P, EC], I32)
        edge = sb("edge", [P, EC])
        limit = sb("limit", [P, EC])
        count = sb("count", [P, 1])
        rank = sb("rank", [P, EC])
        rank_i = sb("rank_i", [P, EC], I32)
        place = sb("place", [P, 1], I32)
        moved = sb("moved", [P, 2], I32)
        s_pad, s_ld, s_copy, s_chk, s_falls, s_flag, s_block, s_used, s_scat = (
            sem("order_" + n) for n in "pad ld copy chk falls flag block used scat".split())
        N_CHECKED = 2
        with nc.Block() as block:
            @block.gpsimd
            def _(pool):
                nc.gpsimd.memset(near[:], NO_DST).then_inc(s_pad, 1)
                nc.gpsimd.memset(one[:], 1.0).then_inc(s_pad, 1)
                nc.gpsimd.memset(pair[:], NO_DST).then_inc(s_pad, 1)
                unordered = pool.alloc_register("order_pool")
                pool.wait_ge(s_flag, 1)
                pool.reg_load([unordered], flag[0:1, 0:1])
                with pool.If_ne(unordered, 0):
                    nc.gpsimd.iota(within_i[:], pattern=[[1, KEYS]], base=0, channel_multiplier=0).then_inc(s_pad, 1)
                    nc.gpsimd.iota(edge_i[:], pattern=[[1, EC]], base=0, channel_multiplier=EC).then_inc(s_pad, 1)
                    pool.wait_ge(s_pad, 5)
                    nc.gpsimd.tensor_copy(within[:], within_i[:]).then_inc(s_pad, 1)
                    nc.gpsimd.tensor_copy(edge[:], edge_i[:]).then_inc(s_pad, 1)
                    pool.wait_ge(s_used, KEY_BLOCKS + 1)
                    pool.wait_ge(s_copy, 32)
                    scatter = PoolGather(pool, E, bound)
                    with pool.Fori(0, EC) as c:
                        nc.gpsimd.tensor_copy(place[:], rank_i[:, bass.ds(c, 1)]).then_inc(s_used, 1)
                        nc.gpsimd.tensor_copy(moved[:], pair[:, :, bass.ds(c, 1)].rearrange("p k a -> p (k a)"))\
                          .then_inc(s_used, 1)
                        scatter.wait(s_used, c * 2 + KEY_BLOCKS + 3)
                        for k, table in enumerate((dst_t, src_t)):
                            pool.indirect_dma_start(table.rearrange("(e a) -> e a", a=1),
                                                    bass.IndirectOffsetOnAxis(ap=place[:, 0:1], axis=0),
                                                    moved[:, k:k + 1], None, bounds_check=bound, oob_is_err=False)\
                                .then_inc(s_scat, 16)
                        scatter.wait(s_scat, c * 32 + 32)

            @block.sync
            def _(sp):
                sp.wait_ge(s_pad, 3)
                sp.dma_start(near[0:124, :], bass.AP(dst.tensor, 0, [[ROW, 124], [1, ROW + 1]])).then_inc(s_ld, 16)
                sp.dma_start(near[124:125, 0:ROW], dst[124 * ROW:E].rearrange("(a k) -> a k", a=1)).then_inc(s_ld, 16)
                sp.dma_start(dst_t.rearrange("(a k) -> a k", k=ROW), dst.rearrange("(a k) -> a k", k=ROW))\
                  .then_inc(s_copy, 16)
                sp.dma_start(src_t.rearrange("(a k) -> a k", k=ROW), src.rearrange("(a k) -> a k", k=ROW))\
                  .then_inc(s_copy, 16)
                load_weights(sp)
                unordered = sp.alloc_register("order_sp")
                sp.wait_ge(s_flag, 1)
                sp.reg_load([unordered], flag[0:1, 0:1])
                with sp.If_ne(unordered, 0):
                    for k, v in enumerate((dst, src)):
                        sp.dma_start(pair[0:P - 1, k, :], v[0:(P - 1) * EC].rearrange("(p c) -> p c", c=EC))\
                          .then_inc(s_ld, 16)
                        sp.dma_start(pair[P - 1:P, k, 0:E_TAIL], v[(P - 1) * EC:E].rearrange("(a k) -> a k", a=1))\
                          .then_inc(s_ld, 16)
                    for b in range(KEY_BLOCKS):
                        wait(sp, s_used, b)
                        sp.dma_start(block_i[:], dst[b * KEYS:(b + 1) * KEYS].partition_broadcast(P))\
                          .then_inc(s_block, 16)
                sp.wait_ge(s_copy, 32)

            @block.tensor
            def _(pe):
                pe.wait_ge(s_falls, 1)
                nc.tensor.matmul(psum[0:1, 0, 0:1], row_falls[:], one[:], start=True, stop=True).then_inc(s_falls, 1)

            @block.vector
            def _(dve):
                link = Chain(dve, s_chk)
                dve.wait_ge(s_ld, 16 * N_CHECKED)
                link(nc.vector.tensor_copy(near_f[:], near[:]))
                link(nc.vector.tensor_tensor(falls[:], near_f[:, 0:ROW], near_f[:, 1:ROW + 1], ALU.is_gt))
                nc.vector.reduce_sum(row_falls[:], falls[:], AX.X).then_inc(s_falls, 1)
                dve.wait_ge(s_falls, 2)
                nc.vector.tensor_copy(flag[:], psum[0:1, 0, 0:1]).then_inc(s_flag, 1)
                unordered = dve.alloc_register("order_dve")
                dve.wait_ge(s_flag, 1)
                dve.reg_load([unordered], flag[0:1, 0:1])
                with dve.If_ne(unordered, 0):
                    dve.wait_ge(s_ld, 16 * (N_CHECKED + 4))
                    dve.wait_ge(s_pad, 7)
                    link(nc.vector.tensor_copy(dst_key[:], pair[:, 0, :]))
                    link(nc.vector.tensor_scalar(dst_key[:], dst_key[:], float(KEYS), None, ALU.mult))
                    link(nc.vector.memset(rank[:], 0.0))
                    for b in range(KEY_BLOCKS):
                        dve.wait_ge(s_block, 16 * (b + 1))
                        conv = nc.vector.tensor_copy(key[:], block_i[:])
                        conv.then_inc(s_used, 1)
                        dve.wait_ge(s_used, b + 1)
                        link(nc.vector.scalar_tensor_tensor(out=key[:], in0=key[:], scalar=float(KEYS), in1=within[:],
                                                            op0=ALU.mult, op1=ALU.add))
                        link(nc.vector.tensor_scalar(limit[:], edge[:], float(-b * KEYS), 0.0, ALU.add, ALU.max))
                        link(nc.vector.scalar_tensor_tensor(out=limit[:], in0=limit[:], scalar=float(KEYS),
                                                            in1=dst_key[:], op0=ALU.min, op1=ALU.add))
                        base = link.k
                        with dve.Fori(0, EC) as c:
                            dve.wait_ge(s_chk, base + 3 * c)
                            nc.vector.tensor_scalar(below[:], key[:], limit[:, bass.ds(c, 1)], None, ALU.is_lt)\
                              .then_inc(s_chk, 1)
                            dve.wait_ge(s_chk, base + 3 * c + 1)
                            nc.vector.reduce_sum(count[:], below[:], AX.X).then_inc(s_chk, 1)
                            dve.wait_ge(s_chk, base + 3 * c + 2)
                            nc.vector.tensor_tensor(rank[:, bass.ds(c, 1)], rank[:, bass.ds(c, 1)], count[:], ALU.add)\
                              .then_inc(s_chk, 1)
                        link.k += 3 * EC
                        dve.wait_ge(s_chk, link.k)
                    nc.vector.tensor_copy(rank_i[:], rank[:]).then_inc(s_used, 1)


def gnn_kernel(nc, x, src, dst, w0, att_s, att_d, bias, rms_w, w_down, wl, wr, att1, w_up, out):
    dst_t = nc.dram_tensor("dst_ordered", (E,), I32, kind="Internal").ap()
    src_t = nc.dram_tensor("src_ordered", (E,), I32, kind="Internal").ap()
    edge_t = nc.dram_tensor("edge_table", (T, 4 * P), F32, kind="Internal").ap()
    local_t = nc.dram_tensor("local_dst", (T, P), F32, kind="Internal").ap()
    as_t = nc.dram_tensor("a_src_table", (NP, H), F32, kind="Internal").ap()
    xp_t = nc.dram_tensor("xp_table", (NP, D), F32, kind="Internal").ap()
    x1_t = nc.dram_tensor("x1_table", (NP, D), F32, kind="Internal").ap()
    xe_t = nc.dram_tensor("edge_rows", (NG, P, U * XLW), F32, kind="Internal").ap()
    xl_t = nc.dram_tensor("xl_table", (NP, XLW), F32, kind="Internal").ap()

    top = ExitStack()

    def sem(name):
        return top.enter_context(nc.semaphore(name))

    with top:
        def keep(name, shape, dt=F32):
            return top.enter_context(nc.sbuf_tensor(name, shape, dt))

        ident = keep("ident", [P, P])
        iotar = keep("iotar", [P, P])
        pidx = keep("pidx", [P, 1])
        ldst = keep("ldst", [P, T])
        isrc = keep("isrc", [P, T])
        isfirst = keep("isfirst", [P, T])
        dtab = keep("dtab", [1, T], I32)
        rs_f = keep("rs_f", [TB, NB, P])
        rs_b = keep("rs_b", [TB, NB, P])
        pen = keep("pen", [TB, NB, P])
        any_f = keep("any_f", [H, T])
        any_b = keep("any_b", [H, T])
        w9 = keep("w9", [P, T, W9])
        nt0 = keep("nt0", [P, NT, PARTS, 2 * H], BF16)
        bound = nc.gpsimd.alloc_register("row_bound")
        psum = top.enter_context(nc.psum_tensor("banks", [P, 8, 512], F32))


        with ExitStack() as ph:
            def sb(name, shape, dt=F32):
                return ph.enter_context(nc.sbuf_tensor(name, shape, dt))
            w_sb = sb("w0_sb", [P, KD, D])
            atts = sb("atts_bc", [P, D])
            attd = sb("attd_bc", [P, D])
            s_att = sem("s_att")
            W_FIRST = 3
            s_w = [sem(f"s_w{k}") for k in range(2)]

            def load_weights(sp):
                sp.dma_start(atts[:], att_s.rearrange("h c -> (h c)").partition_broadcast(P)).then_inc(s_att, 16)
                sp.dma_start(attd[:], att_d.rearrange("h c -> (h c)").partition_broadcast(P)).then_inc(s_att, 16)
                for k in range(KD):
                    sp.dma_start(w_sb[:, k, :], w0[k * P:(k + 1) * P, :]).then_inc(s_w[k >= W_FIRST], 16)
            order_edges(nc, sem, psum, dst, src, dst_t, src_t, bound, load_weights)
            dst, src = dst_t, src_t
            NJ = 8
            junk = sb("junk", [P, NJ, C])
            wa = sb("wa", [P, KD, 2 * H])
            mark0 = sb("mark0", [P, 1])
            mark1 = sb("mark1", [P, 1])
            NPAIR = -(-NT // 2)
            xin = sb("xin", [P, 2, 2, D])
            xT = sb("xT", [P, 2, KD, 2 * P])
            aT = sb("aT", [2 * H, NPAIR, 2 * P])
            a_all = sb("a_all", [P, NT, 2 * H])
            a_sum = sb("a_sum", [P, NT, H])
            nodes = sb("nodes", [P, NT, 2 * H])
            dx = sb("dx", [TB, NB, P + 2], I32)
            sx = sb("sx", [TB, NB, P], I32)
            dxf = sb("dxf", [TB, NB, P + 2])
            ct = sb("ct", [TB, NB, 4, P])
            st = sb("st", [TB, NB, 4, P])
            lasti = sb("lasti", [1, NC], I32)
            lastf = sb("lastf", [1, NC])
            lastw = sb("lastw", [1, NC])
            ioti = sb("ioti", [P, NC], I32)
            iotc = sb("iotc", [1, NC])
            step128 = sb("step128", [TB, NB])
            stepi = sb("stepi", [TB, NB], I32)
            ones = sb("ones", [1, P])
            less = sb("less", [TB, NC])
            ci = sb("ci", [TB, NB])
            cii = sb("cii", [TB, NB], I32)
            di = sb("di", [TB, NB])
            dneg = sb("dneg", [TB, NB])
            dcl = sb("dcl", [TB, NB])
            lrow = sb("lrow", [TB, NB, P])
            val = sb("val", [TB, NB, P])
            fv = sb("fv", [TB, NB, P])
            lv = sb("lv", [TB, NB, P])
            af = sb("af", [TB, NB, H])
            ab = sb("ab", [TB, NB, H])

            s_pad = sem("s_pad")
            s_edges = sem("s_edges")
            s_lrow = sem("s_lrow")
            s_iota = sem("s_iota")
            s_ident = sem("s_ident")
            s_dv = sem("s_setup_chain")
            s_ct = sem("s_ct")
            s_et = sem("s_et")
            s_lastw = sem("s_lastw")
            s_bcast = sem("s_bcast")
            s_ci = sem("s_ci")
            s_st = sem("s_st")
            s_lw = sem("s_lw")
            s_lt = sem("s_ltst")
            s_tp = sem("s_tp")
            s_wa = sem("s_wa")
            s_xi = [sem(f"s_xi{i}") for i in range(2)]
            s_tr = sem("s_tr")
            s_xT = sem("s_xT")
            s_am = sem("s_am")
            s_ac = sem("s_ac")
            s_at = sem("s_at")
            s_all = sem("s_all")
            s_as = sem("s_as")

            with nc.Block() as block:
                @block.gpsimd
                def _(pool):
                    nc.gpsimd.memset(dx[:], NO_DST).then_inc(s_pad, 1)
                    nc.gpsimd.memset(sx[:], 0).then_inc(s_pad, 1)
                    nc.gpsimd.memset(lasti[:], NO_DST).then_inc(s_pad, 1)
                    nc.gpsimd.iota(ioti[:], pattern=[[P, NC]], base=0, channel_multiplier=0).then_inc(s_iota, 1)
                    pool.wait_ge(s_iota, 1)
                    nc.gpsimd.tensor_copy(iotc[:], ioti[0:1, :]).then_inc(s_iota, 1)
                    nc.gpsimd.iota(stepi[:], pattern=[[P * TB, NB]], base=0, channel_multiplier=P).then_inc(s_iota, 1)
                    pool.wait_ge(s_iota, 3)
                    nc.gpsimd.tensor_copy(step128[:], stepi[:]).then_inc(s_iota, 1)
                    nc.gpsimd.iota(ioti[:, 0:P], pattern=[[1, P]], base=0, channel_multiplier=0).then_inc(s_iota, 1)
                    pool.wait_ge(s_iota, 5)
                    nc.gpsimd.tensor_copy(iotar[:], ioti[:, 0:P]).then_inc(s_iota, 1)
                    nc.gpsimd.iota(ioti[:, P:P + 1], pattern=[[0, 1]], base=0, channel_multiplier=1).then_inc(s_iota, 1)
                    pool.wait_ge(s_iota, 7)
                    nc.gpsimd.tensor_copy(pidx[:], ioti[:, P:P + 1]).then_inc(s_iota, 1)
                    nc.gpsimd.memset(ones[:], 1.0).then_inc(s_iota, 1)
                    nc.gpsimd.memset(xin[:], 0.0).then_inc(s_pad, 1)
                    nc.gpsimd.memset(ident[:], 0.0).then_inc(s_ident, 1)
                    pool.wait_ge(s_ident, 1)
                    nc.gpsimd.affine_select(out=ident[:], in_=ident[:], compare_op=ALU.not_equal, fill=1.0,
                                            base=0, pattern=[[-1, P]], channel_multiplier=1).then_inc(s_ident, 1)
                    gather = PoolGather(pool, T, bound)
                    pool.wait_ge(s_ci, 1)
                    pool.wait_ge(s_et, 16)
                    for b in range(NB):
                        gather.rows_of(st[:, b, :, :].rearrange("p f k -> p (f k)"), edge_t, cii[:, b:b + 1])\
                              .then_inc(s_st, 16)

                @block.sync
                def _(sp):
                    sp.wait_ge(s_pad, 3)
                    with nc.allow_non_contiguous_dma(reason="one word of each chunk"):
                        sp.dma_start(lasti[0:1, 0:NCF], dst[0:NCF * P].rearrange("(c k) -> k c", k=P)[P - 1:P, :])\
                          .then_inc(s_lrow, 16)
                    dh = dst.tensor
                    first = sp.dma_start(dx[0:1, 0, 1:P + 2], dst[0:P + 1].rearrange("(a k) -> a k", a=1))
                    first.then_inc(s_edges, 16)
                    n_edge = 1
                    for b in range(NB):
                        c0, c1 = max(1, b * TB), min((b + 1) * TB, NCF)
                        sp.dma_start(dx[c0 - b * TB:c1 - b * TB, b, :],
                                     bass.AP(dh, c0 * P - 1, [[P, c1 - c0], [1, P + 2]])).then_inc(s_edges, 16)
                        c0 = b * TB
                        sp.dma_start(sx[0:c1 - c0, b, :],
                                     src[c0 * P:c1 * P].rearrange("(p k) -> p k", k=P)).then_inc(s_edges, 16)
                        n_edge += 2
                    pl, bl = NCF % TB, NCF // TB
                    sp.dma_start(dx[pl:pl + 1, bl, 0:E_LAST + 1],
                                 dst[NCF * P - 1:E].rearrange("(a k) -> a k", a=1)).then_inc(s_edges, 16)
                    sp.dma_start(sx[pl:pl + 1, bl, 0:E_LAST],
                                 src[NCF * P:E].rearrange("(a k) -> a k", a=1)).then_inc(s_edges, 16)
                    assert n_edge + 2 == N_EDGE_DMAS
                    sp.wait_ge(s_ct, 1)
                    sp.dma_start(edge_t.rearrange("(b p) n -> p b n", b=NB),
                                 ct[:].rearrange("p b f k -> p b (f k)")).then_inc(s_et, 16)
                    sp.wait_ge(s_lw, 1)
                    sp.dma_start(local_t.rearrange("(b p) n -> p b n", b=NB), lrow[:]).then_inc(s_lt, 16)
                    sp.wait_ge(s_all, 1)
                    with nc.allow_non_contiguous_dma(reason="four words a node"):
                        sp.dma_start(as_t.rearrange("(t p) h -> p t h", p=P), a_all[:, :, 0:H]).then_inc(s_as, 16)
                    sp.wait_ge(s_as, 16)
                    sp.wait_ge(s_lt, 16)

                @block.scalar
                def _(act):
                    act.wait_ge(s_pad, 4)

                    def load_x(t, s, m):
                        wait(act, s_tr, 2 * t - 2)
                        if isinstance(t, int) and t == NPAIR - 1:
                            act.dma_start(xin[0:N_LAST, s, 0, :], x[t * 2 * P:N, :]).then_inc(s_xi[s], 16)
                        else:
                            act.dma_start(xin[:, s], x[bass.ds(t * 2 * P, 2 * P), :].rearrange("(a p) d -> p a d", a=2))\
                               .then_inc(s_xi[s], 16)

                    def evict(t, s, m):
                        for a in range(2):
                            act.wait_ge(s_tr, 2 * t + a + 1)
                            if a == 0:
                                wait(act, s_am, t - 1)
                            nc.scalar.activation(xT[:, s, :, a * P:(a + 1) * P],
                                                 psum[:, 2 * a:2 * a + 2].rearrange("p b (k n) -> p (b k) n", n=P),
                                                 ACT.Copy).then_inc(s_xT, 1)

                    def take_a(t, s, m):
                        act.wait_ge(s_am, t + 1)
                        nc.scalar.activation(aT[:, bass.ds(t, 1), :].rearrange("p a n -> p (a n)"),
                                             psum[0:2 * H, 4 + 2 * s, 0:2 * P], ACT.Copy).then_inc(s_ac, 1)

                    pipelined(act, NPAIR, [(0, load_x), (1, evict), (3, take_a)])
                    act.wait_ge(s_at, 1)
                    nc.scalar.activation(a_all[:], psum[:, 4, 0:NT * 2 * H].rearrange("p (t n) -> p t n", n=2 * H),
                                         ACT.Copy).then_inc(s_all, 1)

                @block.tensor
                def _(pe):
                    pe.wait_ge(s_ident, 2)

                    def transposes(t, s, m):
                        pe.wait_ge(s_xi[s], 16 * (m + 1))
                        for a in range(2):
                            wait(pe, s_xT, 2 * t + a - 1)
                            for k in range(KD):
                                last = nc.tensor.transpose(
                                    psum[:, 2 * a + k // 4, (k % 4) * P:(k % 4 + 1) * P],
                                    xin[:, s, a, k * P:(k + 1) * P], ident[:])
                            last.then_inc(s_tr, 1)

                    def products(t, s, m):
                        if isinstance(t, int) and t == 0:
                            pe.wait_ge(s_wa, 1)
                        if isinstance(t, int) and t == 1:
                            pe.wait_ge(s_lastw, 1)
                            nc.tensor.matmul(psum[0:TB, 5, 0:NC], ones[0:1, 0:TB], lastw[:], start=True, stop=True)\
                                .then_inc(s_bcast, 1)
                        pe.wait_ge(s_xT, 2 * t + 2)
                        wait(pe, s_ac, t - 1)
                        for k in range(KD):
                            last = nc.tensor.matmul(psum[0:2 * H, 4 + 2 * s, 0:2 * P], wa[:, k, :], xT[:, s, k, :],
                                                    start=(k == 0), stop=(k == KD - 1))
                        last.then_inc(s_am, 1)

                    pipelined(pe, NPAIR, [(1, transposes), (2, products)])
                    pe.wait_ge(s_ac, NPAIR)
                    for t in range(NT):
                        last = nc.tensor.transpose(psum[:, 4, t * 2 * H:(t + 1) * 2 * H],
                                                   aT[:, t // 2, (t % 2) * P:(t % 2 + 1) * P], ident[0:2 * H, 0:2 * H])
                    last.then_inc(s_at, 1)
                    pe.wait_ge(s_lw, 1)
                    for i, rows in enumerate((lrow, st, fv)):
                        for b in range(NB):
                            a = rows[:, b, 0, :] if rows is st else rows[:, b, :]
                            nc.tensor.transpose(psum[:, i, b * TB:(b + 1) * TB], a, ident[0:TB, 0:TB])
                    for i, v in enumerate((af, ab)):
                        for b in range(NB):
                            nc.tensor.transpose(psum[0:H, 6 + i, b * TB:(b + 1) * TB], v[:, b, :], ident[0:TB, 0:TB])
                    for b in range(NB):
                        last = nc.tensor.transpose(psum[0:1, 3, b * TB:(b + 1) * TB], dcl[:, b:b + 1], ident[0:TB, 0:TB])
                    last.then_inc(s_tp, 1)

                @block.vector
                def _(dve):
                    link = Chain(dve, s_dv)
                    dve.wait_ge(s_att, 32)
                    for k in range(KD):
                        dve.wait_ge(s_w[k >= W_FIRST], 16 * (KD - W_FIRST if k >= W_FIRST else W_FIRST))
                        for i, att in enumerate((atts, attd)):
                            for h in range(H):
                                n = (k * 2 + i) * H + h
                                last = nc.vector.tensor_tensor_reduce(
                                    out=junk[:, n % NJ, :], in0=w_sb[:, k, h * C:(h + 1) * C],
                                    in1=att[:, h * C:(h + 1) * C], scale=1.0, scalar=0.0, op0=ALU.mult, op1=ALU.add,
                                    accum_out=wa[:, k, i * H + h:i * H + h + 1])
                                if n % NJ == NJ - 1:
                                    link(last)
                    dve.wait_ge(s_iota, 9)
                    nc.vector.tensor_copy(mark0[:], pidx[:]).then_inc(s_wa, 1)
                    dve.wait_ge(s_lrow, 16)
                    link(nc.vector.tensor_copy(lastf[:], lasti[:]))
                    nc.vector.tensor_tensor(lastw[:], lastf[:], iotc[:], ALU.add).then_inc(s_lastw, 1)
                    dve.wait_ge(s_edges, 16 * N_EDGE_DMAS)
                    link(nc.vector.tensor_copy(dxf[:], dx[:]))
                    nc.vector.tensor_copy(ct[:, :, 0, :], sx[:])
                    nc.vector.tensor_copy(ct[:, :, 1, :], dxf[:, :, 1:P + 1])
                    nc.vector.tensor_tensor(ct[:, :, 2, :], dxf[:, :, 1:P + 1], dxf[:, :, 0:P], ALU.not_equal)
                    nc.vector.tensor_tensor(ct[:, :, 3, :], dxf[:, :, 1:P + 1], dxf[:, :, 2:P + 2], ALU.not_equal)\
                        .then_inc(s_ct, 1)
                    dve.wait_ge(s_bcast, 1)
                    for b in range(NB):
                        link(nc.vector.tensor_scalar(less[:], psum[0:TB, 5, 0:NC], step128[:, b:b + 1], None, ALU.is_lt))
                        link(nc.vector.reduce_sum(ci[:, b:b + 1], less[:], AX.X))
                    link(nc.vector.tensor_scalar_min(ci[:], ci[:], float(NC - 1)))
                    nc.vector.tensor_copy(cii[:], ci[:]).then_inc(s_ci, 1)
                    link(nc.vector.scalar_tensor_tensor(out=dneg[:], in0=ci[:], scalar=float(P), in1=step128[:],
                                                        op0=ALU.mult, op1=ALU.subtract))
                    link(nc.vector.tensor_scalar(di[:], dneg[:], -1.0 / P, None, ALU.mult))
                    link(nc.vector.tensor_scalar_min(dcl[:], di[:], float(NT - 1)))
                    dve.wait_ge(s_st, 16 * NB)
                    for b in range(NB):
                        nc.vector.tensor_scalar(lrow[:, b, :], st[:, b, 1, :], dneg[:, b:b + 1], None, ALU.add)
                    link(nc.vector.tensor_copy(mark1[:], pidx[:]))
                    link(nc.vector.tensor_scalar(val[:], lrow[:], 0.0, None, ALU.is_ge))
                    link(nc.vector.scalar_tensor_tensor(out=val[:], in0=lrow[:], scalar=float(P), in1=val[:],
                                                        op0=ALU.is_lt, op1=ALU.mult))
                    nc.vector.tensor_scalar(pen[:], val[:], BIG, -BIG, ALU.mult, ALU.add)
                    nc.vector.tensor_tensor(fv[:], st[:, :, 2, :], val[:], ALU.mult)
                    link(nc.vector.tensor_tensor(lv[:], st[:, :, 3, :], val[:], ALU.mult))
                    nc.vector.tensor_scalar(rs_f[:], fv[:], -BIG, None, ALU.mult)
                    link(nc.vector.tensor_scalar(rs_b[:], lv[:], -BIG, None, ALU.mult))
                    for h in range(H):
                        nc.vector.tensor_reduce(out=af[:, :, h], in_=rs_f[:], op=ALU.min, axis=AX.X)
                        last = nc.vector.tensor_reduce(out=ab[:, :, h], in_=rs_b[:], op=ALU.min, axis=AX.X)
                    last.then_inc(s_lw, 1)
                    dve.wait_ge(s_all, 1)
                    nc.vector.tensor_copy(nodes[:, :, 0:H], a_all[:, :, H:2 * H])
                    link(nc.vector.tensor_tensor(a_sum[:], a_all[:, :, 0:H], a_all[:, :, H:2 * H], ALU.add))
                    link(nc.vector.scalar_tensor_tensor(out=nodes[:, :, H:2 * H], in0=a_sum[:], scalar=SLOPE,
                                                        in1=a_sum[:], op0=ALU.mult, op1=ALU.max))
                    for i in range(PARTS):
                        link(nc.vector.tensor_copy(nt0[:, :, i, :], nodes[:]))
                        if i < PARTS - 1:
                            link(nc.vector.tensor_tensor(nodes[:], nodes[:], nt0[:, :, i, :], ALU.subtract))
                    dve.wait_ge(s_tp, 1)
                    nc.vector.tensor_copy(ldst[:], psum[:, 0, 0:T])
                    nc.vector.tensor_copy(isrc[:], psum[:, 1, 0:T])
                    nc.vector.tensor_copy(isfirst[:], psum[:, 2, 0:T])
                    nc.vector.tensor_copy(any_f[:], psum[0:H, 6, 0:T])
                    nc.vector.tensor_copy(any_b[:], psum[0:H, 7, 0:T])
                    nc.vector.tensor_copy(dtab[:], psum[0:1, 3, 0:T])

        with ExitStack() as ph:
            def sb(name, shape, dt=F32):
                return ph.enter_context(nc.sbuf_tensor(name, shape, dt))
            w_sb = sb("w0_sb2", [P, KD, D])
            xin = sb("xin2", [P, D])
            xT = sb("xT2", [P, KD, P])
            xp_st = sb("xp_st", [P, D])
            lt = sb("lt_bc", [P, 2, U, P])
            onehot_t = sb("onehot_t", [P, 2, U, P], BF16)
            at_dst = sb("at_dst", [P, 2, U, 2 * H])
            idx = sb("idx", [P, 4, U], I32)
            ga = sb("ga", [P, 4, U, H])
            esum = sb("esum", [P, 2, U, H])

            s_w = sem("p1_w")
            s_clr = sem("p1_clr")
            s_xi = sem("p1_x")
            s_tr = sem("p1_tr")
            s_xT = sem("p1_xT")
            s_xp = sem("p1_xp")
            s_xe = sem("p1_xe")
            s_xs = sem("p1_xs")
            s_lt = [sem(f"p1_lt{i}") for i in range(2)]
            s_ot = sem("p1_ot")
            s_pg = sem("p1_pg")
            s_ix = sem("p1_ix")
            s_ga = [sem(f"p1_ga{i}") for i in range(4)]
            s_es = sem("p1_es")
            s_lg = sem("p1_lg")

            def units(eng, body):
                body(0, True)
                with eng.Fori(1, NT) as u:
                    body(u, True)
                body(NT, False)

            with nc.Block() as block:
                @block.gpsimd
                def _(pool):
                    nc.gpsimd.memset(xin[:], 0.0).then_inc(s_clr, 1)
                    gather = PoolGather(pool, N, bound)

                    def unit(u, _):
                        for g in range(4):
                            g_all = 4 * u + g
                            gather.wait(s_ix, g_all + 1)
                            gather.wait(s_lg, g_all - 3)
                            for j in range(U):
                                gather.rows_of(ga[:, g, j, :], as_t, idx[:, g, j:j + 1]).then_inc(s_ga[g], 16)
                    units(pool, unit)

                @block.sync
                def _(sp):
                    for k in range(KD):
                        sp.dma_start(w_sb[:, k, :], w0[k * P:(k + 1) * P, :]).then_inc(s_w, 16)
                    sp.wait_ge(s_clr, 1)

                    def load_x(u, rows=P):
                        wait(sp, s_tr, u)
                        sp.dma_start(xin[0:rows, :], x[bass.ds(u * P, rows), :]).then_inc(s_xi, 16)

                    def unit(u, has_x, load=None):
                        if load == "last":
                            load_x(NT - 1, N_LAST)
                        elif load != "none":
                            load_x(u)
                        for g in range(4):
                            g_all = 4 * u + g
                            wait(sp, s_ot, g_all - 1)
                            sp.dma_start(lt[:, g % 2].rearrange("p j e -> p (j e)"),
                                         local_t[bass.ds(g_all * U, U), :].rearrange("j e -> (j e)").partition_broadcast(P))\
                              .then_inc(s_lt[g % 2], 16)
                            if g == 1 and not (isinstance(u, int) and u == 0):
                                sp.wait_ge(s_xe, u)
                                sp.dma_start(xp_t[bass.ds((u - 1) * P, P), :], xp_st[:]).then_inc(s_xs, 16)

                    unit(0, True)
                    with sp.Fori(1, NT - 1) as u:
                        unit(u, True)
                    unit(NT - 1, True, "last")
                    unit(NT, False, "none")
                    sp.wait_ge(s_xs, 16 * NT)

                @block.scalar
                def _(act):
                    def unit(u, has_x):
                        if has_x:
                            act.wait_ge(s_tr, u + 1)
                            nc.scalar.activation(xT[:].rearrange("p k n -> p (k n)"),
                                                 psum[:, 0:2].rearrange("p a b -> p (a b)"), ACT.Copy).then_inc(s_xT, 1)
                            act.wait_ge(s_xp, u + 1)
                            wait(act, s_xs, 16 * u)
                            nc.scalar.activation(xp_st[:], psum[:, 2:4].rearrange("p a b -> p (a b)"),
                                                 ACT.Copy).then_inc(s_xe, 1)
                    units(act, unit)

                @block.tensor
                def _(pe):
                    tiles = StepTiles(pe, dtab, "p1")
                    pe.wait_ge(s_w, 16 * KD)

                    def unit(u, has_x):
                        if has_x:
                            pe.wait_ge(s_xi, 16 * u + 16)
                            for k in range(KD):
                                last = nc.tensor.transpose(psum[:, k // 4, (k % 4) * P:(k % 4 + 1) * P],
                                                           xin[:, k * P:(k + 1) * P], ident[:])
                            last.then_inc(s_tr, 1)
                        for g in range(4):
                            g_all, s = 4 * u + g, g % 2
                            ds = tiles.load(g_all)
                            pe.wait_ge(s_ot, g_all + 1)
                            wait(pe, s_lg, g_all - 1)
                            for j in range(U):
                                last = nc.tensor.matmul(
                                    psum[:, 4 + s, j * PARTS * 2 * H:(j + 1) * PARTS * 2 * H], onehot_t[:, s, j, :],
                                    nt0[:, bass.ds(ds[j], 1)].rearrange("p a k n -> p (a k n)"), start=True, stop=True)
                            last.then_inc(s_pg, 1)
                            if has_x:
                                if g == 0:
                                    pe.wait_ge(s_xT, u + 1)
                                for k in range(2 * g, 2 * g + 2):
                                    for i in range(2):
                                        if g == 0 and k == 0 and i == 0:
                                            wait(pe, s_xe, u)
                                        last = nc.tensor.matmul(psum[:, 2 + i], xT[:, k, :],
                                                                w_sb[:, k, i * 512:(i + 1) * 512],
                                                                start=(k == 0), stop=(k == KD - 1))
                                if g == 3:
                                    last.then_inc(s_xp, 1)
                    units(pe, unit)

                @block.vector
                def _(dve):
                    def onehots(g, s, m):
                        dve.wait_ge(s_lt[s], 16 * m + 16)
                        wait(dve, s_pg, g - 1)
                        nc.vector.tensor_scalar(onehot_t[:, s].rearrange("p j e -> p (j e)"),
                                                lt[:, s].rearrange("p j e -> p (j e)"), pidx[:], None,
                                                ALU.is_equal).then_inc(s_ot, 1)

                    def logits(g, s, m):
                        u, slot = m
                        dve.wait_ge(s_pg, g + 1)
                        dve.wait_ge(s_ga[slot], 64 * u + 64)
                        pv = psum[:, 4 + s, 0:U * PARTS * 2 * H].rearrange("p (j k n) -> p j n k", k=PARTS, n=2 * H)
                        nc.vector.tensor_reduce(out=at_dst[:, s], in_=pv, op=ALU.add, axis=AX.X).then_inc(s_es, 1)
                        dve.wait_ge(s_es, 2 * g + 1)
                        nc.vector.tensor_tensor(esum[:, s], at_dst[:, s, :, 0:H], ga[:, slot], ALU.add).then_inc(s_es, 1)
                        nc.vector.tensor_copy(w9[:, bass.ds(g * U, U), H:2 * H], at_dst[:, s, :, H:2 * H])
                        dve.wait_ge(s_es, 2 * g + 2)
                        nc.vector.scalar_tensor_tensor(out=w9[:, bass.ds(g * U, U), 0:H], in0=esum[:, s], scalar=SLOPE,
                                                       in1=esum[:, s], op0=ALU.mult, op1=ALU.max).then_inc(s_lg, 1)

                    def indices(g, slot):
                        nc.vector.tensor_copy(idx[:, slot, :], isrc[:, bass.ds(g * U, U)]).then_inc(s_ix, 1)

                    def unit(u, _):
                        for g in range(4):
                            onehots(4 * u + g, g % 2, 2 * u + g // 2)
                            if not (isinstance(u, int) and 4 * u + g + 2 >= NG):
                                indices(4 * u + g + 2, (g + 2) % 4)
                            if g or not isinstance(u, int) or u:
                                gp = g - 1
                                logits(4 * u + gp, gp % 2, (u, gp) if g else (u - 1, 3))
                    for g in range(2):
                        indices(g, g)
                    units(dve, unit)
                    logits(NG - 1, 1, (NG // 4 - 1, 3))

        acc = keep("acc", [P, NT, D])
        zacc = keep("zacc", [P, NT, PARTS, W9])
        scan = ScanSems(sem)

        with ExitStack() as ph:
            def sb(name, shape, dt=F32):
                return ph.enter_context(nc.sbuf_tensor(name, shape, dt))
            rows = sb("rows0", [P, 2, U, D])
            idx = sb("idx2", [P, 2, U], I32)
            s_ix = sem("p2_ix")
            s_r = [sem(f"p2_r{i}") for i in range(2)]
            FIRST = 2

            def gather_first(pool):
                gather = PoolGather(pool, N, bound)
                for g in range(FIRST):
                    nc.gpsimd.tensor_copy(idx[:, g, :], isrc[:, g * U:(g + 1) * U]).then_inc(s_ix, 1)
                    pool.wait_ge(s_ix, g + 1)
                    for j in range(U):
                        gather.rows_of(rows[:, g, j, :], xp_t, idx[:, g, j:j + 1]).then_inc(s_r[g], 16)
            weigh_edges(nc, scan, "l0", psum, w9, ident, isfirst, rs_f, rs_b, pen, any_f, any_b, [acc[:], zacc[:]],
                        ("gpsimd", gather_first))

            onehot = sb("onehot0", [P, 2, U, P], BF16)
            parts = sb("parts", [P, 2, U, PARTS, W9], BF16)
            rest = sb("rest", [P, 2, U, W9])
            rest2 = sb("rest2", [P, 2, U, W9])
            wone = sb("wone", [P, 2, U, H, P])
            s_o = sem("p2_o")
            s_pd = sem("p2_pd")
            s_pa = sem("p2_pa")
            s_sp = sem("p2_split")
            s_mm = sem("p2_mm")
            s_acc = sem("p2_acc")
            with nc.Block() as block:
                @block.gpsimd
                def _(pool):
                    gather = PoolGather(pool, N, bound)

                    def group(g, s, m):
                        if not isinstance(g, int) or g >= FIRST:
                            gather.wait(s_r[s], 64 * m)
                            nc.gpsimd.tensor_copy(idx[:, s, :], isrc[:, bass.ds(g * U, U)]).then_inc(s_ix, 1)
                            gather.wait(s_ix, g + 1)
                            for j in range(U):
                                gather.wait(s_mm, (g - 2) * U + j + 1)
                                gather.rows_of(rows[:, s, j, :], xp_t, idx[:, s, j:j + 1]).then_inc(s_r[s], 16)
                        weights = w9[:, bass.ds(g * U, U), :]
                        link = g * 4
                        nc.gpsimd.tensor_copy(parts[:, s, :, 0, :], weights).then_inc(s_sp, 1)
                        gather.wait(s_sp, link + 1)
                        nc.gpsimd.tensor_tensor(rest[:, s], weights, parts[:, s, :, 0, :], ALU.subtract).then_inc(s_sp, 1)
                        gather.wait(s_sp, link + 2)
                        nc.gpsimd.tensor_copy(parts[:, s, :, 1, :], rest[:, s]).then_inc(s_sp, 1)
                        gather.wait(s_sp, link + 3)
                        nc.gpsimd.tensor_tensor(rest2[:, s], rest[:, s], parts[:, s, :, 1, :], ALU.subtract)\
                          .then_inc(s_sp, 1)
                        gather.wait(s_sp, link + 4)
                        nc.gpsimd.tensor_copy(parts[:, s, :, 2, :], rest2[:, s]).then_inc(s_pd, 1)
                    pipelined(pool, NG, [(0, group)], unroll=2)

                @block.scalar
                def _(act):
                    def weights(g, s, m):
                        act.wait_ge(s_o, g + 1)
                        for j in range(U):
                            wait(act, s_mm, (g - 2) * U + j + 1)
                            for h in range(H):
                                last = nc.scalar.activation(wone[:, s, j, h, :], onehot[:, s, j, :], ACT.Copy,
                                                            scale=w9[:, bass.ds(g * U + j, 1), h:h + 1].rearrange("p a b -> p (a b)"))
                            last.then_inc(s_pa, 1)
                    pipelined(act, NG, [(0, weights)], unroll=2)

                @block.tensor
                def _(pe):
                    def group(g, s, m):
                        for j in range(U):
                            i = g * U + j
                            if j == 0:
                                pe.wait_ge(s_r[s], 64 * m + 64)
                                pe.wait_ge(s_pd, g + 1)
                            pe.wait_ge(s_pa, i + 1)
                            wait(pe, s_acc, i - 1)
                            for h in range(H):
                                nc.tensor.matmul(psum[:, 2 * (j % 2) + h // 2, (h % 2) * C:(h % 2 + 1) * C],
                                                 wone[:, s, j, h, :], rows[:, s, j, h * C:(h + 1) * C],
                                                 start=True, stop=True)
                            nc.tensor.matmul(psum[:, 4 + j % 2, 0:PARTS * W9], onehot[:, s, j, :],
                                             parts[:, s, j].rearrange("p k n -> p (k n)"), start=True, stop=True)\
                              .then_inc(s_mm, 1)
                    pipelined(pe, NG, [(0, group)], unroll=2)

                @block.vector
                def _(dve):
                    tiles = StepTiles(dve, dtab, "p2")

                    def group(g, s, m, build=True, add=True):
                        if add:
                            ds = tiles.load(g - 1)
                        for j in range(U):
                            if add:
                                i = (g - 1) * U + j
                                dve.wait_ge(s_mm, i + 1)
                                wait(dve, s_acc, i)
                                av = acc[:, bass.ds(ds[j], 1), :].rearrange("p a n -> p (a n)")
                                zv = zacc[:, bass.ds(ds[j], 1)].rearrange("p a k n -> p (a k n)")
                                nc.vector.tensor_tensor(zv, psum[:, 4 + j % 2, 0:PARTS * W9], zv, ALU.add)
                                nc.vector.tensor_tensor(av, psum[:, 2 * (j % 2):2 * (j % 2) + 2].rearrange("p a b -> p (a b)"),
                                                        av, ALU.add).then_inc(s_acc, 1)
                            if build and j == 0:
                                wait(dve, s_mm, (g - 1) * U)
                                wait(dve, s_pa, (g - 1) * U)
                                nc.vector.tensor_tensor(
                                    onehot[:, s], bc(iotar[:].unsqueeze(1), [P, U, P]),
                                    bc(ldst[:, bass.ds(g * U, U)].unsqueeze(2), [P, U, P]), ALU.is_equal).then_inc(s_o, 1)
                    pipelined(dve, NG, [(0, lambda g, s, m: group(g, s, m, True, not (isinstance(g, int) and g == 0)))], unroll=2)
                    group(NG, 0, NG // 2, False, True)

        xr = acc[:, :, 0:XRW]
        acc1 = acc[:, :, 2 * C:2 * C + ACC1]
        acc1_odd = acc[:, :, 0:ACC1]
        with ExitStack() as ph:
            def sb(name, shape, dt=F32):
                return ph.enter_context(nc.sbuf_tensor(name, shape, dt))
            wd = sb("wd", [P, KD, HID])
            rmsw = sb("rmsw", [P, KD])
            wlr = sb("wlr", [P, KH, 2 * HID + 2 * H])
            bias_bc = sb("bias_bc", [P, D])
            att_bc = sb("att_bc", [P, HID])
            noself = sb("noself", [P, NT])
            wself = sb("wself", [P, NT, H])
            rz = sb("rz", [P, NT, H])
            sw = sb("sw", [P, NT, H])
            eps = sb("eps", [P, 2])
            xpt = sb("xpt", [P, 2, D])
            xin = sb("xin5", [P, 2, D])
            g0 = sb("g0", [P, 2, D])
            y = sb("y", [P, 2, D])
            sq = sb("sq", [P, D])
            xT = sb("xT5", [P, 2, KD, P])
            st = sb("st5", [P, 2, 12])
            mv = sb("mv", [P, 2, 2])
            mark = sb("mark5", [P, 1])
            sd = sb("sd", [P, 2])
            rs = sb("rs", [P, 2, 2])
            ss = sb("ss", [P, 2])
            sr = sb("sr", [P, 2])
            rr = sb("rr", [P, 2])
            hd = sb("hd", [P, 2, HID])
            hT = sb("hT", [P, 2, KH, P])
            xls = sb("xls", [P, 2, XRW])
            tmp2 = sb("tmp52", [P, HID])
            relu_part = sb("relu_part", [P, H])
            both = sb("both", [P, H])
            att_lin = sb("att_lin", [P, HID])
            att_relu = sb("att_relu", [P, HID])
            names = "ldw clr z wd y0 pb B mv sd D rs x1 E sr rr tr xT hp hd ht hT lr xlr sf att".split()
            S = {n: sem("n_" + n) for n in names}
            s_ld = [sem(f"n_ld{i}") for i in range(2)]
            s_x1s = [sem(f"n_x1s{i}") for i in range(2)]
            s_xls = [sem(f"n_xls{i}") for i in range(2)]
            N_LDW = 4 + KH * 2
            AHEAD = 8
            with nc.Block() as block:
                @block.gpsimd
                def _(pool):
                    nc.gpsimd.memset(xin[:], 0.0).then_inc(S["clr"], 1)
                    nc.gpsimd.memset(eps[:, 0:1], LN_EPS).then_inc(S["clr"], 1)
                    nc.gpsimd.memset(eps[:, 1:2], RMS_EPS).then_inc(S["clr"], 1)
                    pool.wait_ge(S["ldw"], 16 * N_LDW)

                    def add_bias(t, s, m):
                        pool.wait_ge(S["y0"], t + 1)
                        nc.gpsimd.tensor_tensor(g0[:, s], g0[:, s], bias_bc[:], ALU.add).then_inc(S["pb"], 1)
                    pipelined(pool, NT, [(1, add_bias)], AHEAD, unroll=2)

                @block.sync
                def _(sp):
                    with nc.allow_non_contiguous_dma(reason="rms weights by rows of W_down, once"):
                        sp.dma_start(rmsw[:], rms_w.rearrange("(k p) -> p k", p=P)).then_inc(S["ldw"], 16)
                    sp.dma_start(wd[:], w_down.rearrange("(k p) n -> p k n", p=P)).then_inc(S["ldw"], 16)
                    sp.dma_start(bias_bc[:], bias.partition_broadcast(P)).then_inc(S["ldw"], 16)
                    sp.dma_start(att_bc[:], att1.rearrange("h c -> (h c)").partition_broadcast(P)).then_inc(S["ldw"], 16)
                    for k in range(KH):
                        sp.dma_start(wlr[:, k, 0:HID], wl[k * P:(k + 1) * P, :]).then_inc(S["ldw"], 16)
                        sp.dma_start(wlr[:, k, XRW:XRW + HID], wr[k * P:(k + 1) * P, :]).then_inc(S["ldw"], 16)
                    sp.wait_ge(S["clr"], 1)

                    def load(t, s, m):
                        wait(sp, S["mv"], t - 1)
                        rows = N_LAST if isinstance(t, int) and t == NT - 1 else P
                        sp.dma_start(xpt[:, s, :], xp_t[bass.ds(t * P, P), :]).then_inc(s_ld[s], 16)
                        sp.dma_start(xin[0:rows, s, :], x[bass.ds(t * P, rows), :]).then_inc(s_ld[s], 16)

                    def store_x1(t, s, m):
                        sp.wait_ge(S["x1"], t + 1)
                        sp.dma_start(x1_t[bass.ds(t * P, P), :], y[:, s, :]).then_inc(s_x1s[s], 16)

                    def store_xl(t, s, m):
                        sp.wait_ge(S["sf"], t + 1)
                        sp.dma_start(xl_t[bass.ds(t * P, P), :], xls[:, s, 0:XLW]).then_inc(s_xls[s], 16)
                    pipelined(sp, NT, [(1, load), (3, store_x1), (6, store_xl)], AHEAD, unroll=2)
                    for s in range(2):
                        sp.wait_ge(s_x1s[s], 16 * ((NT + 1 - s) // 2))
                        sp.wait_ge(s_xls[s], 16 * ((NT + 1 - s) // 2))

                @block.scalar
                def _(act):
                    act.wait_ge(S["z"], 1)
                    act.wait_ge(S["clr"], 3)

                    def divide(t, s, m):
                        wait(act, S["mv"], t - 1)
                        for h in range(H):
                            last = nc.scalar.activation(
                                g0[:, s, h * C:(h + 1) * C],
                                acc[:, bass.ds(t, 1), h * C:(h + 1) * C].rearrange("p a n -> p (a n)"), ACT.Copy,
                                scale=rz[:, bass.ds(t, 1), h:h + 1].rearrange("p a n -> p (a n)"))
                        last.then_inc(S["y0"], 1)

                    def deviation(t, s, m):
                        act.wait_ge(S["mv"], t + 1)
                        nc.scalar.activation(sd[:, s:s + 1], mv[:, s, 1:2], ACT.Sqrt, bias=eps[:, 0:1]).then_inc(S["sd"], 1)

                    def normalise(t, s, m):
                        act.wait_ge(S["rs"], t + 1)
                        nc.scalar.activation(y[:, s, :], y[:, s, :], ACT.Identity, bias=rs[:, s, 1:2],
                                             scale=rs[:, s, 0:1]).then_inc(S["x1"], 1)
                        act.wait_ge(S["x1"], t + 1)
                        wait(act, S["E"], t)
                        nc.scalar.activation(sq[:], y[:, s, :], ACT.Square, accum_out=ss[:, s:s + 1]).then_inc(S["E"], 1)
                        act.wait_ge(S["E"], t + 1)
                        nc.scalar.activation(sr[:, s:s + 1], ss[:, s:s + 1], ACT.Sqrt, bias=eps[:, 1:2],
                                             scale=1.0 / D).then_inc(S["sr"], 1)

                    def take_xT(t, s, m):
                        act.wait_ge(S["tr"], t + 1)
                        wait(act, S["hp"], t - 1)
                        nc.scalar.activation(xT[:, s].rearrange("p k n -> p (k n)"),
                                             psum[:, 2 * s:2 * s + 2].rearrange("p a b -> p (a b)"),
                                             ACT.Copy).then_inc(S["xT"], 1)

                    def take_hT(t, s, m):
                        act.wait_ge(S["ht"], t + 1)
                        wait(act, S["lr"], t - 1)
                        nc.scalar.activation(hT[:, s].rearrange("p k n -> p (k n)"), psum[:, 5, 0:HID],
                                             ACT.Copy).then_inc(S["hT"], 1)

                    def take_xlr(t, s, m):
                        act.wait_ge(S["lr"], t + 1)
                        wait(act, S["sf"], t - 1)
                        wait(act, s_xls[s], 16 * m)
                        nc.scalar.activation(xls[:, s, :], psum[:, 6, 0:XRW], ACT.Copy).then_inc(S["xlr"], 1)
                        nc.scalar.activation(xr[:, bass.ds(t, 1), 0:HID].rearrange("p a n -> p (a n)"),
                                             psum[:, 7, 0:HID], ACT.Copy).then_inc(S["xlr"], 1)
                    pipelined(act, NT, [(5, take_hT), (6, take_xlr), (3, normalise), (3, take_xT), (2, deviation),
                                        (0, divide)], AHEAD, unroll=2)

                @block.tensor
                def _(pe):
                    pe.wait_ge(S["wd"], 1)

                    def transposes(t, s, m):
                        pe.wait_ge(S["x1"], t + 1)
                        wait(pe, S["xT"], t - 1)
                        for k in range(KD):
                            last = nc.tensor.transpose(psum[:, 2 * s + k // 4, (k % 4) * P:(k % 4 + 1) * P],
                                                       y[:, s, k * P:(k + 1) * P], ident[:])
                        last.then_inc(S["tr"], 1)

                    def down(t, s, m):
                        pe.wait_ge(S["xT"], t + 1)
                        wait(pe, S["hd"], t)
                        for k in range(KD):
                            last = nc.tensor.matmul(psum[:, 4, 0:HID], xT[:, s, k, :], wd[:, k, :],
                                                    start=(k == 0), stop=(k == KD - 1))
                        last.then_inc(S["hp"], 1)

                    def transposes_h(t, s, m):
                        pe.wait_ge(S["hd"], t + 1)
                        wait(pe, S["hT"], t)
                        for k in range(KH):
                            last = nc.tensor.transpose(psum[:, 5, k * P:(k + 1) * P], hd[:, s, k * P:(k + 1) * P], ident[:])
                        last.then_inc(S["ht"], 1)

                    def left_right(t, s, m):
                        pe.wait_ge(S["hT"], t + 1)
                        if isinstance(t, int) and t == 0:
                            pe.wait_ge(S["wd"], 2)
                        wait(pe, S["xlr"], 2 * t)
                        for k in range(KH):
                            nc.tensor.matmul(psum[:, 6, 0:XRW], hT[:, s, k, :], wlr[:, k, 0:XRW],
                                             start=(k == 0), stop=(k == KH - 1))
                            last = nc.tensor.matmul(psum[:, 7, 0:HID], hT[:, s, k, :], wlr[:, k, XRW:XRW + HID],
                                                    start=(k == 0), stop=(k == KH - 1))
                        last.then_inc(S["lr"], 1)
                    pipelined(pe, NT, [(5, transposes_h), (4, down), (3, transposes), (5, left_right)], AHEAD, unroll=2)

                @block.vector
                def _(dve):
                    sums = Chain(dve, sem("n_zc"))
                    for k in range(1, PARTS):
                        sums(nc.vector.tensor_tensor(zacc[:, :, 0, :], zacc[:, :, 0, :], zacc[:, :, k, :], ALU.add))
                    divisor(nc, sums, zacc[:, :, 0, :], noself, wself, rz, sw, 0.0).then_inc(S["z"], 1)
                    dve.wait_ge(S["ldw"], 16 * N_LDW)
                    for k in range(KD):
                        last = nc.vector.tensor_scalar(wd[:, k, :], wd[:, k, :], rmsw[:, k:k + 1], None, ALU.mult)
                    last.then_inc(S["wd"], 1)
                    nc.vector.tensor_scalar(att_lin[:], att_bc[:], SLOPE, None, ALU.mult)
                    nc.vector.tensor_scalar(att_relu[:], att_bc[:], 1.0 - SLOPE, None, ALU.mult).then_inc(S["att"], 1)
                    dve.wait_ge(S["att"], 1)
                    for k in range(KH):
                        for i in range(2):
                            for h in range(H):
                                n = (k * 2 + i) * H + h
                                w_cols = i * XRW + h * HD
                                last = nc.vector.tensor_tensor_reduce(
                                    out=sq[:, n * HD:(n + 1) * HD], in0=wlr[:, k, w_cols:w_cols + HD],
                                    in1=att_lin[:, h * HD:(h + 1) * HD], scale=1.0, scalar=0.0, op0=ALU.mult,
                                    op1=ALU.add, accum_out=wlr[:, k, HID + i * H + h:HID + i * H + h + 1])
                    last.then_inc(S["wd"], 1)
                    linkB = Chain(dve, S["B"], 3)
                    linkD = Chain(dve, S["D"], 1)

                    def combine(t, s, m):
                        linkB.tile(t)
                        wait(dve, S["tr"], t - 1)
                        wait(dve, s_x1s[s], 16 * m)
                        dve.wait_ge(S["pb"], t + 1)
                        dve.wait_ge(s_ld[s], 32 * m + 32)
                        for h in range(H):
                            cols = slice(h * C, (h + 1) * C)
                            last = nc.vector.scalar_tensor_tensor(
                                out=y[:, s, cols], in0=xpt[:, s, cols],
                                scalar=sw[:, bass.ds(t, 1), h:h + 1].rearrange("p a n -> p (a n)"),
                                in1=g0[:, s, cols], op0=ALU.mult, op1=ALU.add)
                        linkB(last)
                        linkB(nc.vector.scalar_tensor_tensor(out=y[:, s], in0=y[:, s], scalar=0.0, in1=xin[:, s],
                                                             op0=ALU.max, op1=ALU.add))
                        for i in range(2):
                            last = nc.vector.bn_stats(st[:, s, 6 * i:6 * i + 6], y[:, s, i * 512:(i + 1) * 512])
                        linkB(last)
                        nc.vector.tensor_copy(mark[:], st[:, s, 0:1])
                        nc.vector.bn_aggr(mv[:, s, :], st[:, s, :]).then_inc(S["mv"], 1)

                    def factors(t, s, m):
                        linkD.tile(t)
                        dve.wait_ge(S["sd"], t + 1)
                        linkD(nc.vector.reciprocal(rs[:, s, 0:1], sd[:, s:s + 1]))
                        nc.vector.tensor_scalar(rs[:, s, 1:2], mv[:, s, 0:1], rs[:, s, 0:1], -1.0, ALU.mult, ALU.mult)\
                            .then_inc(S["rs"], 1)

                    def rms(t, s, m):
                        dve.wait_ge(S["sr"], t + 1)
                        nc.vector.reciprocal(rr[:, s:s + 1], sr[:, s:s + 1]).then_inc(S["rr"], 1)

                    def scale_h(t, s, m):
                        dve.wait_ge(S["hp"], t + 1)
                        dve.wait_ge(S["rr"], t + 1)
                        wait(dve, S["ht"], t - 1)
                        nc.vector.tensor_scalar(hd[:, s, :], psum[:, 4, 0:HID], rr[:, s:s + 1], None, ALU.mult)\
                            .then_inc(S["hd"], 1)

                    linkS = Chain(dve, sem("n_sfc"), 3)

                    def self_logit(t, s, m):
                        linkS.tile(t)
                        xrt = xr[:, bass.ds(t, 1), :].rearrange("p a n -> p (a n)")
                        dve.wait_ge(S["xlr"], 2 * t + 2)
                        wait(dve, S["sf"], t)
                        nc.vector.tensor_copy(xrt[:, HID:XLW], xls[:, s, XLW:XRW])
                        linkS(nc.vector.tensor_tensor(tmp2[:], xls[:, s, 0:HID], xrt[:, 0:HID], ALU.add))
                        nc.vector.tensor_tensor(both[:], xls[:, s, HID:XLW], xls[:, s, XLW:XRW], ALU.add)
                        linkS(nc.vector.scalar_tensor_tensor(out=tmp2[:], in0=tmp2[:], scalar=0.0, in1=att_relu[:],
                                                             op0=ALU.max, op1=ALU.mult))
                        linkS(nc.vector.tensor_reduce(out=relu_part[:], in_=tmp2[:].rearrange("p (h c) -> p h c", h=H),
                                                      op=ALU.add, axis=AX.X))
                        nc.vector.tensor_tensor(xrt[:, XLW:XRW], relu_part[:], both[:], ALU.add).then_inc(S["sf"], 1)
                    pipelined(dve, NT, [(3, factors), (2, combine), (4, scale_h), (6, self_logit), (3, rms)], AHEAD, unroll=2)

        with ExitStack() as ph:
            def sb(name, shape, dt=F32):
                return ph.enter_context(nc.sbuf_tensor(name, shape, dt))
            att_bc = sb("att_bc6", [P, HID])
            RING = 4
            lt = sb("lt6", [P, 2, U, P])
            onehot_t = sb("onehot_t6", [P, 2, U, P])
            rows = sb("rows6", [P, RING, U, XLW])
            msg = sb("msg6", [P, 2, U, XLW])
            prod = sb("prod6", [P, 2, U, HID])
            part = sb("part6", [P, 2, U, H])
            att_relu = sb("att_relu6", [P, HID])
            idx = sb("idx6", [P, RING, U], I32)
            s_att = sem("q_att")
            s_lt = [sem(f"q_lt{i}") for i in range(2)]
            s_r = [sem(f"q_r{i}") for i in range(RING)]
            s_xe = [sem(f"q_xe{i}") for i in range(RING)]
            s_ix, s_ot, s_pg, s_ad, s_pr, s_sc, s_pd, s_pt, s_rd = (sem("q_" + n) for n in
                                                              "ix ot pg ad pr sc pd pt rd".split())
            with nc.Block() as block:
                @block.gpsimd
                def _(pool):
                    gather = PoolGather(pool, N, bound)

                    def group(g, s, m):
                        gather.wait(s_ix, g + 1)
                        gather.wait(s_ad, g - RING + 1)
                        gather.wait(s_xe[s], 16 * m)
                        for j in range(U):
                            gather.rows_of(rows[:, s, j, :], xl_t, idx[:, s, j:j + 1]).then_inc(s_r[s], 16)
                    pipelined(pool, NG, [(0, group)], RING, RING, 2)

                @block.sync
                def _(sp):
                    sp.dma_start(att_bc[:], att1.rearrange("h c -> (h c)").partition_broadcast(P)).then_inc(s_att, 16)

                    def load(g, s, m):
                        wait(sp, s_ot, g - 1)
                        s = s % 2
                        sp.dma_start(lt[:, s].rearrange("p j e -> p (j e)"),
                                     local_t[bass.ds(g * U, U), :].rearrange("j e -> (j e)").partition_broadcast(P))\
                          .then_inc(s_lt[s], 16)

                    def store_rows(g, s, m):
                        sp.wait_ge(s_r[s], 64 * m + 64)
                        sp.dma_start(xe_t[bass.ds(g, 1)].rearrange("a p n -> p (a n)"),
                                     rows[:, s].rearrange("p j n -> p (j n)")).then_inc(s_xe[s], 16)
                    pipelined(sp, NG, [(1, store_rows), (0, load)], RING, RING)
                    for s in range(RING):
                        sp.wait_ge(s_xe[s], 16 * NG // RING)

                @block.scalar
                def _(act):
                    def indices(g, s, m):
                        wait(act, s_r[s], 64 * m)
                        nc.scalar.activation(idx[:, s, :], isrc[:, bass.ds(g * U, U)], ACT.Copy).then_inc(s_ix, 1)

                    def self_logits(g, s, m):
                        s = s % 2
                        act.wait_ge(s_ad, g + 1)
                        nc.scalar.activation(w9[:, bass.ds(g * U, U), H:2 * H], psum[:, 4 * s:4 * s + 4, XLW:XRW],
                                             ACT.Copy).then_inc(s_sc, 1)
                    pipelined(act, NG, [(0, indices), (3, self_logits)], RING, RING, 2)

                @block.tensor
                def _(pe):
                    tiles = StepTiles(pe, dtab, "q1")

                    def group(g, s, m):
                        ds = tiles.load(g)
                        pe.wait_ge(s_ot, g + 1)
                        wait(pe, s_sc, g - 1)
                        for j in range(U):
                            last = nc.tensor.matmul(psum[:, 4 * s + j, 0:XRW], onehot_t[:, s, j, :],
                                                    xr[:, bass.ds(ds[j], 1), :], start=True, stop=True)
                        last.then_inc(s_pg, 1)
                    pipelined(pe, NG, [(0, group)])

                @block.vector
                def _(dve):
                    dve.wait_ge(s_att, 16)
                    nc.vector.tensor_scalar(att_relu[:], att_bc[:], 1.0 - SLOPE, None, ALU.mult).then_inc(s_pr, 1)
                    dve.wait_ge(s_pr, 1)

                    def onehots(g, s, m):
                        s2, m2 = s % 2, (RING // 2) * m + s // 2
                        dve.wait_ge(s_lt[s2], 16 * m2 + 16)
                        wait(dve, s_pg, g - 1)
                        nc.vector.tensor_scalar(onehot_t[:, s2].rearrange("p j e -> p (j e)"),
                                                lt[:, s2].rearrange("p j e -> p (j e)"), pidx[:], None,
                                                ALU.is_equal).then_inc(s_ot, 1)

                    def add(g, s, m):
                        dve.wait_ge(s_pg, g + 1)
                        dve.wait_ge(s_r[s], 64 * m + 64)
                        wait(dve, s_rd, g - 1)
                        s2 = s % 2
                        nc.vector.tensor_tensor(msg[:, s2], psum[:, 4 * s2:4 * s2 + 4, 0:XLW], rows[:, s], ALU.add)\
                            .then_inc(s_ad, 1)

                    def reduce(g, s, m):
                        s = s % 2
                        dve.wait_ge(s_ad, g + 1)
                        wait(dve, s_rd, g - 1)
                        nc.vector.scalar_tensor_tensor(out=prod[:, s], in0=msg[:, s, :, 0:HID], scalar=0.0,
                                                       in1=bc(att_relu[:].unsqueeze(1), [P, U, HID]),
                                                       op0=ALU.max, op1=ALU.mult).then_inc(s_pd, 1)
                        dve.wait_ge(s_pd, g + 1)
                        nc.vector.tensor_reduce(out=part[:, s], in_=prod[:, s].rearrange("p j (h c) -> p j h c", h=H),
                                                op=ALU.add, axis=AX.X).then_inc(s_pt, 1)
                        dve.wait_ge(s_pt, g + 1)
                        nc.vector.tensor_tensor(w9[:, bass.ds(g * U, U), 0:H], part[:, s], msg[:, s, :, HID:XLW],
                                                ALU.add).then_inc(s_rd, 1)
                    pipelined(dve, NG, [(0, onehots), (1, add), (2, reduce)], RING, RING, 2)

        with ExitStack() as ph:
            def sb(name, shape, dt=F32):
                return ph.enter_context(nc.sbuf_tensor(name, shape, dt))
            U2 = 2 * U
            NG2 = T // U2
            rows = sb("rows8", [P, 2, U2, XLW])
            s_r = [sem(f"r_r{i}") for i in range(2)]

            def load_rows(sp, g, s):
                sp.dma_start(rows[:, s].rearrange("p (a j) n -> p a (j n)", a=2),
                             xe_t.rearrange("(g a) p n -> g a p n", a=2)[bass.ds(g, 1)]
                             .rearrange("g a p n -> p (g a) n")).then_inc(s_r[s], 16)
            FIRST = 2
            weigh_edges(nc, scan, "l1", psum, w9, ident, isfirst, rs_f, rs_b, pen, any_f, any_b, [acc1, acc1_odd],
                        ("sync", lambda sp: [load_rows(sp, g, g) for g in range(FIRST)]))

            onehot = sb("onehot8", [P, 2, U2, P])
            msg = sb("msg8", [P, 2, U2, ACC1])
            s_o, s_mp, s_ma, s_mm, s_acc = (sem("r_" + n) for n in "o mp ma mm acc".split())
            with nc.Block() as block:
                @block.sync
                def _(sp):
                    def load(g, s, m):
                        if isinstance(g, int) and g < FIRST:
                            return
                        wait(sp, s_ma, (g - 1) * U2)
                        wait(sp, s_mp, g - 1)
                        load_rows(sp, g, s)
                    pipelined(sp, NG2, [(0, load)], unroll=2)

                @block.gpsimd
                def _(pool):
                    waits = PoolGather(pool, N, bound)

                    def weigh(g, s, m):
                        waits.wait(s_mm, (g - 1) * U2)
                        waits.wait(s_r[s], 16 * m + 16)
                        nc.gpsimd.tensor_tensor(
                            msg[:, s, :, 0:POOL_HEADS * HD].rearrange("p j (h c) -> p j h c", c=HD),
                            rows[:, s, :, 0:POOL_HEADS * HD].rearrange("p j (h c) -> p j h c", c=HD),
                            bc(w9[:, bass.ds(g * U2, U2), 0:POOL_HEADS].unsqueeze(3), [P, U2, POOL_HEADS, HD]),
                            ALU.mult).then_inc(s_mp, 1)
                    pipelined(pool, NG2, [(0, weigh)], unroll=2)

                @block.scalar
                def _(act):
                    def weights(g, s, m):
                        wait(act, s_mm, (g - 1) * U2)
                        nc.scalar.activation(msg[:, s, :, HID:ACC1], w9[:, bass.ds(g * U2, U2), :], ACT.Copy)
                        act.wait_ge(s_r[s], 16 * m + 16)
                        for j in range(U2):
                            for h in range(POOL_HEADS, H):
                                cols = slice(h * HD, (h + 1) * HD)
                                last = nc.scalar.activation(
                                    msg[:, s, j, cols], rows[:, s, j, cols], ACT.Copy,
                                    scale=w9[:, bass.ds(g * U2 + j, 1), h:h + 1].rearrange("p a b -> p (a b)"))
                            last.then_inc(s_ma, 1)
                    pipelined(act, NG2, [(0, weights)], unroll=2)

                @block.tensor
                def _(pe):
                    def group(g, s, m):
                        pe.wait_ge(s_o, g + 1)
                        pe.wait_ge(s_mp, g + 1)
                        for j in range(U2):
                            pe.wait_ge(s_ma, g * U2 + j + 1)
                            wait(pe, s_acc, g * U2 + j - 7)
                            nc.tensor.matmul(psum[:, j, 0:ACC1], onehot[:, s, j, :], msg[:, s, j, :],
                                             start=True, stop=True).then_inc(s_mm, 1)
                    pipelined(pe, NG2, [(0, group)], unroll=2)

                @block.vector
                def _(dve):
                    tiles = StepTiles(dve, dtab, "r1", U2)

                    def build(g, s, m):
                        wait(dve, s_mm, (g - 1) * U2)
                        nc.vector.tensor_tensor(
                            onehot[:, s], bc(iotar[:].unsqueeze(1), [P, U2, P]),
                            bc(ldst[:, bass.ds(g * U2, U2)].unsqueeze(2), [P, U2, P]), ALU.is_equal).then_inc(s_o, 1)

                    def add(g, s, m):
                        ds = tiles.load(g)
                        for j in range(U2):
                            i = g * U2 + j
                            dve.wait_ge(s_mm, i + 1)
                            wait(dve, s_acc, i - 1)
                            sums = acc1_odd if j % 2 else acc1
                            av = sums[:, bass.ds(ds[j], 1), :].rearrange("p a n -> p (a n)")
                            nc.vector.tensor_tensor(av, psum[:, j, 0:ACC1], av, ALU.add).then_inc(s_acc, 1)
                    pipelined(dve, NG2, [(0, build), (1, add)], unroll=2)
                    dve.wait_ge(s_acc, T)
                    nc.vector.tensor_tensor(acc1, acc1, acc1_odd, ALU.add)

        with ExitStack() as ph:
            def sb(name, shape, dt=F32):
                return ph.enter_context(nc.sbuf_tensor(name, shape, dt))
            wu = sb("wu", [P, KH, D])
            noself = sb("noself9", [P, NT])
            wself = sb("wself9", [P, NT, H])
            rz = sb("rz9", [P, NT, H])
            sw = sb("sw9", [P, NT, H])
            eps = sb("eps9", [P, 1])
            XL1 = 3
            SELF_PIECES = ((0, XL1), (XL1, 8), (8, 16), (16, NT))
            xl_in = sb("xl_in", [P, NT, HID])
            x1_in = sb("x1_in", [P, 2, D])
            gsum = sb("gsum", [P, 2, HID])
            gT = sb("gT", [P, 2, KH, P])
            y = sb("y9", [P, 2, D])
            o = sb("o9", [P, 2, D])
            st = sb("st9", [P, 2, 12])
            mv = sb("mv9", [P, 2, 2])
            mark = sb("mark9", [P, 1])
            sd = sb("sd9", [P, 2])
            rs = sb("rs9", [P, 2, 2])
            F = {n: sem("f_" + n) for n in "w z eps g0 g tr gT up s mv sd D rs o".split()}
            s_xl = [sem(f"f_xl{i}") for i in range(2)]
            s_x1 = [sem(f"f_x1{i}") for i in range(2)]
            s_out = [sem(f"f_out{i}") for i in range(2)]
            AHEAD = 8
            with nc.Block() as block:
                @block.sync
                def _(sp):
                    sp.dma_start(wu[:], w_up.rearrange("(k p) n -> p k n", p=P)).then_inc(F["w"], 16)

                    for i, (t0, t1) in enumerate(((0, XL1), (XL1, NT))):
                        sp.dma_start(xl_in[:, t0:t1, :], xl_t[t0 * P:t1 * P, 0:HID].rearrange("(t p) n -> p t n", p=P))\
                          .then_inc(s_xl[i], 16)

                    def load_x1(t, s, m):
                        wait(sp, F["s"], 2 * t - 2)
                        sp.dma_start(x1_in[:, s, :], x1_t[bass.ds(t * P, P), :]).then_inc(s_x1[s], 16)

                    def store(t, s, m):
                        sp.wait_ge(F["o"], t + 1)
                        rows = N_LAST if isinstance(t, int) and t == NT - 1 else P
                        sp.dma_start(out[bass.ds(t * P, rows), :], o[0:rows, s, :]).then_inc(s_out[s], 16)
                    pipelined(sp, NT, [(4, load_x1), (7, store)], AHEAD, unroll=2)
                    for s in range(2):
                        sp.wait_ge(s_out[s], 16 * ((NT + 1 - s) // 2))

                @block.gpsimd
                def _(pool):
                    nc.gpsimd.memset(eps[:], LN_EPS).then_inc(F["eps"], 1)
                    pool.wait_ge(F["z"], 1)
                    for i, (t0, t1) in enumerate(SELF_PIECES):
                        pool.wait_ge(s_xl[min(i, 1)], 16)
                        v = xl_in[:, t0:t1, :].rearrange("p t (h c) -> p t h c", h=H)
                        nc.gpsimd.tensor_tensor(v, v, bc(sw[:, t0:t1, :].unsqueeze(3), [P, t1 - t0, H, HD]), ALU.mult)\
                          .then_inc(F["eps"], 1)

                @block.scalar
                def _(act):
                    act.wait_ge(F["z"], 1)
                    act.wait_ge(F["eps"], 1)

                    def divide(t, s, m):
                        wait(act, F["tr"], t - 1)
                        for h in range(H):
                            last = nc.scalar.activation(
                                gsum[:, s, h * HD:(h + 1) * HD],
                                acc1[:, bass.ds(t, 1), h * HD:(h + 1) * HD].rearrange("p a n -> p (a n)"), ACT.Copy,
                                scale=rz[:, bass.ds(t, 1), h:h + 1].rearrange("p a n -> p (a n)"))
                        last.then_inc(F["g0"], 1)

                    def take_gT(t, s, m):
                        act.wait_ge(F["tr"], t + 1)
                        wait(act, F["up"], t - 1)
                        nc.scalar.activation(gT[:, s].rearrange("p k n -> p (k n)"), psum[:, s, 0:HID],
                                             ACT.Copy).then_inc(F["gT"], 1)

                    def deviation(t, s, m):
                        act.wait_ge(F["mv"], t + 1)
                        nc.scalar.activation(sd[:, s:s + 1], mv[:, s, 1:2], ACT.Sqrt, bias=eps[:, 0:1]).then_inc(F["sd"], 1)

                    def normalise(t, s, m):
                        act.wait_ge(F["rs"], t + 1)
                        wait(act, s_out[s], 16 * m)
                        nc.scalar.activation(o[:, s, :], y[:, s, :], ACT.Identity, bias=rs[:, s, 1:2],
                                             scale=rs[:, s, 0:1]).then_inc(F["o"], 1)
                    pipelined(act, NT, [(6, deviation), (3, take_gT), (6, normalise), (0, divide)], AHEAD, unroll=2)

                @block.tensor
                def _(pe):
                    pe.wait_ge(F["w"], 16)

                    def transposes(t, s, m):
                        pe.wait_ge(F["g"], t + 1)
                        wait(pe, F["gT"], t - 1)
                        for k in range(KH):
                            last = nc.tensor.transpose(psum[:, s, k * P:(k + 1) * P], gsum[:, s, k * P:(k + 1) * P], ident[:])
                        last.then_inc(F["tr"], 1)

                    def up(t, s, m):
                        pe.wait_ge(F["gT"], t + 1)
                        wait(pe, F["s"], 2 * t - 2)
                        for k in range(KH):
                            for i in range(2):
                                last = nc.tensor.matmul(psum[:, 2 + 2 * s + i, :], gT[:, s, k, :],
                                                        wu[:, k, i * 512:(i + 1) * 512], start=(k == 0), stop=(k == KH - 1))
                        last.then_inc(F["up"], 1)
                    pipelined(pe, NT, [(2, transposes), (4, up)], AHEAD, unroll=2)

                @block.vector
                def _(dve):
                    divisor(nc, Chain(dve, sem("f_zc")), acc1[:, :, HID:ACC1], noself, wself, rz, sw, DEN_EPS)\
                        .then_inc(F["z"], 1)
                    linkD = Chain(dve, F["D"], 1)

                    def add_self(t, s, m):
                        dve.wait_ge(F["g0"], t + 1)
                        if isinstance(t, int):
                            for i, (t0, t1) in enumerate(SELF_PIECES):
                                if t == t0:
                                    dve.wait_ge(F["eps"], i + 2)
                        elif s == 0:
                            dve.wait_ge(F["eps"], len(SELF_PIECES) + 1)
                        last = nc.vector.tensor_tensor(gsum[:, s], gsum[:, s],
                                                       xl_in[:, bass.ds(t, 1), :].rearrange("p a n -> p (a n)"), ALU.add)
                        last.then_inc(F["g"], 1)

                    def residual(t, s, m):
                        dve.wait_ge(F["up"], t + 1)
                        dve.wait_ge(s_x1[s], 16 * m + 16)
                        wait(dve, F["o"], t - 1)
                        nc.vector.tensor_tensor(y[:, s], psum[:, 2 + 2 * s:4 + 2 * s].rearrange("p a b -> p (a b)"),
                                                x1_in[:, s], ALU.add).then_inc(F["s"], 1)
                        dve.wait_ge(F["s"], 2 * t + 1)
                        for i in range(2):
                            last = nc.vector.bn_stats(st[:, s, 6 * i:6 * i + 6], y[:, s, i * 512:(i + 1) * 512])
                        last.then_inc(F["s"], 1)
                        dve.wait_ge(F["s"], 2 * t + 2)
                        nc.vector.tensor_copy(mark[:], st[:, s, 0:1])
                        nc.vector.bn_aggr(mv[:, s, :], st[:, s, :]).then_inc(F["mv"], 1)

                    def factors(t, s, m):
                        linkD.tile(t)
                        dve.wait_ge(F["sd"], t + 1)
                        linkD(nc.vector.reciprocal(rs[:, s, 0:1], sd[:, s:s + 1]))
                        nc.vector.tensor_scalar(rs[:, s, 1:2], mv[:, s, 0:1], rs[:, s, 0:1], -1.0, ALU.mult, ALU.mult)\
                            .then_inc(F["rs"], 1)
                    pipelined(dve, NT, [(1, add_self), (6, factors), (5, residual)], AHEAD, unroll=2)


def divisor(nc, link, z9, noself, wself, rz, sw, eps):
    link(nc.vector.tensor_scalar(noself[:], z9[:, :, 2 * H], -1.0, 1.0, ALU.mult, ALU.add))
    link(nc.vector.tensor_tensor(wself[:], z9[:, :, H:2 * H], bc(noself[:].unsqueeze(2), [P, NT, H]), ALU.add))
    link(nc.vector.tensor_tensor(rz[:], z9[:, :, 0:H], wself[:], ALU.add))
    if eps:
        link(nc.vector.tensor_scalar_add(rz[:], rz[:], eps))
    link(nc.vector.reciprocal(rz[:], rz[:]))
    return nc.vector.tensor_tensor(sw[:], wself[:], rz[:], ALU.mult)


N_EDGE_DMAS = 3 + 2 * NB


class ScanSems:

    def __init__(self, sem):
        self.signals = {"t1": NB, "sv": NB, "chain": 0, "f1": 1, "t2": 1, "c": 1, "t3": 1, "m": NB, "e": NB, "t4": NB}
        self.sems = {n: sem("scan_" + n) for n in self.signals}
        self.base = {n: 0 for n in self.signals}

    def __getitem__(self, name):
        return self.sems[name]

    def end(self, chained):
        self.base = {n: self.base[n] + (chained if n == "chain" else k) for n, k in self.signals.items()}


def weigh_edges(nc, scan, tag, psum, w9, ident, isfirst, rs_f, rs_b, pen, any_f, any_b, sums,
                first_rows):
    with ExitStack() as ph:
        def sb(name, shape, dt=F32):
            return ph.enter_context(nc.sbuf_tensor(f"{tag}_{name}", shape, dt))
        v = sb("v", [TB, NB, H, P])
        sv = sb("sv", [TB, NB, H, P])
        fw = sb("fw", [TB, NB, H, P])
        bw = sb("bw", [TB, NB, H, P])
        cf = sb("cf", [H, T + 1])
        cb = sb("cb", [H, T + 1])
        cin = sb("cin", [TB, 2, NB, H])
        with nc.Block() as block:
            @block.sync
            def _(sp):
                if first_rows[0] == "sync":
                    first_rows[1](sp)

            @block.gpsimd
            def _(pool):
                if first_rows[0] == "gpsimd":
                    first_rows[1](pool)
                for a in sums:
                    nc.gpsimd.memset(a, 0.0)

            @block.tensor
            def _(pe):
                for b in range(NB):
                    for h in range(H):
                        for i in range(2):
                            last = nc.tensor.transpose(psum[0:TB, 4 * i + b, h * P:(h + 1) * P],
                                                       w9[:, b * TB:(b + 1) * TB, i * H + h], ident[:])
                    last.then_inc(scan["t1"], 1)
                pe.wait_ge(scan["f1"], scan.base["f1"] + 1)
                pe.wait_ge(scan["sv"], scan.base["sv"] + NB)
                for b in range(NB):
                    nc.tensor.transpose(psum[0:H, 0, b * TB:(b + 1) * TB], fw[:, b, :, P - 1], ident[0:TB, 0:TB])
                    last = nc.tensor.transpose(psum[0:H, 1, b * TB:(b + 1) * TB], bw[:, b, :, 0], ident[0:TB, 0:TB])
                last.then_inc(scan["t2"], 1)
                pe.wait_ge(scan["c"], scan.base["c"] + 1)
                for b in range(NB):
                    nc.tensor.transpose(psum[0:TB, 2, b * H:(b + 1) * H], cf[:, b * TB:(b + 1) * TB], ident[0:H, 0:H])
                    last = nc.tensor.transpose(psum[0:TB, 2, (NB + b) * H:(NB + b + 1) * H],
                                               cb[:, b * TB + 1:(b + 1) * TB + 1], ident[0:H, 0:H])
                last.then_inc(scan["t3"], 1)
                for b in range(NB):
                    pe.wait_ge(scan["e"], scan.base["e"] + b + 1)
                    for h in range(H):
                        nc.tensor.transpose(psum[:, b, h * TB:(h + 1) * TB], v[:, b, h, :], ident[0:TB, 0:TB])
                        last = nc.tensor.transpose(psum[:, 4 + b, h * TB:(h + 1) * TB], sv[:, b, h, :], ident[0:TB, 0:TB])
                    last.then_inc(scan["t4"], 1)

            @block.scalar
            def _(act):
                for b in range(NB):
                    act.wait_ge(scan["t1"], scan.base["t1"] + b + 1)
                    nc.scalar.activation(sv[:, b].rearrange("p h e -> p (h e)"), psum[0:TB, 4 + b, :], ACT.Copy)\
                        .then_inc(scan["sv"], 1)
                for b in range(NB):
                    act.wait_ge(scan["m"], scan.base["m"] + b + 1)
                    nc.scalar.activation(v[:, b], v[:, b], ACT.Exp)
                    nc.scalar.activation(sv[:, b], sv[:, b], ACT.Exp).then_inc(scan["e"], 1)
                for b in range(NB):
                    act.wait_ge(scan["t4"], scan.base["t4"] + b + 1)
                    nc.scalar.activation(w9[:, b * TB:(b + 1) * TB, 0:H].rearrange("p t h -> p h t"),
                                         psum[:, b, 0:H * TB].rearrange("p (h t) -> p h t", h=H), ACT.Copy)

            @block.vector
            def _(dve):
                link = Chain(dve, scan["chain"], base=scan.base["chain"])
                nc.vector.memset(cf[:], -BIG)
                nc.vector.memset(cb[:], -BIG)
                for b in range(NB):
                    dve.wait_ge(scan["t1"], scan.base["t1"] + b + 1)
                    link(nc.vector.tensor_tensor(v[:, b], psum[0:TB, b, :].rearrange("p (h e) -> p h e", h=H),
                                                 bc(pen[:, b, :].unsqueeze(1), [TB, H, P]), ALU.add))

                def scans(start):
                    for b in range(NB):
                        for h in range(H):
                            nc.vector.tensor_tensor_scan(fw[:, b, h, :], rs_f[:, b, :], v[:, b, h, :],
                                                         start(0, b, h), ALU.add, ALU.max)
                            last = nc.vector.tensor_tensor_scan(bw[:, b, h, ::-1], rs_b[:, b, ::-1], v[:, b, h, ::-1],
                                                                start(1, b, h), ALU.add, ALU.max)
                    return last
                scans(lambda i, b, h: -BIG).then_inc(scan["f1"], 1)
                dve.wait_ge(scan["t2"], scan.base["t2"] + 1)
                nc.vector.tensor_tensor_scan(cf[:, 1:T + 1], any_f[:], psum[0:H, 0, 0:T], -BIG, ALU.add, ALU.max)
                nc.vector.tensor_tensor_scan(cb[:, T - 1::-1], any_b[:, ::-1], psum[0:H, 1, T - 1::-1], -BIG,
                                             ALU.add, ALU.max).then_inc(scan["c"], 1)
                dve.wait_ge(scan["t3"], scan.base["t3"] + 1)
                link(nc.vector.tensor_copy(cin[:].rearrange("p i b h -> p (i b h)"), psum[0:TB, 2, 0:2 * NB * H]))
                link(scans(lambda i, b, h: cin[:, i, b, h:h + 1]))
                dve.wait_ge(scan["sv"], scan.base["sv"] + NB)
                for b in range(NB):
                    link(nc.vector.tensor_tensor(fw[:, b], fw[:, b], bw[:, b], ALU.max))
                    link(nc.vector.tensor_tensor(fw[:, b], fw[:, b], sv[:, b], ALU.max))
                    nc.vector.tensor_tensor(v[:, b], v[:, b], fw[:, b], ALU.subtract)
                    nc.vector.tensor_tensor(sv[:, b], sv[:, b], fw[:, b], ALU.subtract).then_inc(scan["m"], 1)
                for b in range(NB):
                    dve.wait_ge(scan["t4"], scan.base["t4"] + b + 1)
                    nc.vector.tensor_tensor(w9[:, b * TB:(b + 1) * TB, H:2 * H].rearrange("p t h -> p h t"),
                                            psum[:, 4 + b, 0:H * TB].rearrange("p (h t) -> p h t", h=H),
                                            bc(isfirst[:, b * TB:(b + 1) * TB].unsqueeze(1), [P, H, TB]), ALU.mult)
                nc.vector.tensor_copy(w9[:, :, 2 * H], isfirst[:])
                scan.end(link.k)


_INS = ['x', 'src', 'dst', 'L0_gnn_W', 'L0_gnn_att_src', 'L0_gnn_att_dst', 'L0_gnn_bias', 'L1_gnn_rms_w',
        'L1_gnn_W_down', 'L1_gnn_Wl', 'L1_gnn_Wr', 'L1_gnn_att', 'L1_gnn_W_up']


def kernel(**inputs):
    import numpy as np
    import concourse.bacc as bacc
    from concourse import mybir
    from concourse.bass_utils import run_bass_kernel_spmd
    nc = bacc.Bacc("TRN2", target_bir_lowering=False, num_devices=1)
    arrays, args = {}, []
    for name in _INS:
        a = np.ascontiguousarray(inputs[name])
        arrays["in_" + name] = a
        args.append(nc.dram_tensor("in_" + name, a.shape, mybir.dt.from_np(a.dtype), kind="ExternalInput").ap())
    out = nc.dram_tensor("out_0", (N, D), F32, kind="ExternalOutput").ap()
    gnn_kernel(nc, *args, out)
    r = run_bass_kernel_spmd(nc, [arrays], core_ids=[0])
    return r.results[0]["out_0"]
```
